# Optimizing a Trainium2 kernel written in Bass

```python
import numpy as np
import jax
import jax.numpy as jnp

def _softmax(x, axis=-1):
    return jax.nn.softmax(x, axis=axis)

def _gelu(x):
    return jax.nn.gelu(x, approximate=True)

def _silu(x):
    return jax.nn.silu(x)

def _sigmoid(x):
    return jax.nn.sigmoid(x)

def _layernorm(x, axis=-1, eps=1e-05):
    m = jnp.mean(x, axis=axis, keepdims=True)
    v = jnp.var(x, axis=axis, keepdims=True)
    return (x - m) / jnp.sqrt(v + eps)

def _scatter_add(tgt, idx, src, axis=0):
    return tgt.at[idx].add(src)

def _segment_sum(src, seg, n):
    return jax.ops.segment_sum(src, seg, n)
kernel_name = 'mk_adj_ffn_d1_adj_r2_30f9e1'

def setup_inputs(seed: int=0):
    np.random.seed(seed)
    _w = jnp.asarray

    def _rec_inputs():
        import jax
        import jax.numpy as jnp
        _gk = jax.random.key(seed)
        x = -0.0002928 + 1 * jax.random.normal(jax.random.fold_in(_gk, 1), (8, 1024, 256), jnp.float32)
        _a = jax.random.bernoulli(jax.random.fold_in(_gk, 2), 0.00195312, (8, 1024, 1024))
        adj = _a.astype(jnp.int32)
        return (x, adj)
    x, adj = _rec_inputs()

    def _L0_gnn_setup():
        import jax, jax.numpy as jnp
        import numpy as np
        NEG_SLOPE = 0.2
        key = jax.random.key(seed)
        k1, k2, k3, k4, k5 = jax.random.split(key, 5)
        B, N, H = (8, 512, 256)
        node_features = jax.random.normal(k1, (B, N, H), dtype=jnp.float32)
        adjacency_matrix = jax.random.randint(k2, (B, N, N), 0, 2, dtype=jnp.int32)
        scale = 1.0 / np.sqrt(2 * H)
        attn_w_src = jax.random.uniform(k3, (H,), jnp.float32, -scale, scale)
        attn_w_dst = jax.random.uniform(k4, (H,), jnp.float32, -scale, scale)
        attn_b = jax.random.uniform(k5, (1,), jnp.float32, -scale, scale)
        return {'node_features': node_features, 'adjacency_matrix': adjacency_matrix, 'attn_w_src': attn_w_src, 'attn_w_dst': attn_w_dst, 'attn_b': attn_b}
    _L0_gnn_all = _L0_gnn_setup()
    _L0_gnn_in = {k: v for k, v in _L0_gnn_all.items() if k in ('attn_w_src', 'attn_w_dst', 'attn_b')}
    del _L0_gnn_all

    def _L0_ffn_setup():
        import jax, jax.numpy as jnp
        import numpy as np
        B, S, D = (4, 1024, 256)
        I = 192
        E = 16
        K = 2

        def _inv_softplus(v):
            return float(np.log(np.expm1(v)))

        def swiglu5(h, alpha, gate_scale, up_shift, gate_clamp_raw, up_clamp_raw):
            gate_clamp = jax.nn.softplus(gate_clamp_raw)
            up_clamp = jax.nn.softplus(up_clamp_raw)
            g = jnp.clip(h[..., ::2], -gate_clamp, gate_clamp)
            u = jnp.clip(h[..., 1::2], -up_clamp, up_clamp)
            return g * jax.nn.sigmoid(g * alpha) * gate_scale * (u + up_shift)
        key = jax.random.key(seed)
        ks = jax.random.split(key, 10)
        std = 0.02
        raw = _inv_softplus(7.0)
        act = jnp.array([1.702, 1.0, 1.0, raw, raw], dtype=jnp.float32)
        return {'x': jax.random.normal(ks[0], (B, S, D), dtype=jnp.float32), 'gate_w': jax.random.normal(ks[1], (D, E), dtype=jnp.float32) * 0.01, 'gate_b': jnp.zeros((E,), dtype=jnp.float32), 'shared_w1': jax.random.normal(ks[2], (D, 2 * I), dtype=jnp.float32) * std, 'shared_b1': jnp.zeros((2 * I,), dtype=jnp.float32), 'shared_w2': jax.random.normal(ks[3], (I, D), dtype=jnp.float32) * std, 'shared_b2': jnp.zeros((D,), dtype=jnp.float32), 'shared_act': act, 'expert_w1': jax.random.normal(ks[4], (E, D, 2 * I), dtype=jnp.float32) * std, 'expert_b1': jnp.zeros((E, 2 * I), dtype=jnp.float32), 'expert_w2': jax.random.normal(ks[5], (E, I, D), dtype=jnp.float32) * std, 'expert_b2': jnp.zeros((E, D), dtype=jnp.float32), 'expert_act': jnp.tile(act[None, :], (E, 1))}
    _L0_ffn_all = _L0_ffn_setup()
    _L0_ffn_in = {k: v for k, v in _L0_ffn_all.items() if k in ('gate_w', 'gate_b', 'shared_w1', 'shared_b1', 'shared_w2', 'shared_b2', 'shared_act', 'expert_w1', 'expert_b1', 'expert_w2', 'expert_b2', 'expert_act')}
    del _L0_ffn_all
    return {'x': x, 'adj': adj, 'L0_gnn_attn_w_src': _L0_gnn_in['attn_w_src'], 'L0_gnn_attn_w_dst': _L0_gnn_in['attn_w_dst'], 'L0_gnn_attn_b': _L0_gnn_in['attn_b'], 'L0_ffn_gate_w': _L0_ffn_in['gate_w'], 'L0_ffn_gate_b': _L0_ffn_in['gate_b'], 'L0_ffn_shared_w1': _L0_ffn_in['shared_w1'], 'L0_ffn_shared_b1': _L0_ffn_in['shared_b1'], 'L0_ffn_shared_w2': _L0_ffn_in['shared_w2'], 'L0_ffn_shared_b2': _L0_ffn_in['shared_b2'], 'L0_ffn_shared_act': _L0_ffn_in['shared_act'], 'L0_ffn_expert_w1': _L0_ffn_in['expert_w1'], 'L0_ffn_expert_b1': _L0_ffn_in['expert_b1'], 'L0_ffn_expert_w2': _L0_ffn_in['expert_w2'], 'L0_ffn_expert_b2': _L0_ffn_in['expert_b2'], 'L0_ffn_expert_act': _L0_ffn_in['expert_act']}

def reference(x, adj, L0_gnn_attn_w_src, L0_gnn_attn_w_dst, L0_gnn_attn_b, L0_ffn_gate_w, L0_ffn_gate_b, L0_ffn_shared_w1, L0_ffn_shared_b1, L0_ffn_shared_w2, L0_ffn_shared_b2, L0_ffn_shared_act, L0_ffn_expert_w1, L0_ffn_expert_b1, L0_ffn_expert_w2, L0_ffn_expert_b2, L0_ffn_expert_act):
    import jax
    import jax.numpy as jnp

    def _L0_gnn_ref(node_features, adjacency_matrix, attn_w_src, attn_w_dst, attn_b):
        import jax, jax.numpy as jnp
        import numpy as np
        NEG_SLOPE = 0.2
        B, N, H = node_features.shape
        s_src = jnp.einsum('bnh,h->bn', node_features, attn_w_src)
        s_dst = jnp.einsum('bnh,h->bn', node_features, attn_w_dst)
        scores = s_src[:, :, None] + s_dst[:, None, :] + attn_b[0]
        scores = jax.nn.leaky_relu(scores, negative_slope=NEG_SLOPE)
        adj = adjacency_matrix.astype(jnp.float32) + jnp.eye(N, dtype=jnp.float32)[None]
        scores = jnp.where(adj == 0, -jnp.inf, scores)
        attn = jax.nn.softmax(scores, axis=-1)
        return jnp.einsum('bij,bjh->bih', attn, node_features)

    def _L0_ffn_ref(x, gate_w, gate_b, shared_w1, shared_b1, shared_w2, shared_b2, shared_act, expert_w1, expert_b1, expert_w2, expert_b2, expert_act):
        import jax, jax.numpy as jnp
        import numpy as np
        B, S, D = (4, 1024, 256)
        I = 192
        E = 16
        K = 2

        def _inv_softplus(v):
            return float(np.log(np.expm1(v)))

        def swiglu5(h, alpha, gate_scale, up_shift, gate_clamp_raw, up_clamp_raw):
            gate_clamp = jax.nn.softplus(gate_clamp_raw)
            up_clamp = jax.nn.softplus(up_clamp_raw)
            g = jnp.clip(h[..., ::2], -gate_clamp, gate_clamp)
            u = jnp.clip(h[..., 1::2], -up_clamp, up_clamp)
            return g * jax.nn.sigmoid(g * alpha) * gate_scale * (u + up_shift)
        shape = x.shape
        xf = x.reshape(-1, shape[-1])
        h = xf @ shared_w1 + shared_b1
        t = swiglu5(h, shared_act[0], shared_act[1], shared_act[2], shared_act[3], shared_act[4])
        z = t @ shared_w2 + shared_b2
        gate_logits = xf @ gate_w + gate_b
        gate_probs = jax.nn.softmax(gate_logits, -1)
        w, idx = jax.lax.top_k(gate_probs, K)
        w = w / jnp.sum(w, axis=-1, keepdims=True)
        cw = jnp.sum(jax.nn.one_hot(idx, E, dtype=xf.dtype) * w[..., None], axis=1)
        he = jnp.einsum('nd,edh->enh', xf, expert_w1) + expert_b1[:, None, :]
        a = expert_act
        te = swiglu5(he, a[:, 0, None, None], a[:, 1, None, None], a[:, 2, None, None], a[:, 3, None, None], a[:, 4, None, None])
        oe = jnp.einsum('enh,ehd->end', te, expert_w2) + expert_b2[:, None, :]
        y = jnp.einsum('ne,end->nd', cw, oe)
        return (y + z).reshape(shape)
    x = x + _L0_gnn_ref(_layernorm(x, axis=-1), adj, L0_gnn_attn_w_src, L0_gnn_attn_w_dst, L0_gnn_attn_b)
    x = x + _L0_ffn_ref(_layernorm(x, axis=-1), L0_ffn_gate_w, L0_ffn_gate_b, L0_ffn_shared_w1, L0_ffn_shared_b1, L0_ffn_shared_w2, L0_ffn_shared_b2, L0_ffn_shared_act, L0_ffn_expert_w1, L0_ffn_expert_b1, L0_ffn_expert_w2, L0_ffn_expert_b2, L0_ffn_expert_act)
    return x

_drawn_inputs = setup_inputs


def setup_inputs(seed=0):
    import zlib

    import numpy as np

    out = dict(_drawn_inputs(seed))
    spreads = {'L0_ffn_gate_b': (0.0, 0.1),
     'L0_ffn_shared_b1': (0.0, 0.76),
     'L0_ffn_shared_b2': (0.0, 0.1),
     'L0_ffn_expert_b1': (0.0, 0.8),
     'L0_ffn_expert_b2': (0.0, 0.1)}
    factors = {}
    for name, (base, spread) in spreads.items():
        noise = np.random.default_rng([zlib.crc32(name.encode()), seed]).standard_normal(out[name].shape)
        drawn = base * np.exp(spread * noise) if base else spread * noise
        out[name] = jnp.asarray(drawn.astype(out[name].dtype))
    for name, factor in factors.items():
        out[name] = (out[name] * factor).astype(out[name].dtype)
    return out
```

```python
from contextlib import ExitStack

import concourse.bass as bass
from concourse import mybir

ALU = mybir.AluOpType
ACT = mybir.ActivationFunctionType
F32 = mybir.dt.float32
F16 = mybir.dt.float16
I32 = mybir.dt.int32

P = 128
SLOPE = 0.2
EPS = 1e-5
MASKED = -1.0e30
WS = 256.0
TS = 16.0


BF16 = mybir.dt.bfloat16
AX_X = mybir.AxisListType.X
ds = bass.ds


class Apart:

    def __init__(self, phase):
        self.held, self.phase = {}, phase

    def __call__(self, eng):
        if eng not in self.held:
            self.held[eng] = eng.alloc_register(f"{self.phase}_held")
            eng.reg_mov(self.held[eng], 1)
        eng.reg_alu(self.held[eng], self.held[eng], 1, ALU.max)

    def end(self, eng, passed):
        if eng in self.held:
            eng.wait_ge(passed, self.held[eng])


def attention_phase(nc, k, x, adj, w_src, w_dst, attn_b, gate_w, gate_b):
    B, N, H = x.shape
    E = gate_w.shape[1]
    TPB = N // P
    NT = B * TPB
    HT = TPB // 2
    KT = H // P
    resid, ident, ident16, ones = k.resid, k.ident, k.ident16, k.ones

    ctx = ExitStack()
    with ctx:
        def sb(name, shape, dt=F32):
            return ctx.enter_context(nc.sbuf_tensor(name, shape, dt))

        def ps(name, shape, dt=F32):
            return ctx.enter_context(nc.psum_tensor(name, shape, dt))

        def sem(name):
            return ctx.enter_context(nc.semaphore(name))

        nodes = sb("nodes", [P, 4, TPB, H])
        dst5 = sb("dst5", [P, 2, N])
        pen = sb("pen", [P, TPB, N])
        score = sb("score", [P, 4, N])
        probT = sb("probT", [P, 2, TPB, P])
        ln2 = sb("ln2", [P, 2, H])
        gate_raw = sb("gate_raw", [P, KT, E])
        gate_parts = sb("gate_parts", [P, 2, KT, E], F16)
        gate_row = sb("gate_row", [P, E])
        parts = sb("parts", [P, 4, 2 * H], F16)
        xT = sb("xT", [P, 2, 2 * KT, P], F16)
        zeros = sb("zeros", [P, 2 * H], F16)
        w_rows = sb("w_rows", [P, 2, H])
        b_col = sb("b_col", [P, 1])
        b8_col = sb("b8_col", [P, 1])
        dots_junk = sb("dots_junk", [P, 4, H], mybir.dt.bfloat16)
        diag = sb("diag", [P, 4, P])
        stats1 = sb("stats1", [P, TPB, 6])
        mv1 = sb("mv1", [P, TPB, 2])
        ve1 = sb("ve1", [P, TPB])
        rstd1 = sb("rstd1", [P, TPB])
        ndots = sb("ndots", [P, 2, TPB])
        src8 = sb("src8", [P, 2, TPB])
        rowmax = sb("rowmax", [P, TPB])
        negmax = sb("negmax", [P, TPB])
        rowsum = sb("rowsum", [P, TPB])
        rinv = sb("rinv", [P, TPB])
        stats2 = sb("stats2", [P, TPB, 6])
        mv2 = sb("mv2", [P, TPB, 2])
        ve2 = sb("ve2", [P, TPB])
        rstd2 = sb("rstd2", [P, TPB])
        mhalf = sb("mhalf", [P, TPB])

        ps_half = [ps(f"ps_half{i}", [P, HT, P]) for i in range(2)]
        ps_att = [ps(f"ps_att{i}", [P, 512]) for i in range(2)]
        ps_dst = [ps(f"ps_dst{i}", [P, 512]) for i in range(2)]
        ps_xT = ps("ps_xT", [P, 2 * KT, P], F16)
        ps_gate = ps("ps_gate", [P, TPB, E])

        const_in = sem("const_in")
        x_in = sem("x_in")
        adj_in = [sem(f"adj_in{i}") for i in range(TPB)]
        ident_zeroed = sem("ident_zeroed")
        consts_ready = sem("consts_ready")
        b8_ready = sem("b8_ready")
        stats1_ready = sem("stats1_ready")
        mv1_ready = sem("mv1_ready")
        ve1_ready = sem("ve1_ready")
        rstd1_ready = sem("rstd1_ready")
        nodes_ready = sem("nodes_ready")
        dots_ready = sem("dots_ready")
        src8_ready = sem("src8_ready")
        diag_ready = sem("diag_ready")
        dst_ready = sem("dst_ready")
        dst5_ready = sem("dst5_ready")
        loop_ready = sem("loop_ready")
        mask_ready = sem("mask_ready")
        pen_ready = sem("pen_ready")
        relu_ready = sem("relu_ready")
        score_ready = sem("score_ready")
        negmax_ready = sem("negmax_ready")
        prob_ready = sem("prob_ready")
        half_ready = [sem(f"half_ready{i}") for i in range(2)]
        probT_ready = [sem(f"probT_ready{i}") for i in range(2)]
        att_ready = sem("att_ready")
        rinv_ready = sem("rinv_ready")
        resid_ready = sem("resid_ready")
        stats2_ready = sem("stats2_ready")
        mv2_ready = sem("mv2_ready")
        ve2_ready = sem("ve2_ready")
        rstd2_ready = sem("rstd2_ready")
        ln2_ready = sem("ln2_ready")
        hi_ready = sem("hi_ready")
        lo_ready = sem("lo_ready")
        parts_out = [sem(f"parts_out{i}") for i in range(4)]
        zeros_ready = sem("zeros_ready")
        zeros_stored = sem("zeros_stored")
        gate_parts_ready = sem("gate_parts_ready")
        xT_raw = sem("xT_raw")
        xT_ready = sem("xT_ready")
        gate_ready = sem("gate_ready")
        logits_ready = sem("logits_ready")

        LAST_LAG = 16
        PEELED = 2

        apart = Apart("attention")

        def phase1(eng, step, last=1):
            for b in range(PEELED):
                for t in range(TPB):
                    step(b, t, lambda g: g >= 0, last)
            with eng.Fori(PEELED, B - last) as b:
                for t in range(TPB):
                    step(b, t, lambda g: True, last)
            apart.end(eng, consts_ready)
            for b in range(B - last, B):
                for t in range(TPB + (LAST_LAG if b == B - 1 else 0)):
                    step(b, t, lambda g: g < NT, B - 1 - b)

        def tile_of(b, t, lag):
            return b * TPB + (t - lag), (t - lag) % TPB

        def batch_of(b, t, lag):
            return b + (t - lag) // TPB


        block = ctx.enter_context(nc.Block())

        @block.sync
        def _(sp):
            sp.dma_start(resid[:, 0:TPB, :], x[0].rearrange("(t p) h -> p t h", p=P)).then_inc(x_in, 16)
            for i, w in enumerate((w_src, w_dst)):
                sp.dma_start(w_rows[:, i, :], w.rearrange("(a h) -> a h", a=1).broadcast_to([P, H])).then_inc(const_in, 16)
            sp.dma_start(gate_raw[:, :, :], gate_w.rearrange("(k p) e -> p k e", p=P)).then_inc(const_in, 16)
            sp.dma_start(gate_row[:, :], gate_b.rearrange("(a e) -> a e", a=1).broadcast_to([P, E])).then_inc(const_in, 16)
            sp.dma_start(b_col[:, :], attn_b.rearrange("(a h) -> a h", a=1).broadcast_to([P, 1])).then_inc(const_in, 16)

            def step(b, t, valid, more):
                if t < TPB:
                    load(b, t, more)
                g, j = tile_of(b, t, 15)
                if valid(g):
                    sp.wait_ge(lo_ready, g + 1)
                    sp.dma_start(k.token_x[ds(g, 1)].rearrange("t p c -> p (t c)"), parts[:, j % 4, :]
                                 ).then_inc(parts_out[j % 4], 16)

            def load(b, t, more):
                if t == 4:
                    sp.wait_ge(zeros_ready, 1)
                    rows = k.expert_x.rearrange("(b t p) c -> b p t c", b=B, p=P)
                    sp.dma_start(rows[ds(b, 1)].rearrange("b p t c -> p (b t) c"),
                                 zeros[:, :].rearrange("p (a c) -> p a c", a=1).broadcast_to([P, rows.shape[2], 2 * H])
                                 ).then_inc(zeros_stored, 16)
                if t == 0 and isinstance(b, int) and b == 0:
                    sp.wait_ge(x_in, 16)
                    sp.dma_start(resid[:, TPB:2 * TPB, :], x[1].rearrange("(t p) h -> p t h", p=P)).then_inc(x_in, 16)
                if t == 1 and more >= 2:
                    sp.wait_ge(x_in, (b + 2) * 16)
                    sp.dma_start(resid[:, ds((b + 2) * TPB, TPB), :],
                                 x[ds(b + 2, 1)].rearrange("b (t p) h -> p (b t) h", p=P)).then_inc(x_in, 16)
                if not (isinstance(b, int) and b == 0):
                    sp.wait_ge(score_ready, (b - 1) * TPB + (t + 1))
                sp.dma_start(pen[:, t, :].bitcast(I32),
                             adj[ds(b, 1), t * P:(t + 1) * P, :].rearrange("b p n -> p (b n)")
                             ).then_inc(adj_in[t], 16)
            phase1(sp, step, last=2)
            sp.wait_ge(zeros_stored, 16 * B)
            for i in range(4):
                sp.wait_ge(parts_out[i], 16 * NT // 4)

        @block.gpsimd
        def _(pool):
            nc.gpsimd.memset(ident[:, :], 0.0).then_inc(ident_zeroed, 1)
            nc.gpsimd.memset(ones[:, :], 1.0).then_inc(consts_ready, 1)
            nc.gpsimd.memset(mhalf[:, :], -0.5).then_inc(consts_ready, 1)
            nc.gpsimd.memset(zeros[:, :], 0.0).then_inc(zeros_ready, 1)
            pool.wait_ge(ident_zeroed, 1)
            nc.gpsimd.affine_select(out=ident[:, :], in_=ident[:, :], compare_op=ALU.not_equal, fill=1.0,
                                    base=0, pattern=[[-1, P]], channel_multiplier=1).then_inc(consts_ready, 1)
            pool.wait_ge(consts_ready, 3)
            nc.gpsimd.tensor_copy(ident16[:, :], ident[:, :]).then_inc(consts_ready, 1)
            pool.wait_ge(consts_ready, 4)

            def first_norm_scale(b):
                pool.wait_ge(mv1_ready, (b + 1) * TPB)
                apart(pool)
                nc.gpsimd.tensor_scalar(ve1[:, :], mv1[:, :, 1], EPS, None, ALU.add).then_inc(ve1_ready, 1)
                pool.wait_ge(ve1_ready, b + 1)
                nc.gpsimd.tensor_tensor(rstd1[:, :], ve1[:, :], mhalf[:, :], ALU.pow).then_inc(rstd1_ready, 1)

            def diagonals(b, tiles):
                for j in tiles:
                    pool.wait_ge(dots_ready, b * 2 * TPB + 2 * (j + 1))
                    if j >= 4 or not (isinstance(b, int) and b == 0):
                        pool.wait_ge(dst_ready, b * TPB + (j - 3))
                    apart(pool)
                    nc.gpsimd.tensor_scalar(diag[:, j % 4, :], ident[:, :], ndots[:, 1, j:j + 1], None,
                                            ALU.mult).then_inc(diag_ready, 1)

            def step(b, t, valid, more):
                if more and t == 7:
                    diagonals(b + 1, range(5, 8))
                if t < TPB:
                    g = b * TPB + t
                    if t == 0:
                        pool.wait_ge(dst5_ready, 2 * (b + 1))
                    pool.wait_ge(mask_ready, g + 1)
                    apart(pool)
                    nc.gpsimd.tensor_tensor(pen[:, t, :], pen[:, t, :], dst5[:, ds(b % 2, 1), :],
                                            ALU.add).then_inc(pen_ready, 1)
                if more and t == 2:
                    first_norm_scale(b + 1)
                if more and t == 5:
                    diagonals(b + 1, range(0, 2))
                if more and t == 6:
                    diagonals(b + 1, range(2, 5))
                g, j = tile_of(b, t, 9)
                if valid(g):
                    pool.wait_ge(mv2_ready, g + 1)
                    apart(pool)
                    nc.gpsimd.tensor_scalar(ve2[:, j:j + 1], mv2[:, j, 1:2], EPS, None, ALU.add).then_inc(ve2_ready, 1)
                    pool.wait_ge(ve2_ready, g + 1)
                    nc.gpsimd.tensor_tensor(rstd2[:, j:j + 1], ve2[:, j:j + 1], mhalf[:, 0:1],
                                            ALU.pow).then_inc(rstd2_ready, 1)

            first_norm_scale(0)
            diagonals(0, range(TPB))
            phase1(pool, step)

        @block.vector
        def _(dve):
            def stats(b, tiles):
                if tiles[0] == 0:
                    dve.wait_ge(x_in, (b + 1) * 16)
                for j in tiles:
                    apart(dve)
                    nc.vector.bn_stats(stats1[:, j, :], resid[:, ds(b * TPB + j, 1), :]).then_inc(stats1_ready, 1)

            def aggregate(b):
                for j in range(TPB):
                    dve.wait_ge(stats1_ready, b * TPB + (j + 1))
                    apart(dve)
                    nc.vector.bn_aggr(mv1[:, j, :], stats1[:, j, :]).then_inc(mv1_ready, 1)

            def normalize(b, tiles):
                if tiles[0] == 0:
                    dve.wait_ge(rstd1_ready, b + 1)
                    if not (isinstance(b, int) and b < 4):
                        dve.wait_ge(att_ready, (b - 3) * TPB + 1)
                for j in tiles:
                    nc.vector.tensor_scalar(nodes[:, ds(b % 4, 1), j, :], resid[:, ds(b * TPB + j, 1), :],
                                            mv1[:, j, 0:1], rstd1[:, j:j + 1], ALU.subtract,
                                            ALU.mult).then_inc(nodes_ready, 1)

            def dots(b, tiles):
                for j in tiles:
                    dve.wait_ge(nodes_ready, b * TPB + (j + 1))
                    for i in range(2):
                        if 2 * j + i >= 4 or not (isinstance(b, int) and b == 0):
                            dve.wait_ge(dots_ready, b * 2 * TPB + (2 * j + i - 3))
                        nc.vector.scalar_tensor_tensor(
                            out=dots_junk[:, (2 * j + i) % 4, :], in0=nodes[:, ds(b % 4, 1), j, :].rearrange("p b h -> p (b h)"), scalar=1.0,
                            in1=w_rows[:, i, :], op0=ALU.mult, op1=ALU.mult, accum_out=ndots[:, i, j:j + 1]).then_inc(dots_ready, 1)

            def src_bias(b):
                dve.wait_ge(dots_ready, (b + 1) * 2 * TPB)
                nc.vector.tensor_scalar(src8[:, ds(b % 2, 1), :], ndots[:, 0, :], 1 - SLOPE, b8_col[:, 0:1],
                                        ALU.mult, ALU.add).then_inc(src8_ready, 1)

            def self_loop(b, j, g):
                own = pen[:, j, j * P:(j + 1) * P].bitcast(I32)
                dve.wait_ge(adj_in[j], (b + 1) * 16)
                nc.vector.tensor_tensor(own, own, ident[:, :], ALU.add).then_inc(loop_ready, 1)

            def mask(j, g):
                dve.wait_ge(loop_ready, g + 1)
                nc.vector.tensor_scalar(pen[:, j, :], pen[:, j, :].bitcast(I32), 0.0, MASKED,
                                        ALU.is_equal, ALU.mult).then_inc(mask_ready, 1)

            def step(b, t, valid, more):
                g, j = tile_of(b, t, 16)
                if j == TPB - 1 and valid(g):
                    bb = batch_of(b, t, 16)
                    dve.wait_ge(gate_ready, g + 1)
                    nc.vector.scalar_tensor_tensor(
                        out=k.logits[:, ds(bb * TPB, TPB), :], in0=ps_gate[:, :, :],
                        scalar=1.0 / WS,
                        in1=gate_row[:, :].rearrange("p (a e) -> p a e", a=1).broadcast_to([P, TPB, E]),
                        op0=ALU.mult, op1=ALU.add).then_inc(logits_ready, 1)
                g, j = tile_of(b, t, 1)
                if valid(g):
                    dve.wait_ge(relu_ready, g + 1)
                    dve.wait_ge(pen_ready, g + 1)
                    apart(dve)
                    nc.vector.tensor_tensor_reduce(out=score[:, j % 4, :], in0=score[:, j % 4, :], in1=pen[:, j, :],
                                                   scale=1.0, scalar=-3.0e38, op0=ALU.add, op1=ALU.max,
                                                   accum_out=rowmax[:, j:j + 1]).then_inc(score_ready, 1)
                g, j = tile_of(b, t, -1)
                if valid(g) and t < TPB:
                    self_loop(batch_of(b, t, -1), j, g)
                g, j = tile_of(b, t, 1)
                if valid(g):
                    dve.wait_ge(score_ready, g + 1)
                    nc.vector.tensor_scalar(negmax[:, j:j + 1], rowmax[:, j:j + 1], -1.0, None,
                                            ALU.mult).then_inc(negmax_ready, 1)
                g, j = tile_of(b, t, -1)
                if valid(g) and t < TPB:
                    mask(j, g)
                g, j = tile_of(b, t, 3)
                if valid(g):
                    dve.wait_ge(prob_ready, g + 1)
                    nc.vector.reciprocal(rinv[:, j:j + 1], rowsum[:, j:j + 1]).then_inc(rinv_ready, 1)
                g, j = tile_of(b, t, 6)
                if valid(g):
                    dve.wait_ge(att_ready, g + 1)
                    dve.wait_ge(rinv_ready, g + 1)
                    nc.vector.scalar_tensor_tensor(out=resid[:, ds(g, 1), :].rearrange("p a h -> p (a h)"), in0=ps_att[j % 2][:, 0:H],
                                                   scalar=rinv[:, j:j + 1], in1=resid[:, ds(g, 1), :].rearrange("p a h -> p (a h)"),
                                                   op0=ALU.mult, op1=ALU.add).then_inc(resid_ready, 1)
                g, j = tile_of(b, t, 7)
                if valid(g):
                    dve.wait_ge(resid_ready, g + 1)
                    apart(dve)
                    nc.vector.bn_stats(stats2[:, j, :], resid[:, ds(g, 1), :]).then_inc(stats2_ready, 1)
                g, j = tile_of(b, t, 12)
                if valid(g):
                    dve.wait_ge(hi_ready, g + 1)
                    nc.vector.tensor_tensor(parts[:, j % 4, H:2 * H], ln2[:, j % 2, :], parts[:, j % 4, 0:H],
                                            ALU.subtract).then_inc(lo_ready, 1)
                g, j = tile_of(b, t, 8)
                if valid(g):
                    dve.wait_ge(stats2_ready, g + 1)
                    apart(dve)
                    nc.vector.bn_aggr(mv2[:, j, :], stats2[:, j, :]).then_inc(mv2_ready, 1)
                g, j = tile_of(b, t, 10)
                if valid(g):
                    dve.wait_ge(rstd2_ready, g + 1)
                    if valid(g - 2) if isinstance(g, int) else True:
                        dve.wait_ge(lo_ready, g - 1)
                    nc.vector.tensor_scalar(ln2[:, j % 2, :], resid[:, ds(g, 1), :], mv2[:, j, 0:1], rstd2[:, j:j + 1],
                                            ALU.subtract, ALU.mult).then_inc(ln2_ready, 1)
                if more:
                    if t == 0:
                        stats(b + 1, range(0, 4))
                    if t == 1:
                        stats(b + 1, range(4, 8))
                    if t == 2:
                        aggregate(b + 1)
                    if t == 3:
                        normalize(b + 1, range(0, 5))
                    if t == 4:
                        normalize(b + 1, range(5, 8))
                        dots(b + 1, range(0, 2))
                    if t == 5:
                        dots(b + 1, range(2, 5))
                    if t == 6:
                        dots(b + 1, range(5, 8))
                        src_bias(b + 1)

            dve.wait_ge(const_in, 80)
            dve.wait_ge(gate_parts_ready, 1)
            nc.vector.scalar_tensor_tensor(out=gate_parts[:, 1, :, :], in0=gate_raw[:, :, :], scalar=WS,
                                           in1=gate_parts[:, 0, :, :], op0=ALU.mult,
                                           op1=ALU.subtract).then_inc(gate_parts_ready, 1)
            nc.vector.tensor_scalar(b8_col[:, :], b_col[:, :], 1 - SLOPE, None, ALU.mult).then_inc(b8_ready, 1)
            dve.wait_ge(b8_ready, 1)
            stats(0, range(TPB))
            aggregate(0)
            normalize(0, range(TPB))
            dots(0, range(TPB))
            src_bias(0)
            self_loop(0, 0, 0)
            mask(0, 0)
            phase1(dve, step)

        @block.scalar
        def _(act):
            def dst_rows(b, h):
                act.wait_ge(dst_ready, b * TPB + (h + 1) * HT)
                if h == 0 and not (isinstance(b, int) and b < 2):
                    act.wait_ge(pen_ready, (b - 1) * TPB)
                nc.scalar.activation(dst5[:, ds(b % 2, 1), h * 512:(h + 1) * 512], ps_dst[h][:, :], ACT.Copy,
                                     scale=SLOPE).then_inc(dst5_ready, 1)

            def step(b, t, valid, more):
                g, j = tile_of(b, t, 4)
                if valid(g):
                    act.wait_ge(half_ready[0], g + 1)
                    if valid(g - 2) if isinstance(g, int) else True:
                        act.wait_ge(att_ready, g - 1)
                    nc.scalar.activation(probT[:, j % 2, 0:HT, :], ps_half[0][:, :, :], ACT.Copy).then_inc(probT_ready[0], 1)
                    act.wait_ge(half_ready[1], g + 1)
                    nc.scalar.activation(probT[:, j % 2, HT:TPB, :], ps_half[1][:, :, :], ACT.Copy).then_inc(probT_ready[1], 1)
                g, j = tile_of(b, t, 2)
                if valid(g):
                    act.wait_ge(negmax_ready, g + 1)
                    nc.scalar.activation(score[:, j % 4, :], score[:, j % 4, :], ACT.Exp, bias=negmax[:, j:j + 1],
                                         accum_out=rowsum[:, j:j + 1]).then_inc(prob_ready, 1)
                g, j = tile_of(b, t, 14)
                if valid(g):
                    act.wait_ge(xT_raw, g + 1)
                    if valid(g - 2) if isinstance(g, int) else True:
                        act.wait_ge(gate_ready, g - 1)
                    nc.scalar.activation(xT[:, j % 2, :, :], ps_xT[:, :, :], ACT.Copy).then_inc(xT_ready, 1)
                g, j = tile_of(b, t, 0)
                if t < TPB:
                    if t == 0:
                        act.wait_ge(src8_ready, b + 1)
                        act.wait_ge(dst5_ready, (b + 1) * 2)
                    if valid(g - 4) if isinstance(g, int) else True:
                        act.wait_ge(half_ready[1], g - 3)
                    nc.scalar.activation(score[:, j % 4, :], dst5[:, ds(b % 2, 1), :], ACT.Relu,
                                         bias=src8[:, ds(b % 2, 1), j], scale=(1 - SLOPE) / SLOPE).then_inc(relu_ready, 1)
                g, j = tile_of(b, t, 11)
                if valid(g):
                    act.wait_ge(ln2_ready, g + 1)
                    if not (isinstance(g, int) and g < 4):
                        act.wait_ge(parts_out[j % 4], (batch_of(b, t, 11) * 2 + j // 4) * 16)
                        act.wait_ge(xT_raw, g - 3)
                    nc.scalar.activation(parts[:, j % 4, 0:H], ln2[:, j % 2, :], ACT.Copy).then_inc(hi_ready, 1)
                if more and t == TPB - 1:
                    dst_rows(b + 1, 0)
                    dst_rows(b + 1, 1)

            act.wait_ge(const_in, 80)
            nc.scalar.activation(gate_parts[:, 0, :, :], gate_raw[:, :, :], ACT.Copy, scale=WS).then_inc(gate_parts_ready, 1)
            dst_rows(0, 0)
            dst_rows(0, 1)
            phase1(act, step)

        @block.tensor
        def _(pe):
            def spread_dst(b, tiles):
                for j in tiles:
                    pe.wait_ge(diag_ready, b * TPB + (j + 1))
                    if j % HT == 0 and not (isinstance(b, int) and b == 0):
                        pe.wait_ge(dst5_ready, b * 2 + (j // HT - 1))
                    nc.tensor.matmul(ps_dst[j // HT][:, (j % HT) * P:(j % HT + 1) * P], ones[:, :],
                                     diag[:, j % 4, :], start=True, stop=True).then_inc(dst_ready, 1)

            def step(b, t, valid, more):
                g, j = tile_of(b, t, 5)
                if valid(g):
                    pe.wait_ge(probT_ready[0], g + 1)
                    if valid(g - 2) if isinstance(g, int) else True:
                        pe.wait_ge(resid_ready, g - 1)
                    if j == 0:
                        pe.wait_ge(nodes_ready, (batch_of(b, t, 5) + 1) * TPB)
                    for k in range(TPB):
                        if k == HT:
                            pe.wait_ge(probT_ready[1], g + 1)
                        ins = nc.tensor.matmul(ps_att[j % 2][:, 0:H], probT[:, j % 2, k, :],
                                               nodes[:, ds(batch_of(b, t, 5) % 4, 1), k, :].rearrange("p b h -> p (b h)"),
                                               start=(k == 0), stop=(k == TPB - 1))
                    ins.then_inc(att_ready, 1)
                g, j = tile_of(b, t, 3)
                if valid(g):
                    pe.wait_ge(prob_ready, g + 1)
                    for h in range(2):
                        if valid(g - 1) if isinstance(g, int) else True:
                            pe.wait_ge(probT_ready[h], g)
                        for k in range(HT):
                            c = h * HT + k
                            ins = nc.tensor.transpose(ps_half[h][:, k, :], score[:, j % 4, c * P:(c + 1) * P], ident[:, :])
                        ins.then_inc(half_ready[h], 1)
                g, j = tile_of(b, t, 13)
                if valid(g):
                    pe.wait_ge(lo_ready, g + 1)
                    if valid(g - 1) if isinstance(g, int) else True:
                        pe.wait_ge(xT_ready, g)
                    for c in range(2 * KT):
                        ins = nc.tensor.transpose(ps_xT[:, c, :], parts[:, j % 4, c * P:(c + 1) * P], ident16[:, :])
                    ins.then_inc(xT_raw, 1)
                g, j = tile_of(b, t, 15)
                if valid(g):
                    bb = batch_of(b, t, 15)
                    pe.wait_ge(xT_ready, g + 1)
                    if j == 0 and not (isinstance(bb, int) and bb == 0):
                        pe.wait_ge(logits_ready, bb)
                    terms = [(c, xp, wp) for xp, wp in ((0, 0), (0, 1), (1, 0)) for c in range(KT)]
                    for n, (c, xp, wp) in enumerate(terms):
                        ins = nc.tensor.matmul(ps_gate[:, j, :],
                                               xT[:, j % 2, xp * KT + c, :], gate_parts[:, wp, c, :],
                                               start=(n == 0), stop=(n == len(terms) - 1))
                    ins.then_inc(gate_ready, 1)
                if more and t == 5:
                    spread_dst(b + 1, range(0, 2))
                if more and t == 6:
                    spread_dst(b + 1, range(2, 5))
                if more and t == 7:
                    spread_dst(b + 1, range(5, 8))

            pe.wait_ge(consts_ready, 4)
            pe.wait_ge(gate_parts_ready, 2)
            spread_dst(0, range(TPB))
            phase1(pe, step)


def expert_phases(nc, k, sw1, sb1, sw2, sb2, sact, ew1, eb1, ew2, eb2, eact, out):
    E, H, I2 = ew1.shape
    I = I2 // 2
    KT = H // P
    IT = 2
    IP = I // IT
    B, N, _ = out.shape
    TPB = N // P
    NT = B * TPB
    ST = k.expert_x.shape[0] // P
    U = 4
    resid, ident, ident16, ones, logits = k.resid, k.ident, k.ident16, k.ones, k.logits
    YS = WS * TS
    LAST = 9
    PEELED = -(-(LAST + 1) // U)

    ctx = ExitStack()
    with ctx:
        def sb(name, shape, dt=F32):
            return ctx.enter_context(nc.sbuf_tensor(name, shape, dt))

        def sem(name):
            return ctx.enter_context(nc.semaphore(name))

        slot = sb("slot", [P, 2, NT], I32)
        share = sb("share", [P, 2, NT])
        tile_expert = sb("tile_expert", [P, ST], I32)
        par = sb("par", [P, 7, E + 1])

        routed = sem("routed")

        rctx = ExitStack()
        with rctx:
            def rsb(name, shape, dt=F32):
                return rctx.enter_context(nc.sbuf_tensor(name, shape, dt))

            def rsem(name):
                return rctx.enter_context(nc.semaphore(name))

            NB = ST // 2 - E // 2
            eid = rsb("eid", [P, E])
            steps_row = rsb("steps_row", [P, NB])
            tiles_row = rsb("tiles_row", [P, ST])
            upper = rsb("upper", [P, P])
            hit = rsb("hit", [P, NT, E])
            cand = rsb("cand", [P, NT, E])
            chosen = [rsb(f"chosen{i}", [P, NT, E]) for i in range(2)]
            both = rsb("both", [P, E, NT])
            place = rsb("place", [P, E, NT])
            big = rsb("big", [P, ST, E])
            best = [rsb(f"best{i}", [P, NT]) for i in range(2)]
            pick = [rsb(f"pick{i}", [P, NT]) for i in range(2)]
            slot_f = rsb("slot_f", [P, 2, NT])
            small = rsb("small", [P, 12, E])
            tile_f = rsb("tile_f", [P, ST])
            gap = rsb("gap", [P, NT])
            act_raw = rsb("act_raw", [P, E + 1, 5])
            soft = rsb("soft", [P, 6, 2, E + 1])
            ps_count = rctx.enter_context(nc.psum_tensor("ps_count", [P, 2, E], F32))

            loaded = rsem("loaded")
            made = rsem("made")
            upper_ready = rsem("upper_ready")
            counted = rsem("counted")
            prefixed = rsem("prefixed")
            gap_ready = rsem("gap_ready")
            odds_ready = rsem("odds_ready")
            soft_in = rsem("soft_in")
            soft_exp = rsem("soft_exp")
            soft_ln = rsem("soft_ln")
            chain = rsem("chain")

            block = rctx.enter_context(nc.Block())

            @block.sync
            def _(sp):
                sp.dma_start(act_raw[:, 0:E, :].rearrange("p e c -> p (e c)"),
                             eact.rearrange("(a e) c -> a (e c)", a=1).broadcast_to([P, E * 5])).then_inc(loaded, 16)
                sp.dma_start(act_raw[:, E, :], sact.rearrange("(a c) -> a c", a=1).broadcast_to([P, 5])).then_inc(loaded, 16)

            @block.gpsimd
            def _(pool):
                nc.gpsimd.iota(eid[:, :], [[1, E]], base=-E, channel_multiplier=0,
                               allow_small_or_imprecise_dtypes=True).then_inc(made, 1)
                nc.gpsimd.iota(steps_row[:, :], [[P, NB]], base=0, channel_multiplier=0,
                               allow_small_or_imprecise_dtypes=True).then_inc(made, 1)
                nc.gpsimd.iota(tiles_row[:, :], [[1, ST]], base=0, channel_multiplier=0,
                               allow_small_or_imprecise_dtypes=True).then_inc(made, 1)
                nc.gpsimd.affine_select(out=upper[:, :], in_=ones[:, :], compare_op=ALU.is_gt, fill=0.0,
                                        base=0, pattern=[[1, P]], channel_multiplier=-1).then_inc(upper_ready, 1)

            @block.tensor
            def _(pe):
                pe.wait_ge(upper_ready, 1)
                pe.wait_ge(counted, 1)
                nc.tensor.matmul(ps_count[:, 0, :], upper[:, :], small[:, 0, :], start=True, stop=True)
                nc.tensor.matmul(ps_count[:, 1, :], ones[:, :], small[:, 0, :], start=True, stop=True).then_inc(prefixed, 1)

            @block.scalar
            def _(act):
                act.wait_ge(gap_ready, 1)
                nc.scalar.activation(gap[:, :], gap[:, :], ACT.Exp).then_inc(odds_ready, 1)
                act.wait_ge(soft_in, 1)
                nc.scalar.activation(soft[:, 2, :, :], soft[:, 1, :, :], ACT.Exp).then_inc(soft_exp, 1)
                act.wait_ge(soft_exp, 1)
                nc.scalar.activation(soft[:, 3, :, :], soft[:, 2, :, :], ACT.Ln, bias=ones[:, 0:1]).then_inc(soft_ln, 1)

            @block.vector
            def _(dve):
                count = [0]

                def link(ins):
                    count[0] += 1
                    ins.then_inc(chain, 1)
                    dve.wait_ge(chain, count[0])

                def over_tiles(a):
                    return a.rearrange("p (a e) -> p a e", a=1).broadcast_to([P, NT, E])

                def over_experts(a):
                    return a.rearrange("p (t a) -> p t a", a=1).broadcast_to([P, NT, E])

                dve.wait_ge(made, 3)
                source = logits
                for i in range(2):
                    link(nc.vector.tensor_reduce(best[i][:, :], source[:, :, :], AX_X, ALU.max))
                    link(nc.vector.tensor_tensor(hit[:, :, :], source[:, :, :], over_experts(best[i][:, :]), ALU.is_equal))
                    link(nc.vector.tensor_tensor(hit[:, :, :], hit[:, :, :], over_tiles(eid[:, :]), ALU.mult))
                    link(nc.vector.tensor_reduce(pick[i][:, :], hit[:, :, :], AX_X, ALU.min))
                    link(nc.vector.tensor_tensor(chosen[i][:, :, :], over_tiles(eid[:, :]), over_experts(pick[i][:, :]),
                                                 ALU.is_equal))
                    if i == 0:
                        link(nc.vector.scalar_tensor_tensor(out=cand[:, :, :], in0=chosen[0][:, :, :], scalar=-1.0e30,
                                                            in1=logits[:, :, :], op0=ALU.mult, op1=ALU.add))
                        source = cand
                link(nc.vector.tensor_tensor(both[:, :, :].rearrange("p e t -> p t e"), chosen[0][:, :, :],
                                             chosen[1][:, :, :], ALU.add))
                nc.vector.tensor_reduce(small[:, 0, :], both[:, :, :], AX_X, ALU.add).then_inc(counted, 1)
                nc.vector.tensor_tensor(gap[:, :], best[1][:, :], best[0][:, :], ALU.subtract).then_inc(gap_ready, 1)
                flat = both[:, :, :].rearrange("p e t -> p (e t)")
                link(nc.vector.tensor_tensor_scan(place[:, :, :].rearrange("p e t -> p (e t)"), flat, flat, 0.0,
                                                  ALU.add, ALU.max))
                dve.wait_ge(counted, 1)
                link(nc.vector.tensor_tensor_scan(small[:, 1, :], small[:, 0, :], small[:, 0, :], 0.0, ALU.add, ALU.max))
                dve.wait_ge(prefixed, 1)
                link(nc.vector.tensor_copy(small[:, 2:4, :], ps_count[:, :, :]))
                fills = big[:, 0:NB, :].rearrange("p n e -> p e n")
                link(nc.vector.tensor_tensor(fills, small[:, 3, :].rearrange("p (e a) -> p e a", a=1).broadcast_to([P, E, NB]),
                                             steps_row[:, :].rearrange("p (a n) -> p a n", a=1).broadcast_to([P, E, NB]),
                                             ALU.is_gt))
                link(nc.vector.tensor_reduce(small[:, 4, :], fills, AX_X, ALU.add))
                link(nc.vector.tensor_tensor_scan(small[:, 5, :], small[:, 4, :], small[:, 4, :], 0.0, ALU.add, ALU.max))
                link(nc.vector.tensor_tensor(small[:, 6, :], small[:, 5, :], small[:, 4, :], ALU.subtract))
                link(nc.vector.scalar_tensor_tensor(out=small[:, 7, :], in0=small[:, 6, :], scalar=float(P),
                                                    in1=small[:, 2, :], op0=ALU.mult, op1=ALU.add))
                link(nc.vector.tensor_tensor(small[:, 8, :], small[:, 0, :], small[:, 1, :], ALU.subtract))
                link(nc.vector.scalar_tensor_tensor(out=small[:, 9, :], in0=small[:, 8, :], scalar=-1.0,
                                                    in1=small[:, 7, :], op0=ALU.add, op1=ALU.add))
                link(nc.vector.tensor_tensor(place[:, :, :], place[:, :, :],
                                             small[:, 9, :].rearrange("p (e a) -> p e a", a=1).broadcast_to([P, E, NT]),
                                             ALU.add))
                for i in range(2):
                    link(nc.vector.tensor_tensor(hit[:, :, :], chosen[i][:, :, :], place[:, :, :].rearrange("p e t -> p t e"),
                                                 ALU.mult))
                    link(nc.vector.tensor_reduce(slot_f[:, i, :], hit[:, :, :], AX_X, ALU.add))
                nc.vector.tensor_copy(slot[:, :, :], slot_f[:, :, :]).then_inc(routed, 1)
                link(nc.vector.tensor_tensor(big[:, :, :], small[:, 5, :].rearrange("p (a e) -> p a e", a=1).broadcast_to([P, ST, E]),
                                             tiles_row[:, :].rearrange("p (n a) -> p n a", a=1).broadcast_to([P, ST, E]),
                                             ALU.is_le))
                link(nc.vector.tensor_reduce(tile_f[:, :], big[:, :, :], AX_X, ALU.add))
                nc.vector.tensor_scalar(tile_expert[:, :], tile_f[:, :], float(E - 1), None, ALU.min).then_inc(routed, 1)
                dve.wait_ge(odds_ready, 1)
                link(nc.vector.tensor_scalar(best[0][:, :], gap[:, :], 1.0, None, ALU.add))
                link(nc.vector.reciprocal(share[:, 0, :], best[0][:, :]))
                nc.vector.tensor_tensor(share[:, 1, :], gap[:, :], share[:, 0, :], ALU.mult).then_inc(routed, 1)
                dve.wait_ge(loaded, 32)
                raw = act_raw[:, :, :].rearrange("p e c -> p c e")
                link(nc.vector.tensor_scalar(soft[:, 0, :, :], raw[:, 3:5, :], -1.0, None, ALU.mult))
                nc.vector.tensor_tensor(soft[:, 1, :, :], raw[:, 3:5, :], soft[:, 0, :, :], ALU.min).then_inc(soft_in, 1)
                link(nc.vector.tensor_scalar(soft[:, 4, :, :], raw[:, 3:5, :], 0.0, None, ALU.max))
                dve.wait_ge(soft_ln, 1)
                link(nc.vector.tensor_tensor(soft[:, 5, :, :], soft[:, 3, :, :], soft[:, 4, :, :], ALU.add))
                nc.vector.tensor_scalar(par[:, 0:2, :], soft[:, 5, :, :], WS, None, ALU.mult).then_inc(routed, 1)
                nc.vector.tensor_scalar(par[:, 2:4, :], soft[:, 5, :, :], -WS, None, ALU.mult).then_inc(routed, 1)
                nc.vector.tensor_scalar(par[:, 4, :], raw[:, 2, :], WS, None, ALU.mult).then_inc(routed, 1)
                nc.vector.tensor_scalar(par[:, 5, :], raw[:, 0, :], 1.0 / WS, None, ALU.mult).then_inc(routed, 1)
                nc.vector.tensor_scalar(par[:, 6, :], raw[:, 1, :], TS / (WS * WS), None, ALU.mult).then_inc(routed, 1)

        idx = sb("idx", [P, U, 2], I32)

        wctx = ctx.enter_context(ExitStack())

        def wsb(name, shape, dt=F32):
            return wctx.enter_context(nc.sbuf_tensor(name, shape, dt))

        w1 = wsb("w1", [P, E + 1, KT, 2, I2], F16)
        w2 = wsb("w2", [IP + 2, E + 1, IT, 2, H], F16)
        b1 = wsb("b1", [2, E + 1, I2], F16)
        xrow = wsb("xrow", [P, U, 2 * H], F16)
        xT = wsb("rows_T", [P, U, 2 * KT, P], F16)
        gated = wsb("gated", [P, U, I])
        up = wsb("up", [P, U, I])
        sig = wsb("sig", [P, U, I])
        hid = wsb("hid", [P, U, I])
        hidT = wsb("hidT", [IP + 2, U, 2, IT, P], F16)
        two16 = wsb("two16", [2, P], F16)
        y = wsb("y", [P, U, H])

        def run_tiles(eng, tiles, step, lag):
            for q in range(PEELED):
                for u in range(U):
                    step(q, u, lambda n: n >= 0)
            with eng.Fori(PEELED, tiles // U) as q:
                for u in range(U):
                    step(q, u, lambda n: True)
            for u in range(U, U + lag):
                step(tiles // U - 1, u, lambda n: n < tiles)

        def since(n, before):
            return not isinstance(n, int) or n >= before

        class Signals:

            def __init__(self, name, enter):
                self.xT_raw = enter(nc.semaphore(name + "xT_raw"))
                self.xT_ready = enter(nc.semaphore(name + "xT_ready"))
                self.up_done = enter(nc.semaphore(name + "up_done"))
                self.gated_ready = enter(nc.semaphore(name + "gated_ready"))
                self.up_ready = enter(nc.semaphore(name + "up_ready"))
                self.sig_ready = enter(nc.semaphore(name + "sig_ready"))
                self.prod_ready = enter(nc.semaphore(name + "prod_ready"))
                self.hid_ready = enter(nc.semaphore(name + "hid_ready"))
                self.hidT_raw = enter(nc.semaphore(name + "hidT_raw"))
                self.hidT_high = enter(nc.semaphore(name + "hidT_high"))
                self.hidT_ready = enter(nc.semaphore(name + "hidT_ready"))
                self.down_done = enter(nc.semaphore(name + "down_done"))
                self.y_taken = enter(nc.semaphore(name + "y_taken"))

        def feed_forward(s, psums, tiles, expert_of, x_wait, x_slot_free, take_y, y_engine, prepare):
            ps_xT, ps_h, ps_hT, ps_y = psums
            terms = [(c, xp, wp) for xp, wp in ((0, 0), (0, 1), (1, 0)) for c in range(KT)]
            hid_terms = [(c, xp, wp) for xp, wp in ((0, 0), (0, 1), (1, 0)) for c in range(IT)]

            def at(q, u, lag):
                return q * U + (u - lag), (u - lag) % 2, (u - lag) % U

            def tensor_step(pe):
                def step(q, u, valid):
                    n, b, v = at(q, u, 2)
                    if valid(n):
                        e = expert_of(pe, n)
                        pe.wait_ge(s.xT_ready, n + 1)
                        if since(n, 2):
                            pe.wait_ge(s.up_ready, n - 1)
                        nc.tensor.matmul(ps_h[b][:, :], two16[:, :], b1[:, ds(e, 1), :].rearrange("p e i -> p (e i)"),
                                         start=True, stop=False)
                        for i, (c, xp, wp) in enumerate(terms):
                            ins = nc.tensor.matmul(ps_h[b][:, :], xT[:, v, xp * KT + c, :],
                                                   w1[:, ds(e, 1), c, wp, :].rearrange("p e i -> p (e i)"),
                                                   start=False, stop=(i == len(terms) - 1))
                        ins.then_inc(s.up_done, 1)
                    n, b, v = at(q, u, 6)
                    if valid(n):
                        pe.wait_ge(s.hid_ready, n + 1)
                        if since(n, 2):
                            pe.wait_ge(s.hidT_ready, n - 1)
                        for c in range(IT):
                            ins = nc.tensor.transpose(ps_hT[b][:, c, :], hid[:, v, c * IP:(c + 1) * IP], ident[:, :])
                        ins.then_inc(s.hidT_raw, 1)
                    n, b, v = at(q, u, 8)
                    if valid(n):
                        e = expert_of(pe, n)
                        pe.wait_ge(s.hidT_ready, n + 1)
                        if since(n, 2):
                            pe.wait_ge(s.y_taken, n - 1)
                        for i, (c, xp, wp) in enumerate(hid_terms):
                            rows = IP + 2 if i == 0 else IP
                            ins = nc.tensor.matmul(ps_y[b][:, :], hidT[0:rows, v, xp, c, :],
                                                   w2[0:rows, ds(e, 1), c, wp, :].rearrange("p e h -> p (e h)"),
                                                   start=(i == 0), stop=(i == len(hid_terms) - 1))
                        ins.then_inc(s.down_done, 1)
                    n, b, v = at(q, u, 0)
                    if u < U:
                        x_wait(pe, q, u, n)
                        if since(n, 2):
                            pe.wait_ge(s.xT_ready, n - 1)
                        for c in range(2 * KT):
                            ins = nc.tensor.transpose(ps_xT[b][:, c, :], xrow[:, u, c * P:(c + 1) * P], ident16[:, :])
                        ins.then_inc(s.xT_raw, 1)
                run_tiles(pe, tiles, step, LAST)

            def scalar_step(act):
                def step(q, u, valid):
                    n, b, v = at(q, u, 7)
                    if valid(n):
                        act.wait_ge(s.hidT_raw, n + 1)
                        if since(n, U):
                            act.wait_ge(s.down_done, n - (U - 1))
                        nc.scalar.activation(hidT[0:IP, v, 0, :, :], ps_hT[b][:, :, :], ACT.Copy).then_inc(s.hidT_high, 1)
                    n, b, v = at(q, u, 1)
                    if valid(n):
                        act.wait_ge(s.xT_raw, n + 1)
                        if since(n, U):
                            act.wait_ge(s.up_done, n - (U - 1))
                        nc.scalar.activation(xT[:, v, :, :], ps_xT[b][:, :, :], ACT.Copy).then_inc(s.xT_ready, 1)
                    n, b, v = at(q, u, 4)
                    if valid(n):
                        e = expert_of(act, n)
                        act.wait_ge(s.gated_ready, n + 1)
                        if since(n, U):
                            act.wait_ge(s.hid_ready, n - (U - 1))
                        nc.scalar.activation(sig[:, v, :], gated[:, v, :], ACT.Sigmoid,
                                             scale=par[:, 5, ds(e, 1)]).then_inc(s.sig_ready, 1)
                    n, b, v = at(q, u, 9)
                    if valid(n) and y_engine == "scalar":
                        act.wait_ge(s.down_done, n + 1)
                        take_y(act, s, q, u - 9, n, ps_y[b])
                    if prepare:
                        prepare(act, q, u)
                run_tiles(act, tiles, step, LAST)

            def vector_step(dve):
                def step(q, u, valid):
                    n, b, v = at(q, u, 3)
                    if valid(n):
                        e = expert_of(dve, n)
                        dve.wait_ge(s.up_done, n + 1)
                        if since(n, U):
                            dve.wait_ge(s.sig_ready, n - (U - 1))
                            dve.wait_ge(s.hid_ready, n - (U - 1))
                        nc.vector.tensor_scalar(gated[:, v, :], ps_h[b][:, 0:I], par[:, 2, ds(e, 1)], par[:, 0, ds(e, 1)],
                                                ALU.max, ALU.min).then_inc(s.gated_ready, 1)
                        nc.vector.tensor_scalar(up[:, v, :], ps_h[b][:, I:I2], par[:, 3, ds(e, 1)], par[:, 1, ds(e, 1)],
                                                ALU.max, ALU.min).then_inc(s.up_ready, 1)
                    m, b, v = at(q, u, 7)
                    if valid(m):
                        dve.wait_ge(s.hidT_high, m + 1)
                        nc.vector.tensor_tensor(hidT[0:IP, v, 1, :, :], ps_hT[b][:, :, :], hidT[0:IP, v, 0, :, :],
                                                ALU.subtract).then_inc(s.hidT_ready, 1)
                    n, b, v = at(q, u, 3)
                    if valid(n):
                        dve.wait_ge(s.gated_ready, n + 1)
                        dve.wait_ge(s.up_ready, n + 1)
                        nc.vector.scalar_tensor_tensor(out=up[:, v, :], in0=up[:, v, :], scalar=par[:, 4, ds(e, 1)],
                                                       in1=gated[:, v, :], op0=ALU.add, op1=ALU.mult
                                                       ).then_inc(s.prod_ready, 1)
                    m, b, v = at(q, u, 5)
                    if valid(m):
                        e = expert_of(dve, m)
                        dve.wait_ge(s.prod_ready, m + 1)
                        dve.wait_ge(s.sig_ready, m + 1)
                        if since(m, U):
                            dve.wait_ge(s.hidT_raw, m - (U - 1))
                        nc.vector.scalar_tensor_tensor(out=hid[:, v, :], in0=up[:, v, :], scalar=par[:, 6, ds(e, 1)],
                                                       in1=sig[:, v, :], op0=ALU.mult, op1=ALU.mult
                                                       ).then_inc(s.hid_ready, 1)
                    n, b, v = at(q, u, 9)
                    if valid(n) and y_engine == "vector":
                        dve.wait_ge(s.down_done, n + 1)
                        take_y(dve, s, q, u - 9, n, ps_y[b])
                    if prepare:
                        prepare(dve, q, u)
                run_tiles(dve, tiles, step, LAST)

            return tensor_step, scalar_step, vector_step

        def psum_banks(c, prefix):
            return [[c.enter_context(nc.psum_tensor(f"{prefix}{name}{i}", shape, dt)) for i in range(2)]
                    for name, shape, dt in (("ps_xT", [P, 2 * KT, P], F16), ("ps_h", [P, I2], F32),
                                            ("ps_hT", [IP, IT, P], F32), ("ps_y", [P, H], F32))]

        sctx = ExitStack()
        with sctx:
            def ssem(name):
                return sctx.enter_context(nc.semaphore(name))

            raw1 = sctx.enter_context(nc.sbuf_tensor("raw1", [P, KT, I2], F32))
            raw2 = sctx.enter_context(nc.sbuf_tensor("raw2", [IP, IT, H], F32))
            bias_raw = sctx.enter_context(nc.sbuf_tensor("bias_raw", [E + 1, I2 + H], F32))
            bias_parts = sctx.enter_context(nc.sbuf_tensor("bias_parts", [E + 1, 2, I2 + H], F16))
            psums = psum_banks(sctx, "s_")
            s = Signals("s_", sctx.enter_context)
            x_in = [ssem(f"rows_in{i}") for i in range(U)]
            scattered = [ssem(f"scattered{i}") for i in range(U)]
            idx_ready = ssem("idx_ready")
            two_ready = ssem("two_ready")
            raw1_in = ssem("raw1_in")
            raw2_in = ssem("raw2_in")
            w1_high = ssem("w1_high")
            w1_ready = ssem("w1_ready")
            w2_high = ssem("w2_high")
            w2_ready = ssem("w2_ready")
            bias_in = ssem("bias_in")
            bias_high = ssem("bias_high")
            bias_low = ssem("bias_low")
            bias_stored = ssem("bias_stored")
            bias_ready = ssem("bias_ready")

            def split(eng, e, nth):
                paired = raw1[:, :, :].rearrange("p k (i two) -> p k two i", two=2)
                if eng is nc.scalar:
                    eng.wait_ge(raw1_in, (nth + 1) * 16)
                    nc.scalar.activation(w1[:, ds(e, 1), :, 0, :].rearrange("p e k (two i) -> p (e k) two i", two=2), paired,
                                         ACT.Copy, scale=WS).then_inc(w1_high, 1)
                    eng.wait_ge(raw2_in, (nth + 1) * 16)
                    nc.scalar.activation(w2[0:IP, ds(e, 1), :, 0, :].rearrange("p e c h -> p (e c) h"), raw2[:, :, :],
                                         ACT.Copy, scale=WS).then_inc(w2_high, 1)
                else:
                    eng.wait_ge(w1_high, nth + 1)
                    for c in range(KT):
                        nc.vector.scalar_tensor_tensor(
                            out=w1[:, ds(e, 1), c, 1, :].rearrange("p e (two i) -> p (e two) i", two=2), in0=paired[:, c, :, :],
                            scalar=WS, in1=w1[:, ds(e, 1), c, 0, :].rearrange("p e (two i) -> p (e two) i", two=2),
                            op0=ALU.mult, op1=ALU.subtract).then_inc(w1_ready, 1)
                    eng.wait_ge(w2_high, nth + 1)
                    nc.vector.scalar_tensor_tensor(
                        out=w2[0:IP, ds(e, 1), :, 1, :].rearrange("p e c h -> p (e c) h"), in0=raw2[:, :, :], scalar=WS,
                        in1=w2[0:IP, ds(e, 1), :, 0, :].rearrange("p e c h -> p (e c) h"),
                        op0=ALU.mult, op1=ALU.subtract).then_inc(w2_ready, 1)

            def split_in_loop(eng, q, u):
                if u == U - 1:
                    split(eng, q, q + 1)

            def shared_x_wait(eng, q, u, n):
                eng.wait_ge(x_in[u], (q + 1) * 16)

            def add_shared(dve, s, q, u, n, bank):
                nc.vector.scalar_tensor_tensor(out=resid[:, ds(n, 1), :].rearrange("p t h -> p (t h)"), in0=bank[:, :],
                                               scalar=1.0 / YS, in1=resid[:, ds(n, 1), :].rearrange("p t h -> p (t h)"),
                                               op0=ALU.mult, op1=ALU.add).then_inc(s.y_taken, 1)

            tensor_run, scalar_run, vector_run = feed_forward(
                s, psums, NT, lambda eng, n: E, shared_x_wait, None, add_shared, "vector", split_in_loop)

            apart = Apart("scatter")
            block = sctx.enter_context(nc.Block())

            @block.sync
            def _(sp):
                def load_raw(w1_d, w2_d, nth):
                    if not (isinstance(nth, int) and nth == 0):
                        sp.wait_ge(w1_ready, nth * KT)
                    sp.dma_start(raw1[:, :, :], w1_d).then_inc(raw1_in, 16)
                    if not (isinstance(nth, int) and nth == 0):
                        sp.wait_ge(w2_ready, nth)
                    sp.dma_start(raw2[:, :, :], w2_d).then_inc(raw2_in, 16)

                sp.dma_start(bias_raw[0:E, 0:I2], eb1).then_inc(bias_in, 16)
                sp.dma_start(bias_raw[E:E + 1, 0:I2], sb1.rearrange("(a i) -> a i", a=1)).then_inc(bias_in, 16)
                sp.dma_start(bias_raw[0:E, I2:I2 + H], eb2).then_inc(bias_in, 16)
                sp.dma_start(bias_raw[E:E + 1, I2:I2 + H], sb2.rearrange("(a h) -> a h", a=1)).then_inc(bias_in, 16)
                load_raw(sw1.rearrange("(k p) i -> p k i", p=P), sw2.rearrange("(c p) h -> p c h", p=IP), 0)
                sp.wait_ge(bias_low, 2)
                for i in range(2):
                    sp.dma_start(k.bias_rows[i], bias_parts[:, i, :]).then_inc(bias_stored, 16)
                sp.wait_ge(bias_stored, 32)
                sp.dma_start(b1[:, :, :], k.bias_rows[:, :, 0:I2]).then_inc(bias_ready, 16)
                sp.dma_start(w2[IP:IP + 2, :, 0, 0, :], k.bias_rows[:, :, I2:I2 + H]).then_inc(bias_ready, 16)

                done = sp.alloc_register("scatters_done")
                sp.reg_mov(done, 0)

                def step(q, u, valid):
                    n = q * U + u
                    if u == 0 and since(n, U):
                        sp.reg_alu(done, done, 32, ALU.add)
                    if since(n, U):
                        sp.wait_ge(s.xT_raw, n - (U - 1))
                        sp.wait_ge(scattered[u], done)
                    sp.dma_start(xrow[:, u, :], k.token_x[ds(n, 1)].rearrange("t p c -> p (t c)")).then_inc(x_in[u], 16)
                    if u == U - 1:
                        load_raw(ew1[ds(q, 1)].rearrange("e (k p) i -> p (e k) i", p=P),
                                 ew2[ds(q, 1)].rearrange("e (c p) h -> p (e c) h", p=IP), q + 1)
                run_tiles(sp, NT, step, 0)

            @block.gpsimd
            def _(pool):
                nc.gpsimd.memset(two16[:, :], 1.0).then_inc(two_ready, 1)
                nc.gpsimd.memset(hidT[IP:IP + 2, :, 0, 0, :], 1.0).then_inc(two_ready, 1)
                pool.wait_ge(two_ready, 2)

                def step(q, u, valid):
                    n = q * U + u
                    if since(n, U):
                        pool.wait_ge(scattered[u], q * 32)
                    nc.gpsimd.tensor_copy(idx[:, u, :], slot[:, :, ds(n, 1)].rearrange("p c n -> p (c n)")).then_inc(idx_ready, 1)
                    pool.wait_ge(x_in[u], (q + 1) * 16)
                    pool.wait_ge(idx_ready, n + 1)
                    apart(pool)
                    for i in range(2):
                        nc.gpsimd.indirect_dma_start(
                            out=k.expert_x[:, :], out_offset=bass.IndirectOffsetOnAxis(ap=idx[:, u, i:i + 1], axis=0),
                            in_=xrow[:, u, :], in_offset=None).then_inc(scattered[u], 16)
                run_tiles(pool, NT, step, 0)
                apart.end(pool, idx_ready)
                for u in range(U):
                    pool.wait_ge(scattered[u], NT // U * 32)

            @block.tensor
            def _(pe):
                pe.wait_ge(two_ready, 2)
                pe.wait_ge(w1_ready, KT)
                pe.wait_ge(w2_ready, 1)
                pe.wait_ge(bias_ready, 32)
                tensor_run(pe)

            @block.scalar
            def _(act):
                act.wait_ge(bias_in, 64)
                nc.scalar.activation(bias_parts[:, 0, 0:I2].rearrange("p (two i) -> p two i", two=2),
                                     bias_raw[:, 0:I2].rearrange("p (i two) -> p two i", two=2), ACT.Copy,
                                     scale=WS).then_inc(bias_high, 1)
                nc.scalar.activation(bias_parts[:, 0, I2:I2 + H], bias_raw[:, I2:I2 + H], ACT.Copy,
                                     scale=YS).then_inc(bias_high, 1)
                split(nc.scalar, E, 0)
                scalar_run(act)

            @block.vector
            def _(dve):
                dve.wait_ge(bias_high, 2)
                nc.vector.scalar_tensor_tensor(out=bias_parts[:, 1, 0:I2].rearrange("p (two i) -> p two i", two=2),
                                               in0=bias_raw[:, 0:I2].rearrange("p (i two) -> p two i", two=2), scalar=WS,
                                               in1=bias_parts[:, 0, 0:I2].rearrange("p (two i) -> p two i", two=2),
                                               op0=ALU.mult, op1=ALU.subtract).then_inc(bias_low, 1)
                nc.vector.scalar_tensor_tensor(out=bias_parts[:, 1, I2:I2 + H], in0=bias_raw[:, I2:I2 + H], scalar=YS,
                                               in1=bias_parts[:, 0, I2:I2 + H],
                                               op0=ALU.mult, op1=ALU.subtract).then_inc(bias_low, 1)
                split(nc.vector, E, 0)
                vector_run(dve)

        ectx = ExitStack()
        with ectx:
            psums = psum_banks(ectx, "e_")
            s = Signals("e_", ectx.enter_context)
            x_in = [ectx.enter_context(nc.semaphore(f"e_rows_in{i}")) for i in range(U)]
            y_out = [ectx.enter_context(nc.semaphore(f"e_y_out{i}")) for i in range(U)]

            def routed_expert(eng, n):
                return eng.value_load(tile_expert[0:1, ds(n, 1)], min_val=0, max_val=E - 1)

            def expert_x_wait(eng, q, u, n):
                eng.wait_ge(x_in[u], (q + 1) * 16)

            def store_y(act, s, q, u, n, bank):
                if since(n, U):
                    act.wait_ge(y_out[u % U], (q + u // U) * 16)
                nc.scalar.activation(y[:, u % U, :], bank[:, :], ACT.Copy, scale=1.0 / YS).then_inc(s.y_taken, 1)

            tensor_run, scalar_run, vector_run = feed_forward(
                s, psums, ST, routed_expert, expert_x_wait, None, store_y, "scalar", None)

            block = ectx.enter_context(nc.Block())

            @block.sync
            def _(sp):
                def step(q, u, valid):
                    n = q * U + u
                    if u < U:
                        if since(n, U):
                            sp.wait_ge(s.xT_raw, n - (U - 1))
                        sp.dma_start(xrow[:, u, :], k.expert_x[ds(n * P, P), :]).then_inc(x_in[u], 16)
                    n = q * U + (u - LAST)
                    if valid(n):
                        sp.wait_ge(s.y_taken, n + 1)
                        sp.dma_start(k.expert_y[ds(n * P, P), :], y[:, (u - LAST) % U, :]).then_inc(y_out[(u - LAST) % U], 16)
                run_tiles(sp, ST, step, LAST)
                for u in range(U):
                    sp.wait_ge(y_out[u], ST // U * 16)

            @block.tensor
            def _(pe):
                tensor_run(pe)

            @block.scalar
            def _(act):
                scalar_run(act)

            @block.vector
            def _(dve):
                vector_run(dve)

        wctx.close()
        cctx = ExitStack()
        with cctx:
            choice = [cctx.enter_context(nc.sbuf_tensor(f"choice{i}", [P, U, H], F32)) for i in range(2)]
            total = cctx.enter_context(nc.sbuf_tensor("total", [P, U, H], F32))
            idx_copied = cctx.enter_context(nc.semaphore("idx_copied"))
            gathered = [cctx.enter_context(nc.semaphore(f"gathered{i}")) for i in range(U)]
            half_added = cctx.enter_context(nc.semaphore("half_added"))
            both_added = cctx.enter_context(nc.semaphore("both_added"))
            stored = [cctx.enter_context(nc.semaphore(f"stored{i}")) for i in range(U)]
            out_tiles = out.rearrange("b (t p) h -> (b t) p h", p=P)

            apart = Apart("gather")
            block = cctx.enter_context(nc.Block())

            @block.gpsimd
            def _(pool):
                def step(q, u, valid):
                    n = q * U + u
                    if since(n, U):
                        pool.wait_ge(gathered[u], q * 32)
                    nc.gpsimd.tensor_copy(idx[:, u, :], slot[:, :, ds(n, 1)].rearrange("p c n -> p (c n)")).then_inc(idx_copied, 1)
                    pool.wait_ge(idx_copied, n + 1)
                    if since(n, U):
                        pool.wait_ge(both_added, n - (U - 1))
                    apart(pool)
                    for i in range(2):
                        nc.gpsimd.indirect_dma_start(
                            out=choice[i][:, u, :], out_offset=None, in_=k.expert_y[:, :],
                            in_offset=bass.IndirectOffsetOnAxis(ap=idx[:, u, i:i + 1], axis=0)).then_inc(gathered[u], 16)
                run_tiles(pool, NT, step, 0)
                apart.end(pool, idx_copied)

            @block.vector
            def _(dve):
                def step(q, u, valid):
                    n = q * U + u
                    dve.wait_ge(gathered[u], (q + 1) * 32)
                    if since(n, U):
                        dve.wait_ge(stored[u], q * 16)
                    nc.vector.scalar_tensor_tensor(out=total[:, u, :], in0=choice[0][:, u, :], scalar=share[:, 0, ds(n, 1)],
                                                   in1=resid[:, ds(n, 1), :].rearrange("p t h -> p (t h)"),
                                                   op0=ALU.mult, op1=ALU.add).then_inc(half_added, 1)
                    dve.wait_ge(half_added, n + 1)
                    nc.vector.scalar_tensor_tensor(out=total[:, u, :], in0=choice[1][:, u, :], scalar=share[:, 1, ds(n, 1)],
                                                   in1=total[:, u, :], op0=ALU.mult, op1=ALU.add).then_inc(both_added, 1)
                run_tiles(dve, NT, step, 0)

            @block.sync
            def _(sp):
                def step(q, u, valid):
                    n = q * U + u
                    sp.wait_ge(both_added, n + 1)
                    sp.dma_start(out_tiles[ds(n, 1)].rearrange("t p h -> p (t h)"), total[:, u, :]).then_inc(stored[u], 16)
                run_tiles(sp, NT, step, 0)
                for u in range(U):
                    sp.wait_ge(stored[u], NT // U * 16)


class Kept:
    pass


def gnn_moe_kernel(nc, x, adj, w_src, w_dst, attn_b, gate_w, gate_b, sw1, sb1, sw2, sb2, sact,
                   ew1, eb1, ew2, eb2, eact, out):
    B, N, H = x.shape
    E, _, I2 = ew1.shape
    NT = B * N // P
    K = 2
    ST = NT * K + E
    k = Kept()
    k.token_x = nc.dram_tensor("token_x", (NT, P, 2 * H), F16, kind="Internal").ap()
    k.expert_x = nc.dram_tensor("expert_x", (ST * P, 2 * H), F16, kind="Internal").ap()
    k.expert_y = nc.dram_tensor("expert_y", (ST * P, H), F32, kind="Internal").ap()
    k.bias_rows = nc.dram_tensor("bias_rows", (2, E + 1, I2 + H), F16, kind="Internal").ap()
    with ExitStack() as ctx:
        k.resid = ctx.enter_context(nc.sbuf_tensor("resid", [P, NT, H], F32))
        k.ident = ctx.enter_context(nc.sbuf_tensor("ident", [P, P], F32))
        k.ident16 = ctx.enter_context(nc.sbuf_tensor("ident16", [P, P], F16))
        k.ones = ctx.enter_context(nc.sbuf_tensor("ones", [P, P], F32))
        k.logits = ctx.enter_context(nc.sbuf_tensor("logits", [P, NT, E], F32))
        attention_phase(nc, k, x, adj, w_src, w_dst, attn_b, gate_w, gate_b)
        expert_phases(nc, k, sw1, sb1, sw2, sb2, sact, ew1, eb1, ew2, eb2, eact, out)



_INS = ["x", "adj", "L0_gnn_attn_w_src", "L0_gnn_attn_w_dst", "L0_gnn_attn_b", "L0_ffn_gate_w", "L0_ffn_gate_b",
        "L0_ffn_shared_w1", "L0_ffn_shared_b1", "L0_ffn_shared_w2", "L0_ffn_shared_b2", "L0_ffn_shared_act",
        "L0_ffn_expert_w1", "L0_ffn_expert_b1", "L0_ffn_expert_w2", "L0_ffn_expert_b2", "L0_ffn_expert_act"]


def kernel(**inputs):
    import numpy as np
    import concourse.bacc as bacc
    from concourse import mybir as mb
    from concourse.bass_utils import run_bass_kernel_spmd

    nc = bacc.Bacc("TRN2", target_bir_lowering=False, num_devices=1)
    arrays, args = {}, []
    for name in _INS:
        a = np.ascontiguousarray(inputs[name])
        arrays[f"in_{name}"] = a
        args.append(nc.dram_tensor(f"in_{name}", a.shape, mb.dt.from_np(a.dtype), kind="ExternalInput").ap())
    out = nc.dram_tensor("out_x", inputs["x"].shape, mb.dt.float32, kind="ExternalOutput").ap()
    gnn_moe_kernel(nc, *args, out)
    r = run_bass_kernel_spmd(nc, [arrays], core_ids=[0])
    return r.results[0]["out_x"]
```

```python
from contextlib import ExitStack

import concourse.bass as bass
from concourse import mybir

ALU = mybir.AluOpType
ACT = mybir.ActivationFunctionType
F32 = mybir.dt.float32
F16 = mybir.dt.float16
I32 = mybir.dt.int32

P = 128
SLOPE = 0.2
EPS = 1e-5
MASKED = -1.0e30
WS = 256.0
TS = 16.0


BF16 = mybir.dt.bfloat16
AX_X = mybir.AxisListType.X
ds = bass.ds


class Apart:

    def __init__(self, phase):
        self.held, self.phase = {}, phase

    def __call__(self, eng):
        if eng not in self.held:
            self.held[eng] = eng.alloc_register(f"{self.phase}_held")
            eng.reg_mov(self.held[eng], 1)
        eng.reg_alu(self.held[eng], self.held[eng], 1, ALU.max)

    def end(self, eng, passed):
        if eng in self.held:
            eng.wait_ge(passed, self.held[eng])


def attention_phase(nc, k, x, adj, w_src, w_dst, attn_b, gate_w, gate_b):
    B, N, H = x.shape
    E = gate_w.shape[1]
    TPB = N // P
    NT = B * TPB
    HT = TPB // 2
    KT = H // P
    resid, ident, ident16, ones = k.resid, k.ident, k.ident16, k.ones

    ctx = ExitStack()
    with ctx:
        def sb(name, shape, dt=F32):
            return ctx.enter_context(nc.sbuf_tensor(name, shape, dt))

        def ps(name, shape, dt=F32):
            return ctx.enter_context(nc.psum_tensor(name, shape, dt))

        def sem(name):
            return ctx.enter_context(nc.semaphore(name))

        nodes = sb("nodes", [P, 4, TPB, H])
        dst5 = sb("dst5", [P, 2, N])
        pen = sb("pen", [P, TPB, N])
        score = sb("score", [P, 4, N])
        probT = sb("probT", [P, 2, TPB, P])
        ln2 = sb("ln2", [P, 2, H])
        gate_raw = sb("gate_raw", [P, KT, E])
        gate_parts = sb("gate_parts", [P, 2, KT, E], F16)
        gate_row = sb("gate_row", [P, E])
        parts = sb("parts", [P, 4, 2 * H], F16)
        xT = sb("xT", [P, 2, 2 * KT, P], F16)
        blank = sb("blank", [P, k.row], F16)
        w_rows = sb("w_rows", [P, 2, H])
        b_col = sb("b_col", [P, 1])
        b8_col = sb("b8_col", [P, 1])
        dots_junk = sb("dots_junk", [P, 4, H], mybir.dt.bfloat16)
        diag = sb("diag", [P, 4, P])
        stats1 = sb("stats1", [P, TPB, 6])
        mv1 = sb("mv1", [P, TPB, 2])
        ve1 = sb("ve1", [P, TPB])
        rstd1 = sb("rstd1", [P, TPB])
        ndots = sb("ndots", [P, 2, TPB])
        src8 = sb("src8", [P, 2, TPB])
        rowmax = sb("rowmax", [P, TPB])
        negmax = sb("negmax", [P, TPB])
        rowsum = sb("rowsum", [P, TPB])
        rinv = sb("rinv", [P, TPB])
        stats2 = sb("stats2", [P, TPB, 6])
        mv2 = sb("mv2", [P, TPB, 2])
        ve2 = sb("ve2", [P, TPB])
        rstd2 = sb("rstd2", [P, TPB])
        mhalf = sb("mhalf", [P, TPB])

        ps_half = [ps(f"ps_half{i}", [P, HT, P]) for i in range(2)]
        ps_att = [ps(f"ps_att{i}", [P, 512]) for i in range(2)]
        ps_dst = [ps(f"ps_dst{i}", [P, 512]) for i in range(2)]
        ps_xT = ps("ps_xT", [P, 2 * KT, P], F16)
        ps_gate = ps("ps_gate", [P, TPB, E])

        const_in = sem("const_in")
        x_in = sem("x_in")
        adj_in = [sem(f"adj_in{i}") for i in range(TPB)]
        ident_zeroed = sem("ident_zeroed")
        consts_ready = sem("consts_ready")
        b8_ready = sem("b8_ready")
        stats1_ready = sem("stats1_ready")
        mv1_ready = sem("mv1_ready")
        ve1_ready = sem("ve1_ready")
        rstd1_ready = sem("rstd1_ready")
        nodes_ready = sem("nodes_ready")
        dots_ready = sem("dots_ready")
        src8_ready = sem("src8_ready")
        diag_ready = sem("diag_ready")
        dst_ready = sem("dst_ready")
        dst5_ready = sem("dst5_ready")
        loop_ready = sem("loop_ready")
        mask_ready = sem("mask_ready")
        pen_ready = sem("pen_ready")
        relu_ready = sem("relu_ready")
        score_ready = sem("score_ready")
        negmax_ready = sem("negmax_ready")
        prob_ready = sem("prob_ready")
        half_ready = [sem(f"half_ready{i}") for i in range(2)]
        probT_ready = [sem(f"probT_ready{i}") for i in range(2)]
        att_ready = sem("att_ready")
        rinv_ready = sem("rinv_ready")
        resid_ready = sem("resid_ready")
        stats2_ready = sem("stats2_ready")
        mv2_ready = sem("mv2_ready")
        ve2_ready = sem("ve2_ready")
        rstd2_ready = sem("rstd2_ready")
        ln2_ready = sem("ln2_ready")
        hi_ready = sem("hi_ready")
        lo_ready = sem("lo_ready")
        parts_out = [sem(f"parts_out{i}") for i in range(4)]
        blank_ready = sem("blank_ready")
        blanks_stored = sem("blanks_stored")
        gate_parts_ready = sem("gate_parts_ready")
        xT_raw = sem("xT_raw")
        xT_ready = sem("xT_ready")
        gate_ready = sem("gate_ready")
        logits_ready = sem("logits_ready")

        LAST_LAG = 16
        PEELED = 2

        apart = Apart("attention")

        def phase1(eng, step, last=1):
            for b in range(PEELED):
                for t in range(TPB):
                    step(b, t, lambda g: g >= 0, last)
            with eng.Fori(PEELED, B - last) as b:
                for t in range(TPB):
                    step(b, t, lambda g: True, last)
            apart.end(eng, consts_ready)
            for b in range(B - last, B):
                for t in range(TPB + (LAST_LAG if b == B - 1 else 0)):
                    step(b, t, lambda g: g < NT, B - 1 - b)

        def tile_of(b, t, lag):
            return b * TPB + (t - lag), (t - lag) % TPB

        def batch_of(b, t, lag):
            return b + (t - lag) // TPB


        block = ctx.enter_context(nc.Block())

        @block.sync
        def _(sp):
            sp.dma_start(resid[:, 0:TPB, :], x[0].rearrange("(t p) h -> p t h", p=P)).then_inc(x_in, 16)
            for i, w in enumerate((w_src, w_dst)):
                sp.dma_start(w_rows[:, i, :], w.rearrange("(a h) -> a h", a=1).broadcast_to([P, H])).then_inc(const_in, 16)
            sp.dma_start(gate_raw[:, :, :], gate_w.rearrange("(k p) e -> p k e", p=P)).then_inc(const_in, 16)
            sp.dma_start(gate_row[:, :], gate_b.rearrange("(a e) -> a e", a=1).broadcast_to([P, E])).then_inc(const_in, 16)
            sp.dma_start(b_col[:, :], attn_b.rearrange("(a h) -> a h", a=1).broadcast_to([P, 1])).then_inc(const_in, 16)

            def step(b, t, valid, more):
                if t < TPB:
                    load(b, t, more)
                g, j = tile_of(b, t, 15)
                if valid(g):
                    sp.wait_ge(lo_ready, g + 1)
                    sp.dma_start(k.token_x[ds(g, 1)].rearrange("t p c -> p (t c)"), parts[:, j % 4, :]
                                 ).then_inc(parts_out[j % 4], 16)

            def load(b, t, more):
                if t == 4:
                    sp.wait_ge(blank_ready, 4)
                    rows = k.expert_x.rearrange("(b t p) c -> b p t c", b=B, p=P)
                    sp.dma_start(rows[ds(b, 1)].rearrange("b p t c -> p (b t) c"),
                                 blank[:, :].rearrange("p (a c) -> p a c", a=1).broadcast_to([P, rows.shape[2], k.row])
                                 ).then_inc(blanks_stored, 16)
                if t == 0 and isinstance(b, int) and b == 0:
                    sp.wait_ge(x_in, 16)
                    sp.dma_start(resid[:, TPB:2 * TPB, :], x[1].rearrange("(t p) h -> p t h", p=P)).then_inc(x_in, 16)
                if t == 1 and more >= 2:
                    sp.wait_ge(x_in, (b + 2) * 16)
                    sp.dma_start(resid[:, ds((b + 2) * TPB, TPB), :],
                                 x[ds(b + 2, 1)].rearrange("b (t p) h -> p (b t) h", p=P)).then_inc(x_in, 16)
                if not (isinstance(b, int) and b == 0):
                    sp.wait_ge(score_ready, (b - 1) * TPB + (t + 1))
                sp.dma_start(pen[:, t, :].bitcast(I32),
                             adj[ds(b, 1), t * P:(t + 1) * P, :].rearrange("b p n -> p (b n)")
                             ).then_inc(adj_in[t], 16)
            phase1(sp, step, last=2)
            sp.wait_ge(blanks_stored, 16 * B)
            for i in range(4):
                sp.wait_ge(parts_out[i], 16 * NT // 4)

        @block.gpsimd
        def _(pool):
            nc.gpsimd.memset(ident[:, :], 0.0).then_inc(ident_zeroed, 1)
            nc.gpsimd.memset(ones[:, :], 1.0).then_inc(consts_ready, 1)
            nc.gpsimd.memset(mhalf[:, :], -0.5).then_inc(consts_ready, 1)
            nc.gpsimd.memset(blank[:, 0:2 * H], 0.0).then_inc(blank_ready, 1)
            nc.gpsimd.memset(blank[:, 2 * H:2 * H + 1], float(NT)).then_inc(blank_ready, 1)
            nc.gpsimd.iota(blank[:, 2 * H + 1:2 * H + 2], [[0, 1]], base=0, channel_multiplier=2,
                           allow_small_or_imprecise_dtypes=True).then_inc(blank_ready, 1)
            nc.gpsimd.memset(blank[:, 2 * H + 2:2 * H + 4], -1.0).then_inc(blank_ready, 1)
            pool.wait_ge(blank_ready, 4)
            pool.wait_ge(ident_zeroed, 1)
            nc.gpsimd.affine_select(out=ident[:, :], in_=ident[:, :], compare_op=ALU.not_equal, fill=1.0,
                                    base=0, pattern=[[-1, P]], channel_multiplier=1).then_inc(consts_ready, 1)
            pool.wait_ge(consts_ready, 3)
            nc.gpsimd.tensor_copy(ident16[:, :], ident[:, :]).then_inc(consts_ready, 1)
            pool.wait_ge(consts_ready, 4)

            def first_norm_scale(b):
                pool.wait_ge(mv1_ready, (b + 1) * TPB)
                apart(pool)
                nc.gpsimd.tensor_scalar(ve1[:, :], mv1[:, :, 1], EPS, None, ALU.add).then_inc(ve1_ready, 1)
                pool.wait_ge(ve1_ready, b + 1)
                nc.gpsimd.tensor_tensor(rstd1[:, :], ve1[:, :], mhalf[:, :], ALU.pow).then_inc(rstd1_ready, 1)

            def diagonals(b, tiles):
                for j in tiles:
                    pool.wait_ge(dots_ready, b * 2 * TPB + 2 * (j + 1))
                    if j >= 4 or not (isinstance(b, int) and b == 0):
                        pool.wait_ge(dst_ready, b * TPB + (j - 3))
                    apart(pool)
                    nc.gpsimd.tensor_scalar(diag[:, j % 4, :], ident[:, :], ndots[:, 1, j:j + 1], None,
                                            ALU.mult).then_inc(diag_ready, 1)

            def step(b, t, valid, more):
                if more and t == 7:
                    diagonals(b + 1, range(5, 8))
                if t < TPB:
                    g = b * TPB + t
                    if t == 0:
                        pool.wait_ge(dst5_ready, 2 * (b + 1))
                    pool.wait_ge(mask_ready, g + 1)
                    apart(pool)
                    nc.gpsimd.tensor_tensor(pen[:, t, :], pen[:, t, :], dst5[:, ds(b % 2, 1), :],
                                            ALU.add).then_inc(pen_ready, 1)
                if more and t == 2:
                    first_norm_scale(b + 1)
                if more and t == 5:
                    diagonals(b + 1, range(0, 2))
                if more and t == 6:
                    diagonals(b + 1, range(2, 5))
                g, j = tile_of(b, t, 9)
                if valid(g):
                    pool.wait_ge(mv2_ready, g + 1)
                    apart(pool)
                    nc.gpsimd.tensor_scalar(ve2[:, j:j + 1], mv2[:, j, 1:2], EPS, None, ALU.add).then_inc(ve2_ready, 1)
                    pool.wait_ge(ve2_ready, g + 1)
                    nc.gpsimd.tensor_tensor(rstd2[:, j:j + 1], ve2[:, j:j + 1], mhalf[:, 0:1],
                                            ALU.pow).then_inc(rstd2_ready, 1)

            first_norm_scale(0)
            diagonals(0, range(TPB))
            phase1(pool, step)

        @block.vector
        def _(dve):
            def stats(b, tiles):
                if tiles[0] == 0:
                    dve.wait_ge(x_in, (b + 1) * 16)
                for j in tiles:
                    apart(dve)
                    nc.vector.bn_stats(stats1[:, j, :], resid[:, ds(b * TPB + j, 1), :]).then_inc(stats1_ready, 1)

            def aggregate(b):
                for j in range(TPB):
                    dve.wait_ge(stats1_ready, b * TPB + (j + 1))
                    apart(dve)
                    nc.vector.bn_aggr(mv1[:, j, :], stats1[:, j, :]).then_inc(mv1_ready, 1)

            def normalize(b, tiles):
                if tiles[0] == 0:
                    dve.wait_ge(rstd1_ready, b + 1)
                    if not (isinstance(b, int) and b < 4):
                        dve.wait_ge(att_ready, (b - 3) * TPB + 1)
                for j in tiles:
                    nc.vector.tensor_scalar(nodes[:, ds(b % 4, 1), j, :], resid[:, ds(b * TPB + j, 1), :],
                                            mv1[:, j, 0:1], rstd1[:, j:j + 1], ALU.subtract,
                                            ALU.mult).then_inc(nodes_ready, 1)

            def dots(b, tiles):
                for j in tiles:
                    dve.wait_ge(nodes_ready, b * TPB + (j + 1))
                    for i in range(2):
                        if 2 * j + i >= 4 or not (isinstance(b, int) and b == 0):
                            dve.wait_ge(dots_ready, b * 2 * TPB + (2 * j + i - 3))
                        nc.vector.scalar_tensor_tensor(
                            out=dots_junk[:, (2 * j + i) % 4, :], in0=nodes[:, ds(b % 4, 1), j, :].rearrange("p b h -> p (b h)"), scalar=1.0,
                            in1=w_rows[:, i, :], op0=ALU.mult, op1=ALU.mult, accum_out=ndots[:, i, j:j + 1]).then_inc(dots_ready, 1)

            def src_bias(b):
                dve.wait_ge(dots_ready, (b + 1) * 2 * TPB)
                nc.vector.tensor_scalar(src8[:, ds(b % 2, 1), :], ndots[:, 0, :], 1 - SLOPE, b8_col[:, 0:1],
                                        ALU.mult, ALU.add).then_inc(src8_ready, 1)

            def self_loop(b, j, g):
                own = pen[:, j, j * P:(j + 1) * P].bitcast(I32)
                dve.wait_ge(adj_in[j], (b + 1) * 16)
                nc.vector.tensor_tensor(own, own, ident[:, :], ALU.add).then_inc(loop_ready, 1)

            def mask(j, g):
                dve.wait_ge(loop_ready, g + 1)
                nc.vector.tensor_scalar(pen[:, j, :], pen[:, j, :].bitcast(I32), 0.0, MASKED,
                                        ALU.is_equal, ALU.mult).then_inc(mask_ready, 1)

            def step(b, t, valid, more):
                g, j = tile_of(b, t, 16)
                if j == TPB - 1 and valid(g):
                    bb = batch_of(b, t, 16)
                    dve.wait_ge(gate_ready, g + 1)
                    nc.vector.scalar_tensor_tensor(
                        out=k.logits[:, ds(bb * TPB, TPB), :], in0=ps_gate[:, :, :],
                        scalar=1.0 / WS,
                        in1=gate_row[:, :].rearrange("p (a e) -> p a e", a=1).broadcast_to([P, TPB, E]),
                        op0=ALU.mult, op1=ALU.add).then_inc(logits_ready, 1)
                g, j = tile_of(b, t, 1)
                if valid(g):
                    dve.wait_ge(relu_ready, g + 1)
                    dve.wait_ge(pen_ready, g + 1)
                    apart(dve)
                    nc.vector.tensor_tensor_reduce(out=score[:, j % 4, :], in0=score[:, j % 4, :], in1=pen[:, j, :],
                                                   scale=1.0, scalar=-3.0e38, op0=ALU.add, op1=ALU.max,
                                                   accum_out=rowmax[:, j:j + 1]).then_inc(score_ready, 1)
                g, j = tile_of(b, t, -1)
                if valid(g) and t < TPB:
                    self_loop(batch_of(b, t, -1), j, g)
                g, j = tile_of(b, t, 1)
                if valid(g):
                    dve.wait_ge(score_ready, g + 1)
                    nc.vector.tensor_scalar(negmax[:, j:j + 1], rowmax[:, j:j + 1], -1.0, None,
                                            ALU.mult).then_inc(negmax_ready, 1)
                g, j = tile_of(b, t, -1)
                if valid(g) and t < TPB:
                    mask(j, g)
                g, j = tile_of(b, t, 3)
                if valid(g):
                    dve.wait_ge(prob_ready, g + 1)
                    nc.vector.reciprocal(rinv[:, j:j + 1], rowsum[:, j:j + 1]).then_inc(rinv_ready, 1)
                g, j = tile_of(b, t, 6)
                if valid(g):
                    dve.wait_ge(att_ready, g + 1)
                    dve.wait_ge(rinv_ready, g + 1)
                    nc.vector.scalar_tensor_tensor(out=resid[:, ds(g, 1), :].rearrange("p a h -> p (a h)"), in0=ps_att[j % 2][:, 0:H],
                                                   scalar=rinv[:, j:j + 1], in1=resid[:, ds(g, 1), :].rearrange("p a h -> p (a h)"),
                                                   op0=ALU.mult, op1=ALU.add).then_inc(resid_ready, 1)
                g, j = tile_of(b, t, 7)
                if valid(g):
                    dve.wait_ge(resid_ready, g + 1)
                    apart(dve)
                    nc.vector.bn_stats(stats2[:, j, :], resid[:, ds(g, 1), :]).then_inc(stats2_ready, 1)
                g, j = tile_of(b, t, 12)
                if valid(g):
                    dve.wait_ge(hi_ready, g + 1)
                    nc.vector.tensor_tensor(parts[:, j % 4, H:2 * H], ln2[:, j % 2, :], parts[:, j % 4, 0:H],
                                            ALU.subtract).then_inc(lo_ready, 1)
                g, j = tile_of(b, t, 8)
                if valid(g):
                    dve.wait_ge(stats2_ready, g + 1)
                    apart(dve)
                    nc.vector.bn_aggr(mv2[:, j, :], stats2[:, j, :]).then_inc(mv2_ready, 1)
                g, j = tile_of(b, t, 10)
                if valid(g):
                    dve.wait_ge(rstd2_ready, g + 1)
                    if valid(g - 2) if isinstance(g, int) else True:
                        dve.wait_ge(lo_ready, g - 1)
                    nc.vector.tensor_scalar(ln2[:, j % 2, :], resid[:, ds(g, 1), :], mv2[:, j, 0:1], rstd2[:, j:j + 1],
                                            ALU.subtract, ALU.mult).then_inc(ln2_ready, 1)
                if more:
                    if t == 0:
                        stats(b + 1, range(0, 4))
                    if t == 1:
                        stats(b + 1, range(4, 8))
                    if t == 2:
                        aggregate(b + 1)
                    if t == 3:
                        normalize(b + 1, range(0, 5))
                    if t == 4:
                        normalize(b + 1, range(5, 8))
                        dots(b + 1, range(0, 2))
                    if t == 5:
                        dots(b + 1, range(2, 5))
                    if t == 6:
                        dots(b + 1, range(5, 8))
                        src_bias(b + 1)

            dve.wait_ge(const_in, 80)
            dve.wait_ge(gate_parts_ready, 1)
            nc.vector.scalar_tensor_tensor(out=gate_parts[:, 1, :, :], in0=gate_raw[:, :, :], scalar=WS,
                                           in1=gate_parts[:, 0, :, :], op0=ALU.mult,
                                           op1=ALU.subtract).then_inc(gate_parts_ready, 1)
            nc.vector.tensor_scalar(b8_col[:, :], b_col[:, :], 1 - SLOPE, None, ALU.mult).then_inc(b8_ready, 1)
            dve.wait_ge(b8_ready, 1)
            stats(0, range(TPB))
            aggregate(0)
            normalize(0, range(TPB))
            dots(0, range(TPB))
            src_bias(0)
            self_loop(0, 0, 0)
            mask(0, 0)
            phase1(dve, step)

        @block.scalar
        def _(act):
            def dst_rows(b, h):
                act.wait_ge(dst_ready, b * TPB + (h + 1) * HT)
                if h == 0 and not (isinstance(b, int) and b < 2):
                    act.wait_ge(pen_ready, (b - 1) * TPB)
                nc.scalar.activation(dst5[:, ds(b % 2, 1), h * 512:(h + 1) * 512], ps_dst[h][:, :], ACT.Copy,
                                     scale=SLOPE).then_inc(dst5_ready, 1)

            def step(b, t, valid, more):
                g, j = tile_of(b, t, 4)
                if valid(g):
                    act.wait_ge(half_ready[0], g + 1)
                    if valid(g - 2) if isinstance(g, int) else True:
                        act.wait_ge(att_ready, g - 1)
                    nc.scalar.activation(probT[:, j % 2, 0:HT, :], ps_half[0][:, :, :], ACT.Copy).then_inc(probT_ready[0], 1)
                    act.wait_ge(half_ready[1], g + 1)
                    nc.scalar.activation(probT[:, j % 2, HT:TPB, :], ps_half[1][:, :, :], ACT.Copy).then_inc(probT_ready[1], 1)
                g, j = tile_of(b, t, 2)
                if valid(g):
                    act.wait_ge(negmax_ready, g + 1)
                    nc.scalar.activation(score[:, j % 4, :], score[:, j % 4, :], ACT.Exp, bias=negmax[:, j:j + 1],
                                         accum_out=rowsum[:, j:j + 1]).then_inc(prob_ready, 1)
                g, j = tile_of(b, t, 14)
                if valid(g):
                    act.wait_ge(xT_raw, g + 1)
                    if valid(g - 2) if isinstance(g, int) else True:
                        act.wait_ge(gate_ready, g - 1)
                    nc.scalar.activation(xT[:, j % 2, :, :], ps_xT[:, :, :], ACT.Copy).then_inc(xT_ready, 1)
                g, j = tile_of(b, t, 0)
                if t < TPB:
                    if t == 0:
                        act.wait_ge(src8_ready, b + 1)
                        act.wait_ge(dst5_ready, (b + 1) * 2)
                    if valid(g - 4) if isinstance(g, int) else True:
                        act.wait_ge(half_ready[1], g - 3)
                    nc.scalar.activation(score[:, j % 4, :], dst5[:, ds(b % 2, 1), :], ACT.Relu,
                                         bias=src8[:, ds(b % 2, 1), j], scale=(1 - SLOPE) / SLOPE).then_inc(relu_ready, 1)
                g, j = tile_of(b, t, 11)
                if valid(g):
                    act.wait_ge(ln2_ready, g + 1)
                    if not (isinstance(g, int) and g < 4):
                        act.wait_ge(parts_out[j % 4], (batch_of(b, t, 11) * 2 + j // 4) * 16)
                        act.wait_ge(xT_raw, g - 3)
                    nc.scalar.activation(parts[:, j % 4, 0:H], ln2[:, j % 2, :], ACT.Copy).then_inc(hi_ready, 1)
                if more and t == TPB - 1:
                    dst_rows(b + 1, 0)
                    dst_rows(b + 1, 1)

            act.wait_ge(const_in, 80)
            nc.scalar.activation(gate_parts[:, 0, :, :], gate_raw[:, :, :], ACT.Copy, scale=WS).then_inc(gate_parts_ready, 1)
            dst_rows(0, 0)
            dst_rows(0, 1)
            phase1(act, step)

        @block.tensor
        def _(pe):
            def spread_dst(b, tiles):
                for j in tiles:
                    pe.wait_ge(diag_ready, b * TPB + (j + 1))
                    if j % HT == 0 and not (isinstance(b, int) and b == 0):
                        pe.wait_ge(dst5_ready, b * 2 + (j // HT - 1))
                    nc.tensor.matmul(ps_dst[j // HT][:, (j % HT) * P:(j % HT + 1) * P], ones[:, :],
                                     diag[:, j % 4, :], start=True, stop=True).then_inc(dst_ready, 1)

            def step(b, t, valid, more):
                g, j = tile_of(b, t, 5)
                if valid(g):
                    pe.wait_ge(probT_ready[0], g + 1)
                    if valid(g - 2) if isinstance(g, int) else True:
                        pe.wait_ge(resid_ready, g - 1)
                    if j == 0:
                        pe.wait_ge(nodes_ready, (batch_of(b, t, 5) + 1) * TPB)
                    for k in range(TPB):
                        if k == HT:
                            pe.wait_ge(probT_ready[1], g + 1)
                        ins = nc.tensor.matmul(ps_att[j % 2][:, 0:H], probT[:, j % 2, k, :],
                                               nodes[:, ds(batch_of(b, t, 5) % 4, 1), k, :].rearrange("p b h -> p (b h)"),
                                               start=(k == 0), stop=(k == TPB - 1))
                    ins.then_inc(att_ready, 1)
                g, j = tile_of(b, t, 3)
                if valid(g):
                    pe.wait_ge(prob_ready, g + 1)
                    for h in range(2):
                        if valid(g - 1) if isinstance(g, int) else True:
                            pe.wait_ge(probT_ready[h], g)
                        for k in range(HT):
                            c = h * HT + k
                            ins = nc.tensor.transpose(ps_half[h][:, k, :], score[:, j % 4, c * P:(c + 1) * P], ident[:, :])
                        ins.then_inc(half_ready[h], 1)
                g, j = tile_of(b, t, 13)
                if valid(g):
                    pe.wait_ge(lo_ready, g + 1)
                    if valid(g - 1) if isinstance(g, int) else True:
                        pe.wait_ge(xT_ready, g)
                    for c in range(2 * KT):
                        ins = nc.tensor.transpose(ps_xT[:, c, :], parts[:, j % 4, c * P:(c + 1) * P], ident16[:, :])
                    ins.then_inc(xT_raw, 1)
                g, j = tile_of(b, t, 15)
                if valid(g):
                    bb = batch_of(b, t, 15)
                    pe.wait_ge(xT_ready, g + 1)
                    if j == 0 and not (isinstance(bb, int) and bb == 0):
                        pe.wait_ge(logits_ready, bb)
                    terms = [(c, xp, wp) for xp, wp in ((0, 0), (0, 1), (1, 0)) for c in range(KT)]
                    for n, (c, xp, wp) in enumerate(terms):
                        ins = nc.tensor.matmul(ps_gate[:, j, :],
                                               xT[:, j % 2, xp * KT + c, :], gate_parts[:, wp, c, :],
                                               start=(n == 0), stop=(n == len(terms) - 1))
                    ins.then_inc(gate_ready, 1)
                if more and t == 5:
                    spread_dst(b + 1, range(0, 2))
                if more and t == 6:
                    spread_dst(b + 1, range(2, 5))
                if more and t == 7:
                    spread_dst(b + 1, range(5, 8))

            pe.wait_ge(consts_ready, 4)
            pe.wait_ge(gate_parts_ready, 2)
            spread_dst(0, range(TPB))
            phase1(pe, step)


def expert_phases(nc, k, sw1, sb1, sw2, sb2, sact, ew1, eb1, ew2, eb2, eact, out):
    E, H, I2 = ew1.shape
    I = I2 // 2
    KT = H // P
    IT = 2
    IP = I // IT
    B, N, _ = out.shape
    TPB = N // P
    NT = B * TPB
    ST = k.expert_x.shape[0] // P
    U = 4
    resid, ident, ident16, ones, logits = k.resid, k.ident, k.ident16, k.ones, k.logits
    YS = WS * TS
    UP_LAG, DOWN_LAG = 2, 8
    LAST = 9
    PEELED = -(-(LAST + 1) // U)

    ctx = ExitStack()
    with ctx:
        def sb(name, shape, dt=F32):
            return ctx.enter_context(nc.sbuf_tensor(name, shape, dt))

        def sem(name):
            return ctx.enter_context(nc.semaphore(name))

        slot = sb("slot", [P, 2, NT], I32)
        share = sb("share", [P, 2, NT])
        GROUPS = ST // U + PEELED
        words = sb("words", [P, 2, GROUPS], I32)
        par = sb("par", [P, 8, ST + 1])
        note = sb("note", [P, NT, 4], F16)

        routed = sem("routed")

        rctx = ExitStack()
        with rctx:
            def rsb(name, shape, dt=F32):
                return rctx.enter_context(nc.sbuf_tensor(name, shape, dt))

            def rsem(name):
                return rctx.enter_context(nc.semaphore(name))

            NB = ST // 2 - E // 2
            eid = rsb("eid", [P, E])
            steps_row = rsb("steps_row", [P, NB])
            tiles_row = rsb("tiles_row", [P, ST])
            upper = rsb("upper", [P, P])
            hit = rsb("hit", [P, NT, E])
            cand = rsb("cand", [P, NT, E])
            chosen = [rsb(f"chosen{i}", [P, NT, E]) for i in range(2)]
            both = rsb("both", [P, E, NT])
            place = rsb("place", [P, E, NT])
            big = rsb("big", [P, ST, E])
            best = [rsb(f"best{i}", [P, NT]) for i in range(2)]
            pick = [rsb(f"pick{i}", [P, NT]) for i in range(2)]
            slot_f = rsb("slot_f", [P, 2, NT])
            small = rsb("small", [P, 12, E])
            tile_f = rsb("tile_f", [P, ST])
            lead = DOWN_LAG
            tile_expert = rsb("tile_expert", [P, GROUPS * U + lead])
            words_f = rsb("words_f", [P, 2, GROUPS])
            gap = rsb("gap", [P, NT])
            act_raw = rsb("act_raw", [E + 1, 5])
            soft = rsb("soft", [E + 1, 6, 2])
            scalars = rsb("scalars", [E + 1, 8])
            own_no = rsb("own_no", [E + 1, 1])
            own_tile = rsb("own_tile", [E + 1, ST + 1])
            spread = rsb("spread", [E + 1, 8, P])
            ps_par = [rctx.enter_context(nc.psum_tensor(f"ps_par{i}", [P, 2, 256], F32)) for i in range(4)]
            ps_count = rctx.enter_context(nc.psum_tensor("ps_count", [P, 2, E], F32))

            loaded = rsem("loaded")
            made = rsem("made")
            upper_ready = rsem("upper_ready")
            counted = rsem("counted")
            prefixed = rsem("prefixed")
            gap_ready = rsem("gap_ready")
            odds_ready = rsem("odds_ready")
            soft_in = rsem("soft_in")
            soft_exp = rsem("soft_exp")
            soft_ln = rsem("soft_ln")
            chain = rsem("chain")
            spread_ready = rsem("spread_ready")
            par_spread = rsem("par_spread")

            block = rctx.enter_context(nc.Block())

            @block.sync
            def _(sp):
                sp.dma_start(act_raw[0:E, :], eact).then_inc(loaded, 16)
                sp.dma_start(act_raw[E:E + 1, :], sact.rearrange("(a c) -> a c", a=1)).then_inc(loaded, 16)

            @block.gpsimd
            def _(pool):
                nc.gpsimd.iota(eid[:, :], [[1, E]], base=-E, channel_multiplier=0,
                               allow_small_or_imprecise_dtypes=True).then_inc(made, 1)
                nc.gpsimd.iota(steps_row[:, :], [[P, NB]], base=0, channel_multiplier=0,
                               allow_small_or_imprecise_dtypes=True).then_inc(made, 1)
                nc.gpsimd.iota(tiles_row[:, :], [[1, ST]], base=0, channel_multiplier=0,
                               allow_small_or_imprecise_dtypes=True).then_inc(made, 1)
                nc.gpsimd.iota(note[:, :, 0], [[1, NT]], base=0, channel_multiplier=0,
                               allow_small_or_imprecise_dtypes=True).then_inc(made, 1)
                nc.gpsimd.iota(note[:, :, 1], [[0, NT]], base=0, channel_multiplier=2,
                               allow_small_or_imprecise_dtypes=True).then_inc(made, 1)
                nc.gpsimd.iota(own_no[:, :], [[0, 1]], base=0, channel_multiplier=1,
                               allow_small_or_imprecise_dtypes=True).then_inc(made, 1)
                nc.gpsimd.affine_select(out=upper[:, :], in_=ones[:, :], compare_op=ALU.is_gt, fill=0.0,
                                        base=0, pattern=[[1, P]], channel_multiplier=-1).then_inc(upper_ready, 1)

            @block.tensor
            def _(pe):
                pe.wait_ge(upper_ready, 1)
                pe.wait_ge(counted, 1)
                nc.tensor.matmul(ps_count[:, 0, :], upper[:, :], small[:, 0, :], start=True, stop=True)
                nc.tensor.matmul(ps_count[:, 1, :], ones[:, :], small[:, 0, :], start=True, stop=True).then_inc(prefixed, 1)
                pe.wait_ge(spread_ready, 1)
                for c in range(8):
                    nc.tensor.matmul(ps_par[c // 2][:, c % 2, 0:ST + 1], spread[:, c, :], own_tile[:, :],
                                     start=True, stop=True).then_inc(par_spread, 1)

            @block.scalar
            def _(act):
                act.wait_ge(gap_ready, 1)
                nc.scalar.activation(gap[:, :], gap[:, :], ACT.Exp).then_inc(odds_ready, 1)
                act.wait_ge(soft_in, 1)
                nc.scalar.activation(soft[:, 2, :], soft[:, 1, :], ACT.Exp).then_inc(soft_exp, 1)
                act.wait_ge(soft_exp, 1)
                nc.scalar.activation(soft[:, 3, :], soft[:, 2, :], ACT.Ln, bias=ones[0:E + 1, 0:1]).then_inc(soft_ln, 1)

            @block.vector
            def _(dve):
                count = [0]

                def link(ins):
                    count[0] += 1
                    ins.then_inc(chain, 1)
                    dve.wait_ge(chain, count[0])

                def over_tiles(a):
                    return a.rearrange("p (a e) -> p a e", a=1).broadcast_to([P, NT, E])

                def over_experts(a):
                    return a.rearrange("p (t a) -> p t a", a=1).broadcast_to([P, NT, E])

                dve.wait_ge(loaded, 32)
                link(nc.vector.tensor_scalar(soft[:, 0, :], act_raw[:, 3:5], -1.0, None, ALU.mult))
                nc.vector.tensor_tensor(soft[:, 1, :], act_raw[:, 3:5], soft[:, 0, :], ALU.min).then_inc(soft_in, 1)
                link(nc.vector.tensor_scalar(soft[:, 4, :], act_raw[:, 3:5], 0.0, None, ALU.max))
                link(nc.vector.tensor_scalar(scalars[:, 4:5], act_raw[:, 2:3], WS, None, ALU.mult))
                link(nc.vector.tensor_scalar(scalars[:, 5:6], act_raw[:, 0:1], 1.0 / WS, None, ALU.mult))
                link(nc.vector.tensor_scalar(scalars[:, 6:7], act_raw[:, 1:2], TS / (WS * WS), None, ALU.mult))
                dve.wait_ge(made, 6)
                link(nc.vector.tensor_copy(scalars[:, 7:8], own_no[:, :]))
                source = logits
                for i in range(2):
                    link(nc.vector.tensor_reduce(best[i][:, :], source[:, :, :], AX_X, ALU.max))
                    link(nc.vector.tensor_tensor(hit[:, :, :], source[:, :, :], over_experts(best[i][:, :]), ALU.is_equal))
                    link(nc.vector.tensor_tensor(hit[:, :, :], hit[:, :, :], over_tiles(eid[:, :]), ALU.mult))
                    link(nc.vector.tensor_reduce(pick[i][:, :], hit[:, :, :], AX_X, ALU.min))
                    link(nc.vector.tensor_tensor(chosen[i][:, :, :], over_tiles(eid[:, :]), over_experts(pick[i][:, :]),
                                                 ALU.is_equal))
                    if i == 0:
                        link(nc.vector.scalar_tensor_tensor(out=cand[:, :, :], in0=chosen[0][:, :, :], scalar=-1.0e30,
                                                            in1=logits[:, :, :], op0=ALU.mult, op1=ALU.add))
                        source = cand
                link(nc.vector.tensor_tensor(both[:, :, :].rearrange("p e t -> p t e"), chosen[0][:, :, :],
                                             chosen[1][:, :, :], ALU.add))
                nc.vector.tensor_reduce(small[:, 0, :], both[:, :, :], AX_X, ALU.add).then_inc(counted, 1)
                nc.vector.tensor_tensor(gap[:, :], best[1][:, :], best[0][:, :], ALU.subtract).then_inc(gap_ready, 1)
                flat = both[:, :, :].rearrange("p e t -> p (e t)")
                link(nc.vector.tensor_tensor_scan(place[:, :, :].rearrange("p e t -> p (e t)"), flat, flat, 0.0,
                                                  ALU.add, ALU.max))
                dve.wait_ge(counted, 1)
                link(nc.vector.tensor_tensor_scan(small[:, 1, :], small[:, 0, :], small[:, 0, :], 0.0, ALU.add, ALU.max))
                dve.wait_ge(prefixed, 1)
                link(nc.vector.tensor_copy(small[:, 2:4, :], ps_count[:, :, :]))
                fills = big[:, 0:NB, :].rearrange("p n e -> p e n")
                link(nc.vector.tensor_tensor(fills, small[:, 3, :].rearrange("p (e a) -> p e a", a=1).broadcast_to([P, E, NB]),
                                             steps_row[:, :].rearrange("p (a n) -> p a n", a=1).broadcast_to([P, E, NB]),
                                             ALU.is_gt))
                link(nc.vector.tensor_reduce(small[:, 4, :], fills, AX_X, ALU.add))
                link(nc.vector.tensor_tensor_scan(small[:, 5, :], small[:, 4, :], small[:, 4, :], 0.0, ALU.add, ALU.max))
                link(nc.vector.tensor_tensor(small[:, 6, :], small[:, 5, :], small[:, 4, :], ALU.subtract))
                link(nc.vector.scalar_tensor_tensor(out=small[:, 7, :], in0=small[:, 6, :], scalar=float(P),
                                                    in1=small[:, 2, :], op0=ALU.mult, op1=ALU.add))
                link(nc.vector.tensor_tensor(small[:, 8, :], small[:, 0, :], small[:, 1, :], ALU.subtract))
                link(nc.vector.scalar_tensor_tensor(out=small[:, 9, :], in0=small[:, 8, :], scalar=-1.0,
                                                    in1=small[:, 7, :], op0=ALU.add, op1=ALU.add))
                link(nc.vector.tensor_tensor(place[:, :, :], place[:, :, :],
                                             small[:, 9, :].rearrange("p (e a) -> p e a", a=1).broadcast_to([P, E, NT]),
                                             ALU.add))
                for i in range(2):
                    link(nc.vector.tensor_tensor(hit[:, :, :], chosen[i][:, :, :], place[:, :, :].rearrange("p e t -> p t e"),
                                                 ALU.mult))
                    link(nc.vector.tensor_reduce(slot_f[:, i, :], hit[:, :, :], AX_X, ALU.add))
                nc.vector.tensor_copy(slot[:, :, :], slot_f[:, :, :]).then_inc(routed, 1)
                for c in (2, 3):
                    nc.vector.tensor_scalar(note[:, :, c], pick[1][:, :], float(E), None, ALU.add).then_inc(routed, 1)
                link(nc.vector.tensor_tensor(big[:, :, :], small[:, 5, :].rearrange("p (a e) -> p a e", a=1).broadcast_to([P, ST, E]),
                                             tiles_row[:, :].rearrange("p (n a) -> p n a", a=1).broadcast_to([P, ST, E]),
                                             ALU.is_le))
                link(nc.vector.tensor_reduce(tile_f[:, :], big[:, :, :], AX_X, ALU.add))
                link(nc.vector.memset(tile_expert[:, :], 0.0))
                link(nc.vector.tensor_scalar(tile_expert[:, lead:lead + ST], tile_f[:, :], float(E - 1), None, ALU.min))
                for i, first in enumerate((lead - UP_LAG, lead - DOWN_LAG)):
                    def member(j):
                        return tile_expert[:, first + j:first + j + (GROUPS - 1) * U + 1:U]

                    link(nc.vector.scalar_tensor_tensor(out=words_f[:, i, :], in0=member(3), scalar=16.0, in1=member(2),
                                                        op0=ALU.mult, op1=ALU.add))
                    link(nc.vector.scalar_tensor_tensor(out=words_f[:, i, :], in0=words_f[:, i, :], scalar=16.0,
                                                        in1=member(1), op0=ALU.mult, op1=ALU.add))
                    link(nc.vector.scalar_tensor_tensor(out=words_f[:, i, :], in0=words_f[:, i, :], scalar=16.0,
                                                        in1=member(0), op0=ALU.mult, op1=ALU.add))
                nc.vector.tensor_copy(words[:, :, :], words_f[:, :, :]).then_inc(routed, 1)
                dve.wait_ge(odds_ready, 1)
                link(nc.vector.tensor_scalar(best[0][:, :], gap[:, :], 1.0, None, ALU.add))
                link(nc.vector.reciprocal(share[:, 0, :], best[0][:, :]))
                nc.vector.tensor_tensor(share[:, 1, :], gap[:, :], share[:, 0, :], ALU.mult).then_inc(routed, 1)
                link(nc.vector.tensor_scalar(own_tile[:, 0:ST], tile_expert[0:E + 1, lead:lead + ST], own_no[:, :], None, ALU.is_equal))
                link(nc.vector.tensor_scalar(own_tile[:, ST:ST + 1], own_no[:, :], float(E), None, ALU.is_equal))
                dve.wait_ge(soft_ln, 1)
                link(nc.vector.tensor_tensor(soft[:, 5, :], soft[:, 3, :], soft[:, 4, :], ALU.add))
                link(nc.vector.tensor_scalar(scalars[:, 0:2], soft[:, 5, :], WS, None, ALU.mult))
                link(nc.vector.tensor_scalar(scalars[:, 2:4], soft[:, 5, :], -WS, None, ALU.mult))
                for c in range(8):
                    ins = nc.vector.tensor_scalar(spread[:, c, :], ones[0:E + 1, :], scalars[:, c:c + 1], None, ALU.mult)
                    if c < 7:
                        link(ins)
                ins.then_inc(spread_ready, 1)
                for c in range(8):
                    dve.wait_ge(par_spread, c + 1 if c % 2 else c + 2)
                    nc.vector.tensor_copy(par[:, c, :], ps_par[c // 2][:, c % 2, 0:ST + 1]).then_inc(routed, 1)

        idx = sb("idx", [P, 2, U, 2], I32)
        dest = sb("dest", [P, U], I32)

        wctx = ctx.enter_context(ExitStack())

        def wsb(name, shape, dt=F32):
            return wctx.enter_context(nc.sbuf_tensor(name, shape, dt))

        w1 = wsb("w1", [P, E + 1, KT, 2, I2], F16)
        w2 = wsb("w2", [IP + 2, E + 1, IT, 2, H], F16)
        b1 = wsb("b1", [2, E + 1, I2], F16)
        xrow = wsb("xrow", [P, U, k.row], F16)
        xT = wsb("rows_T", [P, U, 2 * KT, P], F16)
        gated = wsb("gated", [P, U, I])
        up = wsb("up", [P, U, I])
        sig = wsb("sig", [P, U, I])
        hid = wsb("hid", [P, U, I])
        hidT = wsb("hidT", [IP + 2, U, 2, IT, P], F16)
        two16 = wsb("two16", [2, P], F16)

        def run_tiles(eng, tiles, step, lag):
            for q in range(PEELED):
                for u in range(U):
                    step(q, u, lambda n: n >= 0)
            with eng.Fori(PEELED, tiles // U) as q:
                for u in range(U):
                    step(q, u, lambda n: True)
            for u in range(U, U + lag):
                step(tiles // U - 1, u, lambda n: n < tiles)

        def since(n, before):
            return not isinstance(n, int) or n >= before

        class Signals:

            def __init__(self, name, enter):
                self.xT_raw = enter(nc.semaphore(name + "xT_raw"))
                self.xT_ready = enter(nc.semaphore(name + "xT_ready"))
                self.up_done = enter(nc.semaphore(name + "up_done"))
                self.gated_ready = enter(nc.semaphore(name + "gated_ready"))
                self.up_ready = enter(nc.semaphore(name + "up_ready"))
                self.sig_ready = enter(nc.semaphore(name + "sig_ready"))
                self.prod_ready = enter(nc.semaphore(name + "prod_ready"))
                self.hid_ready = enter(nc.semaphore(name + "hid_ready"))
                self.hidT_raw = enter(nc.semaphore(name + "hidT_raw"))
                self.hidT_high = enter(nc.semaphore(name + "hidT_high"))
                self.hidT_ready = enter(nc.semaphore(name + "hidT_ready"))
                self.down_done = enter(nc.semaphore(name + "down_done"))
                self.y_taken = enter(nc.semaphore(name + "y_taken"))

        def feed_forward(s, psums, tiles, experts_of, par_at, x_wait, take_y, y_engine, prepare):
            ps_xT, ps_h, ps_hT, ps_y = psums
            terms = [(c, xp, wp) for xp, wp in ((0, 0), (0, 1), (1, 0)) for c in range(KT)]
            hid_terms = [(c, xp, wp) for xp, wp in ((0, 0), (0, 1), (1, 0)) for c in range(IT)]

            def at(q, u, lag):
                return q * U + (u - lag), (u - lag) % 2, (u - lag) % U

            def tensor_step(pe):
                group = [None]

                def step(q, u, valid):
                    n, b, v = at(q, u, 6)
                    if valid(n):
                        pe.wait_ge(s.hid_ready, n + 1)
                        if since(n, 2):
                            pe.wait_ge(s.hidT_ready, n - 1)
                        for c in range(IT):
                            ins = nc.tensor.transpose(ps_hT[b][:, c, :], hid[:, v, c * IP:(c + 1) * IP], ident[:, :])
                        ins.then_inc(s.hidT_raw, 1)
                    if u % U == 0:
                        group[0] = experts_of(pe, q + u // U)
                    e_up, e_down = group[0](u % U)
                    n, b, v = at(q, u, 0)
                    if u < U:
                        x_wait(pe, q, u, n)
                        if since(n, 2):
                            pe.wait_ge(s.xT_ready, n - 1)
                        for c in range(2 * KT):
                            ins = nc.tensor.transpose(ps_xT[b][:, c, :], xrow[:, u, c * P:(c + 1) * P], ident16[:, :])
                        ins.then_inc(s.xT_raw, 1)
                    n, b, v = at(q, u, UP_LAG)
                    if valid(n):
                        pe.wait_ge(s.xT_ready, n + 1)
                        if since(n, 2):
                            pe.wait_ge(s.up_ready, n - 1)
                        nc.tensor.matmul(ps_h[b][:, :], two16[:, :], b1[:, ds(e_up, 1), :].rearrange("p e i -> p (e i)"),
                                         start=True, stop=False)
                        for i, (c, xp, wp) in enumerate(terms):
                            ins = nc.tensor.matmul(ps_h[b][:, :], xT[:, v, xp * KT + c, :],
                                                   w1[:, ds(e_up, 1), c, wp, :].rearrange("p e i -> p (e i)"),
                                                   start=False, stop=(i == len(terms) - 1))
                        ins.then_inc(s.up_done, 1)
                    n, b, v = at(q, u, DOWN_LAG)
                    if valid(n):
                        pe.wait_ge(s.hidT_ready, n + 1)
                        if since(n, 2):
                            pe.wait_ge(s.y_taken, n - 1)
                        for i, (c, xp, wp) in enumerate(hid_terms):
                            rows = IP + 2 if i == 0 else IP
                            ins = nc.tensor.matmul(ps_y[b][:, :], hidT[0:rows, v, xp, c, :],
                                                   w2[0:rows, ds(e_down, 1), c, wp, :].rearrange("p e h -> p (e h)"),
                                                   start=(i == 0), stop=(i == len(hid_terms) - 1))
                        ins.then_inc(s.down_done, 1)
                run_tiles(pe, tiles, step, LAST)

            def scalar_step(act):
                def step(q, u, valid):
                    n, b, v = at(q, u, 7)
                    if valid(n):
                        act.wait_ge(s.hidT_raw, n + 1)
                        if since(n, U):
                            act.wait_ge(s.down_done, n - (U - 1))
                        nc.scalar.activation(hidT[0:IP, v, 0, :, :], ps_hT[b][:, :, :], ACT.Copy).then_inc(s.hidT_high, 1)
                    n, b, v = at(q, u, 1)
                    if valid(n):
                        act.wait_ge(s.xT_raw, n + 1)
                        if since(n, U):
                            act.wait_ge(s.up_done, n - (U - 1))
                        nc.scalar.activation(xT[:, v, :, :], ps_xT[b][:, :, :], ACT.Copy).then_inc(s.xT_ready, 1)
                    n, b, v = at(q, u, 4)
                    if valid(n):
                        e = par_at(n)
                        act.wait_ge(s.gated_ready, n + 1)
                        if since(n, U):
                            act.wait_ge(s.hid_ready, n - (U - 1))
                        nc.scalar.activation(sig[:, v, :], gated[:, v, :], ACT.Sigmoid,
                                             scale=par[:, 5, ds(e, 1)]).then_inc(s.sig_ready, 1)
                    n, b, v = at(q, u, 9)
                    if valid(n) and y_engine == "scalar":
                        act.wait_ge(s.down_done, n + 1)
                        take_y(act, s, q, u - 9, n, ps_y[b])
                    if prepare:
                        prepare(act, q, u)
                run_tiles(act, tiles, step, LAST)

            def vector_step(dve):
                def step(q, u, valid):
                    n, b, v = at(q, u, 3)
                    if valid(n):
                        e = par_at(n)
                        dve.wait_ge(s.up_done, n + 1)
                        if since(n, U):
                            dve.wait_ge(s.sig_ready, n - (U - 1))
                            dve.wait_ge(s.hid_ready, n - (U - 1))
                        nc.vector.tensor_scalar(gated[:, v, :], ps_h[b][:, 0:I], par[:, 2, ds(e, 1)], par[:, 0, ds(e, 1)],
                                                ALU.max, ALU.min).then_inc(s.gated_ready, 1)
                        nc.vector.tensor_scalar(up[:, v, :], ps_h[b][:, I:I2], par[:, 3, ds(e, 1)], par[:, 1, ds(e, 1)],
                                                ALU.max, ALU.min).then_inc(s.up_ready, 1)
                    m, b, v = at(q, u, 7)
                    if valid(m):
                        dve.wait_ge(s.hidT_high, m + 1)
                        nc.vector.tensor_tensor(hidT[0:IP, v, 1, :, :], ps_hT[b][:, :, :], hidT[0:IP, v, 0, :, :],
                                                ALU.subtract).then_inc(s.hidT_ready, 1)
                    n, b, v = at(q, u, 3)
                    if valid(n):
                        dve.wait_ge(s.gated_ready, n + 1)
                        dve.wait_ge(s.up_ready, n + 1)
                        nc.vector.scalar_tensor_tensor(out=up[:, v, :], in0=up[:, v, :], scalar=par[:, 4, ds(e, 1)],
                                                       in1=gated[:, v, :], op0=ALU.add, op1=ALU.mult
                                                       ).then_inc(s.prod_ready, 1)
                    m, b, v = at(q, u, 5)
                    if valid(m):
                        e = par_at(m)
                        dve.wait_ge(s.prod_ready, m + 1)
                        dve.wait_ge(s.sig_ready, m + 1)
                        if since(m, U):
                            dve.wait_ge(s.hidT_raw, m - (U - 1))
                        nc.vector.scalar_tensor_tensor(out=hid[:, v, :], in0=up[:, v, :], scalar=par[:, 6, ds(e, 1)],
                                                       in1=sig[:, v, :], op0=ALU.mult, op1=ALU.mult
                                                       ).then_inc(s.hid_ready, 1)
                    n, b, v = at(q, u, 9)
                    if valid(n) and y_engine == "vector":
                        dve.wait_ge(s.down_done, n + 1)
                        take_y(dve, s, q, u - 9, n, ps_y[b])
                    if prepare:
                        prepare(dve, q, u)
                run_tiles(dve, tiles, step, LAST)

            return tensor_step, scalar_step, vector_step

        def psum_banks(c, prefix):
            return [[c.enter_context(nc.psum_tensor(f"{prefix}{name}{i}", shape, dt)) for i in range(2)]
                    for name, shape, dt in (("ps_xT", [P, 2 * KT, P], F16), ("ps_h", [P, I2], F32),
                                            ("ps_hT", [IP, IT, P], F32), ("ps_y", [P, H], F32))]

        sctx = ExitStack()
        with sctx:
            def ssem(name):
                return sctx.enter_context(nc.semaphore(name))

            raw1 = sctx.enter_context(nc.sbuf_tensor("raw1", [P, KT, I2], F32))
            raw2 = sctx.enter_context(nc.sbuf_tensor("raw2", [IP, IT, H], F32))
            bias_raw = sctx.enter_context(nc.sbuf_tensor("bias_raw", [E + 1, I2 + H], F32))
            bias_parts = sctx.enter_context(nc.sbuf_tensor("bias_parts", [E + 1, 2, I2 + H], F16))
            psums = psum_banks(sctx, "s_")
            s = Signals("s_", sctx.enter_context)
            x_in = [ssem(f"rows_in{i}") for i in range(U)]
            scattered = [ssem(f"scattered{i}") for i in range(U)]
            idx_ready = ssem("idx_ready")
            noted = ssem("noted")
            two_ready = ssem("two_ready")
            raw1_in = ssem("raw1_in")
            raw2_in = ssem("raw2_in")
            w1_high = ssem("w1_high")
            w1_ready = ssem("w1_ready")
            w2_high = ssem("w2_high")
            w2_ready = ssem("w2_ready")
            bias_in = ssem("bias_in")
            bias_high = ssem("bias_high")
            bias_low = ssem("bias_low")
            bias_stored = ssem("bias_stored")
            bias_ready = ssem("bias_ready")

            def split(eng, e, nth):
                paired = raw1[:, :, :].rearrange("p k (i two) -> p k two i", two=2)
                if eng is nc.scalar:
                    eng.wait_ge(raw1_in, (nth + 1) * 16)
                    nc.scalar.activation(w1[:, ds(e, 1), :, 0, :].rearrange("p e k (two i) -> p (e k) two i", two=2), paired,
                                         ACT.Copy, scale=WS).then_inc(w1_high, 1)
                    eng.wait_ge(raw2_in, (nth + 1) * 16)
                    nc.scalar.activation(w2[0:IP, ds(e, 1), :, 0, :].rearrange("p e c h -> p (e c) h"), raw2[:, :, :],
                                         ACT.Copy, scale=WS).then_inc(w2_high, 1)
                else:
                    eng.wait_ge(w1_high, nth + 1)
                    for c in range(KT):
                        nc.vector.scalar_tensor_tensor(
                            out=w1[:, ds(e, 1), c, 1, :].rearrange("p e (two i) -> p (e two) i", two=2), in0=paired[:, c, :, :],
                            scalar=WS, in1=w1[:, ds(e, 1), c, 0, :].rearrange("p e (two i) -> p (e two) i", two=2),
                            op0=ALU.mult, op1=ALU.subtract).then_inc(w1_ready, 1)
                    eng.wait_ge(w2_high, nth + 1)
                    nc.vector.scalar_tensor_tensor(
                        out=w2[0:IP, ds(e, 1), :, 1, :].rearrange("p e c h -> p (e c) h"), in0=raw2[:, :, :], scalar=WS,
                        in1=w2[0:IP, ds(e, 1), :, 0, :].rearrange("p e c h -> p (e c) h"),
                        op0=ALU.mult, op1=ALU.subtract).then_inc(w2_ready, 1)

            def note_and_split(eng, q, u):
                if eng is nc.scalar and u < U:
                    n = q * U + u
                    if since(n, U):
                        eng.wait_ge(scattered[u], q * 32)
                    nc.scalar.activation(xrow[:, u, 2 * H:2 * H + 4],
                                         note[:, ds(n, 1), :].rearrange("p n c -> p (n c)"), ACT.Copy).then_inc(noted, 1)
                if u == U - 1:
                    split(eng, q, q + 1)

            def shared_x_wait(eng, q, u, n):
                eng.wait_ge(x_in[u], (q + 1) * 16)

            def add_shared(dve, s, q, u, n, bank):
                nc.vector.scalar_tensor_tensor(out=resid[:, ds(n, 1), :].rearrange("p t h -> p (t h)"), in0=bank[:, :],
                                               scalar=1.0 / YS, in1=resid[:, ds(n, 1), :].rearrange("p t h -> p (t h)"),
                                               op0=ALU.mult, op1=ALU.add).then_inc(s.y_taken, 1)

            tensor_run, scalar_run, vector_run = feed_forward(
                s, psums, NT, lambda pe, q: lambda u: (E, E), lambda n: ST, shared_x_wait, add_shared, "vector", note_and_split)

            apart = Apart("scatter")
            block = sctx.enter_context(nc.Block())

            @block.sync
            def _(sp):
                def load_raw(w1_d, w2_d, nth):
                    if not (isinstance(nth, int) and nth == 0):
                        sp.wait_ge(w1_ready, nth * KT)
                    sp.dma_start(raw1[:, :, :], w1_d).then_inc(raw1_in, 16)
                    if not (isinstance(nth, int) and nth == 0):
                        sp.wait_ge(w2_ready, nth)
                    sp.dma_start(raw2[:, :, :], w2_d).then_inc(raw2_in, 16)

                sp.dma_start(bias_raw[0:E, 0:I2], eb1).then_inc(bias_in, 16)
                sp.dma_start(bias_raw[E:E + 1, 0:I2], sb1.rearrange("(a i) -> a i", a=1)).then_inc(bias_in, 16)
                sp.dma_start(bias_raw[0:E, I2:I2 + H], eb2).then_inc(bias_in, 16)
                sp.dma_start(bias_raw[E:E + 1, I2:I2 + H], sb2.rearrange("(a h) -> a h", a=1)).then_inc(bias_in, 16)
                load_raw(sw1.rearrange("(k p) i -> p k i", p=P), sw2.rearrange("(c p) h -> p c h", p=IP), 0)
                sp.wait_ge(bias_low, 2)
                for i in range(2):
                    sp.dma_start(k.bias_rows[i], bias_parts[:, i, :]).then_inc(bias_stored, 16)
                sp.wait_ge(bias_stored, 32)
                sp.dma_start(b1[:, :, :], k.bias_rows[:, :, 0:I2]).then_inc(bias_ready, 16)
                sp.dma_start(w2[IP:IP + 2, :, 0, 0, :], k.bias_rows[:, :, I2:I2 + H]).then_inc(bias_ready, 16)

                done = sp.alloc_register("scatters_done")
                sp.reg_mov(done, 0)

                def step(q, u, valid):
                    n = q * U + u
                    if u == 0 and since(n, U):
                        sp.reg_alu(done, done, 32, ALU.add)
                    if since(n, U):
                        sp.wait_ge(s.xT_raw, n - (U - 1))
                        sp.wait_ge(scattered[u], done)
                    sp.dma_start(xrow[:, u, 0:2 * H], k.token_x[ds(n, 1)].rearrange("t p c -> p (t c)")).then_inc(x_in[u], 16)
                    if u == U - 1:
                        load_raw(ew1[ds(q, 1)].rearrange("e (k p) i -> p (e k) i", p=P),
                                 ew2[ds(q, 1)].rearrange("e (c p) h -> p (e c) h", p=IP), q + 1)
                run_tiles(sp, NT, step, 0)

            @block.gpsimd
            def _(pool):
                nc.gpsimd.memset(two16[:, :], 1.0).then_inc(two_ready, 1)
                nc.gpsimd.memset(hidT[IP:IP + 2, :, 0, 0, :], 1.0).then_inc(two_ready, 1)
                pool.wait_ge(two_ready, 2)

                def scatter(r, h):
                    first = isinstance(r, int) and r == 0
                    if not first:
                        for u in range(U):
                            pool.wait_ge(scattered[u], (2 * r + (h - 1)) * 32)
                    apart(pool)
                    nc.gpsimd.tensor_copy(idx[:, h, :, :].rearrange("p u c -> p c u"),
                                          slot[:, :, ds(r * 2 * U + h * U, U)]).then_inc(idx_ready, 1)
                    pool.wait_ge(idx_ready, 2 * r + (h + 1))
                    for u in range(U):
                        pool.wait_ge(x_in[u], (2 * r + (h + 1)) * 16)
                        pool.wait_ge(noted, r * 2 * U + (h * U + u + 1))
                        apart(pool)
                        for i in range(2):
                            nc.gpsimd.indirect_dma_start(
                                out=k.expert_x[:, :], out_offset=bass.IndirectOffsetOnAxis(ap=idx[:, h, u, i:i + 1], axis=0),
                                in_=xrow[:, u, :], in_offset=None).then_inc(scattered[u], 16)

                scatter(0, 0)
                scatter(0, 1)
                with pool.Fori(1, NT // (2 * U)) as r:
                    scatter(r, 0)
                    scatter(r, 1)
                apart.end(pool, idx_ready)
                for u in range(U):
                    pool.wait_ge(scattered[u], NT // U * 32)

            @block.tensor
            def _(pe):
                pe.wait_ge(two_ready, 2)
                pe.wait_ge(w1_ready, KT)
                pe.wait_ge(w2_ready, 1)
                pe.wait_ge(bias_ready, 32)
                tensor_run(pe)

            @block.scalar
            def _(act):
                act.wait_ge(bias_in, 64)
                nc.scalar.activation(bias_parts[:, 0, 0:I2].rearrange("p (two i) -> p two i", two=2),
                                     bias_raw[:, 0:I2].rearrange("p (i two) -> p two i", two=2), ACT.Copy,
                                     scale=WS).then_inc(bias_high, 1)
                nc.scalar.activation(bias_parts[:, 0, I2:I2 + H], bias_raw[:, I2:I2 + H], ACT.Copy,
                                     scale=YS).then_inc(bias_high, 1)
                split(nc.scalar, E, 0)
                scalar_run(act)

            @block.vector
            def _(dve):
                dve.wait_ge(bias_high, 2)
                nc.vector.scalar_tensor_tensor(out=bias_parts[:, 1, 0:I2].rearrange("p (two i) -> p two i", two=2),
                                               in0=bias_raw[:, 0:I2].rearrange("p (i two) -> p two i", two=2), scalar=WS,
                                               in1=bias_parts[:, 0, 0:I2].rearrange("p (two i) -> p two i", two=2),
                                               op0=ALU.mult, op1=ALU.subtract).then_inc(bias_low, 1)
                nc.vector.scalar_tensor_tensor(out=bias_parts[:, 1, I2:I2 + H], in0=bias_raw[:, I2:I2 + H], scalar=YS,
                                               in1=bias_parts[:, 0, I2:I2 + H],
                                               op0=ALU.mult, op1=ALU.subtract).then_inc(bias_low, 1)
                split(nc.vector, E, 0)
                vector_run(dve)

        ectx = ExitStack()
        with ectx:
            psums = psum_banks(ectx, "e_")
            y = ectx.enter_context(nc.sbuf_tensor("y", [P, U, H], F32))
            dest_f = ectx.enter_context(nc.sbuf_tensor("dest_f", [P, ST], F32))
            noted = ectx.enter_context(nc.semaphore("e_noted"))
            within = ectx.enter_context(nc.sbuf_tensor("within", [P, 2], F32))
            within_ready = ectx.enter_context(nc.semaphore("within_ready"))
            dest_ready = ectx.enter_context(nc.semaphore("dest_ready"))
            s = Signals("e_", ectx.enter_context)
            x_in = [ectx.enter_context(nc.semaphore(f"e_rows_in{i}")) for i in range(U)]
            y_out = [ectx.enter_context(nc.semaphore(f"e_y_out{i}")) for i in range(U)]

            def routed_experts(pe, q):
                up_word, down_word = [pe.value_load(words[0:1, i, ds(q, 1)], min_val=0, max_val=16 ** U - 1)
                                      for i in range(2)]
                return lambda u: ((up_word >> 4 * u) & (E - 1), (down_word >> 4 * u) & (E - 1))

            def expert_x_wait(eng, q, u, n):
                eng.wait_ge(x_in[u], (q + 1) * 16)

            def store_y(act, s, q, u, n, bank):
                if since(n, U):
                    act.wait_ge(y_out[u % U], (q + u // U) * 16)
                nc.scalar.activation(y[:, u % U, :], bank[:, :], ACT.Copy, scale=1.0 / YS).then_inc(s.y_taken, 1)

            def place_rows(eng, q, u):
                if eng is nc.vector and u < U:
                    tail = xrow[:, u, 2 * H:2 * H + 4]
                    n = q * U + u
                    eng.wait_ge(x_in[u], (q + 1) * 16)
                    if since(n, 2):
                        eng.wait_ge(noted, n - 1)
                    nc.vector.scalar_tensor_tensor(out=within[:, u % 2:u % 2 + 1], in0=tail[:, 2:3], scalar=par[:, 7, ds(n, 1)],
                                                   in1=tail[:, 1:2], op0=ALU.is_equal, op1=ALU.add).then_inc(within_ready, 1)
                    eng.wait_ge(within_ready, n + 1)
                    nc.vector.scalar_tensor_tensor(out=dest_f[:, ds(n, 1)], in0=tail[:, 0:1], scalar=2.0 * P,
                                                   in1=within[:, u % 2:u % 2 + 1], op0=ALU.mult, op1=ALU.add).then_inc(noted, 1)

            tensor_run, scalar_run, vector_run = feed_forward(
                s, psums, ST, routed_experts, lambda n: n, expert_x_wait, store_y, "scalar", place_rows)

            apart = Apart("place")
            block = ectx.enter_context(nc.Block())

            @block.sync
            def _(sp):
                def step(q, u, valid):
                    n = q * U + u
                    if since(n, U):
                        sp.wait_ge(s.xT_raw, n - (U - 1))
                        sp.wait_ge(noted, n - (U - 1))
                    sp.dma_start(xrow[:, u, :], k.expert_x[ds(n * P, P), :]).then_inc(x_in[u], 16)
                run_tiles(sp, ST, step, 0)

            @block.gpsimd
            def _(pool):
                def step(q, u, valid):
                    n, v = q * U + (u - LAST), (u - LAST) % U
                    if valid(n):
                        if since(n, U):
                            pool.wait_ge(y_out[v], (q + (u - LAST) // U) * 16)
                        pool.wait_ge(noted, n + 1)
                        apart(pool)
                        nc.gpsimd.tensor_copy(dest[:, v:v + 1], dest_f[:, ds(n, 1)]).then_inc(dest_ready, 1)
                        pool.wait_ge(dest_ready, n + 1)
                        pool.wait_ge(s.y_taken, n + 1)
                        apart(pool)
                        nc.gpsimd.indirect_dma_start(
                            out=k.choice_y[:, :], out_offset=bass.IndirectOffsetOnAxis(ap=dest[:, v:v + 1], axis=0),
                            in_=y[:, v, :], in_offset=None, bounds_check=2 * NT * P - 1, oob_is_err=False
                            ).then_inc(y_out[v], 16)
                run_tiles(pool, ST, step, LAST)
                apart.end(pool, dest_ready)
                for u in range(U):
                    pool.wait_ge(y_out[u], ST // U * 16)

            @block.tensor
            def _(pe):
                tensor_run(pe)

            @block.scalar
            def _(act):
                scalar_run(act)

            @block.vector
            def _(dve):
                vector_run(dve)

        wctx.close()
        cctx = ExitStack()
        with cctx:
            CU, CB = 2, 4
            STEPS = NT // CU
            choice = cctx.enter_context(nc.sbuf_tensor("choice", [P, CB, CU, 2, H], F32))
            chosen_in = [cctx.enter_context(nc.semaphore(f"chosen_in{i}")) for i in range(CB)]
            half_added = cctx.enter_context(nc.semaphore("half_added"))
            both_added = cctx.enter_context(nc.semaphore("both_added"))
            stored = cctx.enter_context(nc.semaphore("stored"))
            out_tiles = out.rearrange("b (t p) h -> p (b t) h", p=P)
            choice_rows = k.choice_y.rearrange("(t p c) h -> p t c h", p=P, c=2)

            block = cctx.enter_context(nc.Block())

            def run_steps(eng, step):
                for v in range(CB):
                    step(0, v)
                with eng.Fori(1, STEPS // CB) as r:
                    for v in range(CB):
                        step(r, v)

            @block.sync
            def _(sp):
                def step(r, v):
                    m = r * CB + v
                    if not (isinstance(r, int) and r == 0):
                        sp.wait_ge(both_added, (m - (CB - 1)) * CU)
                    sp.dma_start(choice[:, v, :, :, :].rearrange("p t c h -> p t (c h)"),
                                 choice_rows[:, ds(m * CU, CU), :, :].rearrange("p t c h -> p t (c h)")
                                 ).then_inc(chosen_in[v], 16)
                run_steps(sp, step)

            @block.vector
            def _(dve):
                def step(r, v):
                    m = r * CB + v
                    dve.wait_ge(chosen_in[v], (r + 1) * 16)
                    for i in range(2):
                        for c in range(CU):
                            n = m * CU + c
                            if i == 1:
                                dve.wait_ge(half_added, n + 1)
                            tile = resid[:, ds(n, 1), :].rearrange("p t h -> p (t h)")
                            nc.vector.scalar_tensor_tensor(
                                out=tile, in0=choice[:, v, c, i, :], scalar=share[:, i, ds(n, 1)], in1=tile,
                                op0=ALU.mult, op1=ALU.add).then_inc((half_added, both_added)[i], 1)
                run_steps(dve, step)

            @block.scalar
            def _(act):
                def step(r, v):
                    m = r * CB + v
                    act.wait_ge(both_added, (m + 1) * CU)
                    act.dma_start(out_tiles[:, ds(m * CU, CU), :], resid[:, ds(m * CU, CU), :]).then_inc(stored, 16)
                run_steps(act, step)
                act.wait_ge(stored, STEPS * 16)


class Kept:
    pass


def gnn_moe_kernel(nc, x, adj, w_src, w_dst, attn_b, gate_w, gate_b, sw1, sb1, sw2, sb2, sact,
                   ew1, eb1, ew2, eb2, eact, out):
    B, N, H = x.shape
    E, _, I2 = ew1.shape
    NT = B * N // P
    K = 2
    ST = NT * K + E
    k = Kept()
    k.token_x = nc.dram_tensor("token_x", (NT, P, 2 * H), F16, kind="Internal").ap()
    k.row = 2 * H + 4
    k.expert_x = nc.dram_tensor("expert_x", (ST * P, k.row), F16, kind="Internal").ap()
    k.choice_y = nc.dram_tensor("choice_y", (NT * P * K, H), F32, kind="Internal").ap()
    k.bias_rows = nc.dram_tensor("bias_rows", (2, E + 1, I2 + H), F16, kind="Internal").ap()
    with ExitStack() as ctx:
        k.resid = ctx.enter_context(nc.sbuf_tensor("resid", [P, NT, H], F32))
        k.ident = ctx.enter_context(nc.sbuf_tensor("ident", [P, P], F32))
        k.ident16 = ctx.enter_context(nc.sbuf_tensor("ident16", [P, P], F16))
        k.ones = ctx.enter_context(nc.sbuf_tensor("ones", [P, P], F32))
        k.logits = ctx.enter_context(nc.sbuf_tensor("logits", [P, NT, E], F32))
        attention_phase(nc, k, x, adj, w_src, w_dst, attn_b, gate_w, gate_b)
        expert_phases(nc, k, sw1, sb1, sw2, sb2, sact, ew1, eb1, ew2, eb2, eact, out)



_INS = ["x", "adj", "L0_gnn_attn_w_src", "L0_gnn_attn_w_dst", "L0_gnn_attn_b", "L0_ffn_gate_w", "L0_ffn_gate_b",
        "L0_ffn_shared_w1", "L0_ffn_shared_b1", "L0_ffn_shared_w2", "L0_ffn_shared_b2", "L0_ffn_shared_act",
        "L0_ffn_expert_w1", "L0_ffn_expert_b1", "L0_ffn_expert_w2", "L0_ffn_expert_b2", "L0_ffn_expert_act"]


def kernel(**inputs):
    import numpy as np
    import concourse.bacc as bacc
    from concourse import mybir as mb
    from concourse.bass_utils import run_bass_kernel_spmd

    nc = bacc.Bacc("TRN2", target_bir_lowering=False, num_devices=1)
    arrays, args = {}, []
    for name in _INS:
        a = np.ascontiguousarray(inputs[name])
        arrays[f"in_{name}"] = a
        args.append(nc.dram_tensor(f"in_{name}", a.shape, mb.dt.from_np(a.dtype), kind="ExternalInput").ap())
    out = nc.dram_tensor("out_x", inputs["x"].shape, mb.dt.float32, kind="ExternalOutput").ap()
    gnn_moe_kernel(nc, *args, out)
    r = run_bass_kernel_spmd(nc, [arrays], core_ids=[0])
    return r.results[0]["out_x"]
```

```python
from contextlib import ExitStack

import concourse.bass as bass
from concourse import mybir

ALU = mybir.AluOpType
ACT = mybir.ActivationFunctionType
F32 = mybir.dt.float32
F16 = mybir.dt.float16
I32 = mybir.dt.int32

P = 128
SLOPE = 0.2
EPS = 1e-5
MASKED = -1.0e30
WS = 256.0
TS = 16.0


BF16 = mybir.dt.bfloat16
AX_X = mybir.AxisListType.X
ds = bass.ds


class Apart:

    def __init__(self, phase):
        self.held, self.phase = {}, phase

    def __call__(self, eng):
        if eng not in self.held:
            self.held[eng] = eng.alloc_register(f"{self.phase}_held")
            eng.reg_mov(self.held[eng], 1)
        eng.reg_alu(self.held[eng], self.held[eng], 1, ALU.max)

    def end(self, eng, passed):
        if eng in self.held:
            eng.wait_ge(passed, self.held[eng])


def attention_phase(nc, k, x, adj, w_src, w_dst, attn_b, gate_w, gate_b):
    B, N, H = x.shape
    E = gate_w.shape[1]
    TPB = N // P
    NT = B * TPB
    HT = TPB // 2
    KT = H // P
    resid, ident, ident16, ones = k.resid, k.ident, k.ident16, k.ones

    ctx = ExitStack()
    with ctx:
        def sb(name, shape, dt=F32):
            return ctx.enter_context(nc.sbuf_tensor(name, shape, dt))

        def ps(name, shape, dt=F32):
            return ctx.enter_context(nc.psum_tensor(name, shape, dt))

        def sem(name):
            return ctx.enter_context(nc.semaphore(name))

        nodes = sb("nodes", [P, 4, TPB, H])
        dst5 = sb("dst5", [P, 2, N])
        pen = sb("pen", [P, TPB, N])
        score = sb("score", [P, 4, N])
        probT = sb("probT", [P, 2, TPB, P])
        ln2 = sb("ln2", [P, 2, H])
        gate_raw = sb("gate_raw", [P, KT, E])
        gate_parts = sb("gate_parts", [P, 2, KT, E], F16)
        gate_row = sb("gate_row", [P, E])
        parts = sb("parts", [P, 4, 2 * H], F16)
        xT = sb("xT", [P, 2, 2 * KT, P], F16)
        blank = sb("blank", [P, k.row], F16)
        w_rows = sb("w_rows", [P, 2, H])
        b_col = sb("b_col", [P, 1])
        b8_col = sb("b8_col", [P, 1])
        dots_junk = sb("dots_junk", [P, 4, H], mybir.dt.bfloat16)
        diag = sb("diag", [P, 4, P])
        stats1 = sb("stats1", [P, TPB, 6])
        mv1 = sb("mv1", [P, TPB, 2])
        ve1 = sb("ve1", [P, TPB])
        rstd1 = sb("rstd1", [P, TPB])
        center1 = sb("center1", [P, TPB])
        shift1 = sb("shift1", [P, TPB])
        ndots = sb("ndots", [P, 2, TPB])
        src8 = sb("src8", [P, 2, TPB])
        rowmax = sb("rowmax", [P, TPB])
        negmax = sb("negmax", [P, TPB])
        rowsum = sb("rowsum", [P, TPB])
        rinv = sb("rinv", [P, TPB])
        stats2 = sb("stats2", [P, TPB, 6])
        mv2 = sb("mv2", [P, TPB, 2])
        ve2 = sb("ve2", [P, TPB])
        rstd2 = sb("rstd2", [P, TPB])
        shift2 = sb("shift2", [P, TPB])
        mhalf = sb("mhalf", [P, TPB])

        ps_half = [ps(f"ps_half{i}", [P, HT, P]) for i in range(2)]
        ps_att = [ps(f"ps_att{i}", [P, 512]) for i in range(2)]
        ps_dst = [ps(f"ps_dst{i}", [P, 512]) for i in range(2)]
        ps_xT = ps("ps_xT", [P, 2 * KT, P], F16)
        ps_gate = ps("ps_gate", [P, TPB, E])

        const_in = sem("const_in")
        x_in = sem("x_in")
        adj_in = [sem(f"adj_in{i}") for i in range(TPB)]
        ident_zeroed = sem("ident_zeroed")
        consts_ready = sem("consts_ready")
        b8_ready = sem("b8_ready")
        stats1_ready = sem("stats1_ready")
        mv1_ready = sem("mv1_ready")
        ve1_ready = sem("ve1_ready")
        rstd1_ready = sem("rstd1_ready")
        center1_ready = sem("center1_ready")
        shift1_ready = sem("shift1_ready")
        nodes_ready = [sem("even_nodes_ready"), sem("odd_nodes_ready")]
        dots_ready = sem("dots_ready")
        src8_ready = sem("src8_ready")
        diag_ready = sem("diag_ready")
        dst_ready = sem("dst_ready")
        dst5_ready = sem("dst5_ready")
        loop_ready = sem("loop_ready")
        mask_ready = sem("mask_ready")
        pen_ready = sem("pen_ready")
        relu_ready = sem("relu_ready")
        score_ready = sem("score_ready")
        negmax_ready = sem("negmax_ready")
        prob_ready = sem("prob_ready")
        half_ready = [sem(f"half_ready{i}") for i in range(2)]
        probT_ready = [sem(f"probT_ready{i}") for i in range(2)]
        att_ready = sem("att_ready")
        rinv_ready = sem("rinv_ready")
        resid_ready = sem("resid_ready")
        stats2_ready = sem("stats2_ready")
        mv2_ready = sem("mv2_ready")
        ve2_ready = sem("ve2_ready")
        rstd2_ready = sem("rstd2_ready")
        shift2_ready = sem("shift2_ready")
        ln2_ready = sem("ln2_ready")
        hi_ready = sem("hi_ready")
        lo_ready = sem("lo_ready")
        parts_out = [sem(f"parts_out{i}") for i in range(4)]
        blank_ready = sem("blank_ready")
        blanks_stored = sem("blanks_stored")
        gate_parts_ready = sem("gate_parts_ready")
        xT_raw = sem("xT_raw")
        xT_ready = sem("xT_ready")
        gate_ready = sem("gate_ready")
        logits_ready = sem("logits_ready")

        LAST_LAG = 16
        PEELED = 2

        apart = Apart("attention")

        def phase1(eng, step, last=1):
            for b in range(PEELED):
                for t in range(TPB):
                    step(b, t, lambda g: g >= 0, last)
            with eng.Fori(PEELED, B - last) as b:
                for t in range(TPB):
                    step(b, t, lambda g: True, last)
            apart.end(eng, consts_ready)
            for b in range(B - last, B):
                for t in range(TPB + (LAST_LAG if b == B - 1 else 0)):
                    step(b, t, lambda g: g < NT, B - 1 - b)

        def tile_of(b, t, lag):
            return b * TPB + (t - lag), (t - lag) % TPB

        def batch_of(b, t, lag):
            return b + (t - lag) // TPB


        block = ctx.enter_context(nc.Block())

        @block.sync
        def _(sp):
            sp.dma_start(resid[:, 0:TPB, :], x[0].rearrange("(t p) h -> p t h", p=P)).then_inc(x_in, 16)
            for i, w in enumerate((w_src, w_dst)):
                sp.dma_start(w_rows[:, i, :], w.rearrange("(a h) -> a h", a=1).broadcast_to([P, H])).then_inc(const_in, 16)
            sp.dma_start(gate_raw[:, :, :], gate_w.rearrange("(k p) e -> p k e", p=P)).then_inc(const_in, 16)
            sp.dma_start(gate_row[:, :], gate_b.rearrange("(a e) -> a e", a=1).broadcast_to([P, E])).then_inc(const_in, 16)
            sp.dma_start(b_col[:, :], attn_b.rearrange("(a h) -> a h", a=1).broadcast_to([P, 1])).then_inc(const_in, 16)

            def step(b, t, valid, more):
                if t < TPB:
                    load(b, t, more)
                g, j = tile_of(b, t, 15)
                if valid(g):
                    sp.wait_ge(lo_ready, g + 1)
                    sp.dma_start(k.token_x[ds(g, 1)].rearrange("t p c -> p (t c)"), parts[:, j % 4, :]
                                 ).then_inc(parts_out[j % 4], 16)

            def load(b, t, more):
                if t == 4:
                    sp.wait_ge(blank_ready, 4)
                    rows = k.expert_x.rearrange("(b t p) c -> b p t c", b=B, p=P)
                    sp.dma_start(rows[ds(b, 1)].rearrange("b p t c -> p (b t) c"),
                                 blank[:, :].rearrange("p (a c) -> p a c", a=1).broadcast_to([P, rows.shape[2], k.row])
                                 ).then_inc(blanks_stored, 16)
                if t == 0 and isinstance(b, int) and b == 0:
                    sp.wait_ge(x_in, 16)
                    sp.dma_start(resid[:, TPB:2 * TPB, :], x[1].rearrange("(t p) h -> p t h", p=P)).then_inc(x_in, 16)
                if t == 1 and more >= 2:
                    sp.wait_ge(x_in, (b + 2) * 16)
                    sp.dma_start(resid[:, ds((b + 2) * TPB, TPB), :],
                                 x[ds(b + 2, 1)].rearrange("b (t p) h -> p (b t) h", p=P)).then_inc(x_in, 16)
                if not (isinstance(b, int) and b == 0):
                    sp.wait_ge(score_ready, (b - 1) * TPB + (t + 1))
                sp.dma_start(pen[:, t, :].bitcast(I32),
                             adj[ds(b, 1), t * P:(t + 1) * P, :].rearrange("b p n -> p (b n)")
                             ).then_inc(adj_in[t], 16)
            phase1(sp, step, last=2)
            sp.wait_ge(blanks_stored, 16 * B)
            for i in range(4):
                sp.wait_ge(parts_out[i], 16 * NT // 4)

        @block.gpsimd
        def _(pool):
            nc.gpsimd.memset(ident[:, :], 0.0).then_inc(ident_zeroed, 1)
            nc.gpsimd.memset(ones[:, :], 1.0).then_inc(consts_ready, 1)
            nc.gpsimd.memset(mhalf[:, :], -0.5).then_inc(consts_ready, 1)
            nc.gpsimd.memset(blank[:, 0:2 * H], 0.0).then_inc(blank_ready, 1)
            nc.gpsimd.memset(blank[:, 2 * H:2 * H + 1], float(NT)).then_inc(blank_ready, 1)
            nc.gpsimd.iota(blank[:, 2 * H + 1:2 * H + 2], [[0, 1]], base=0, channel_multiplier=2,
                           allow_small_or_imprecise_dtypes=True).then_inc(blank_ready, 1)
            nc.gpsimd.memset(blank[:, 2 * H + 2:2 * H + 4], -1.0).then_inc(blank_ready, 1)
            pool.wait_ge(blank_ready, 4)
            pool.wait_ge(ident_zeroed, 1)
            nc.gpsimd.affine_select(out=ident[:, :], in_=ident[:, :], compare_op=ALU.not_equal, fill=1.0,
                                    base=0, pattern=[[-1, P]], channel_multiplier=1).then_inc(consts_ready, 1)
            pool.wait_ge(consts_ready, 3)
            nc.gpsimd.tensor_copy(ident16[:, :], ident[:, :]).then_inc(consts_ready, 1)
            pool.wait_ge(consts_ready, 4)

            def first_norm_scale(b):
                pool.wait_ge(mv1_ready, (b + 1) * TPB)
                apart(pool)
                nc.gpsimd.tensor_scalar(ve1[:, :], mv1[:, :, 1], EPS, None, ALU.add).then_inc(ve1_ready, 1)
                pool.wait_ge(ve1_ready, b + 1)
                if not (isinstance(b, int) and b == 0):
                    for half in range(2):
                        pool.wait_ge(nodes_ready[half], b * (TPB // 2))
                apart(pool)
                nc.gpsimd.tensor_tensor(rstd1[:, :], ve1[:, :], mhalf[:, :], ALU.pow).then_inc(rstd1_ready, 1)
                pool.wait_ge(rstd1_ready, b + 1)
                apart(pool)
                nc.gpsimd.tensor_tensor(center1[:, :], mv1[:, :, 0], rstd1[:, :], ALU.mult).then_inc(center1_ready, 1)
                pool.wait_ge(center1_ready, b + 1)
                apart(pool)
                nc.gpsimd.tensor_scalar(shift1[:, :], center1[:, :], -1.0, None, ALU.mult).then_inc(shift1_ready, 1)

            def diagonals(b, tiles):
                for j in tiles:
                    pool.wait_ge(dots_ready, b * 2 * TPB + 2 * (j + 1))
                    if j >= 4 or not (isinstance(b, int) and b == 0):
                        pool.wait_ge(dst_ready, b * TPB + (j - 3))
                    apart(pool)
                    nc.gpsimd.tensor_scalar(diag[:, j % 4, :], ident[:, :], ndots[:, 1, j:j + 1], None,
                                            ALU.mult).then_inc(diag_ready, 1)

            def step(b, t, valid, more):
                if t < TPB:
                    g = b * TPB + t
                    if t == 0:
                        pool.wait_ge(dst5_ready, 2 * (b + 1))
                    pool.wait_ge(mask_ready, g + 1)
                    apart(pool)
                    nc.gpsimd.tensor_tensor(pen[:, t, :], pen[:, t, :], dst5[:, ds(b % 2, 1), :],
                                            ALU.add).then_inc(pen_ready, 1)
                if more and t in (3, 4, 5, 6):
                    diagonals(b + 1, range(2 * t - 6, 2 * t - 4))
                g, j = tile_of(b, t, 9)
                if valid(g):
                    pool.wait_ge(mv2_ready, g + 1)
                    apart(pool)
                    nc.gpsimd.tensor_scalar(ve2[:, j:j + 1], mv2[:, j, 1:2], EPS, None, ALU.add).then_inc(ve2_ready, 1)
                    pool.wait_ge(ve2_ready, g + 1)
                    nc.gpsimd.tensor_tensor(rstd2[:, j:j + 1], ve2[:, j:j + 1], mhalf[:, 0:1],
                                            ALU.pow).then_inc(rstd2_ready, 1)
                    pool.wait_ge(rstd2_ready, g + 1)
                    apart(pool)
                    nc.gpsimd.tensor_scalar(shift2[:, j:j + 1], mv2[:, j, 0:1], rstd2[:, j:j + 1], -1.0,
                                            ALU.mult, ALU.mult).then_inc(shift2_ready, 1)
                if more >= 2 and t == 7:
                    first_norm_scale(b + 2)

            first_norm_scale(0)
            diagonals(0, range(TPB))
            first_norm_scale(1)
            phase1(pool, step, last=2)

        @block.vector
        def _(dve):
            def stats(b, tiles):
                if tiles[0] == 0:
                    dve.wait_ge(x_in, (b + 1) * 16)
                for j in tiles:
                    apart(dve)
                    nc.vector.bn_stats(stats1[:, j, :], resid[:, ds(b * TPB + j, 1), :]).then_inc(stats1_ready, 1)

            def aggregate(b):
                for j in range(TPB):
                    dve.wait_ge(stats1_ready, b * TPB + (j + 1))
                    apart(dve)
                    nc.vector.bn_aggr(mv1[:, j, :], stats1[:, j, :]).then_inc(mv1_ready, 1)

            def normalize(b, tiles):
                if tiles[0] == 1:
                    dve.wait_ge(rstd1_ready, b + 1)
                    if not (isinstance(b, int) and b < 4):
                        dve.wait_ge(att_ready, (b - 3) * TPB + 1)
                for j in tiles:
                    nc.vector.tensor_scalar(nodes[:, ds(b % 4, 1), j, :], resid[:, ds(b * TPB + j, 1), :],
                                            mv1[:, j, 0:1], rstd1[:, j:j + 1], ALU.subtract,
                                            ALU.mult).then_inc(nodes_ready[1], 1)

            def dots(b, tiles):
                for j in tiles:
                    dve.wait_ge(nodes_ready[j % 2], b * (TPB // 2) + (j // 2 + 1))
                    for i in range(2):
                        if 2 * j + i >= 4 or not (isinstance(b, int) and b == 0):
                            dve.wait_ge(dots_ready, b * 2 * TPB + (2 * j + i - 3))
                        nc.vector.scalar_tensor_tensor(
                            out=dots_junk[:, (2 * j + i) % 4, :], in0=nodes[:, ds(b % 4, 1), j, :].rearrange("p b h -> p (b h)"), scalar=1.0,
                            in1=w_rows[:, i, :], op0=ALU.mult, op1=ALU.mult, accum_out=ndots[:, i, j:j + 1]).then_inc(dots_ready, 1)

            def src_bias(b):
                dve.wait_ge(dots_ready, (b + 1) * 2 * TPB)
                nc.vector.tensor_scalar(src8[:, ds(b % 2, 1), :], ndots[:, 0, :], 1 - SLOPE, b8_col[:, 0:1],
                                        ALU.mult, ALU.add).then_inc(src8_ready, 1)

            def self_loop(b, j, g):
                own = pen[:, j, j * P:(j + 1) * P].bitcast(I32)
                dve.wait_ge(adj_in[j], (b + 1) * 16)
                nc.vector.tensor_tensor(own, own, ident[:, :], ALU.add).then_inc(loop_ready, 1)

            def mask(j, g):
                dve.wait_ge(loop_ready, g + 1)
                nc.vector.tensor_scalar(pen[:, j, :], pen[:, j, :].bitcast(I32), 0.0, MASKED,
                                        ALU.is_equal, ALU.mult).then_inc(mask_ready, 1)

            def step(b, t, valid, more):
                g, j = tile_of(b, t, 16)
                if j == TPB - 1 and valid(g):
                    bb = batch_of(b, t, 16)
                    dve.wait_ge(gate_ready, g + 1)
                    nc.vector.scalar_tensor_tensor(
                        out=k.logits[:, ds(bb * TPB, TPB), :], in0=ps_gate[:, :, :],
                        scalar=1.0 / WS,
                        in1=gate_row[:, :].rearrange("p (a e) -> p a e", a=1).broadcast_to([P, TPB, E]),
                        op0=ALU.mult, op1=ALU.add).then_inc(logits_ready, 1)
                g, j = tile_of(b, t, 1)
                if valid(g):
                    dve.wait_ge(relu_ready, g + 1)
                    dve.wait_ge(pen_ready, g + 1)
                    apart(dve)
                    nc.vector.tensor_tensor_reduce(out=score[:, j % 4, :], in0=score[:, j % 4, :], in1=pen[:, j, :],
                                                   scale=1.0, scalar=-3.0e38, op0=ALU.add, op1=ALU.max,
                                                   accum_out=rowmax[:, j:j + 1]).then_inc(score_ready, 1)
                g, j = tile_of(b, t, -1)
                if valid(g) and t < TPB:
                    self_loop(batch_of(b, t, -1), j, g)
                g, j = tile_of(b, t, 1)
                if valid(g):
                    dve.wait_ge(score_ready, g + 1)
                    nc.vector.tensor_scalar(negmax[:, j:j + 1], rowmax[:, j:j + 1], -1.0, None,
                                            ALU.mult).then_inc(negmax_ready, 1)
                g, j = tile_of(b, t, -1)
                if valid(g) and t < TPB:
                    mask(j, g)
                g, j = tile_of(b, t, 3)
                if valid(g):
                    dve.wait_ge(prob_ready, g + 1)
                    nc.vector.reciprocal(rinv[:, j:j + 1], rowsum[:, j:j + 1]).then_inc(rinv_ready, 1)
                g, j = tile_of(b, t, 6)
                if valid(g):
                    dve.wait_ge(att_ready, g + 1)
                    dve.wait_ge(rinv_ready, g + 1)
                    nc.vector.scalar_tensor_tensor(out=resid[:, ds(g, 1), :].rearrange("p a h -> p (a h)"), in0=ps_att[j % 2][:, 0:H],
                                                   scalar=rinv[:, j:j + 1], in1=resid[:, ds(g, 1), :].rearrange("p a h -> p (a h)"),
                                                   op0=ALU.mult, op1=ALU.add).then_inc(resid_ready, 1)
                g, j = tile_of(b, t, 7)
                if valid(g):
                    dve.wait_ge(resid_ready, g + 1)
                    apart(dve)
                    nc.vector.bn_stats(stats2[:, j, :], resid[:, ds(g, 1), :]).then_inc(stats2_ready, 1)
                g, j = tile_of(b, t, 12)
                if valid(g):
                    dve.wait_ge(hi_ready, g + 1)
                    nc.vector.tensor_tensor(parts[:, j % 4, H:2 * H], ln2[:, j % 2, :], parts[:, j % 4, 0:H],
                                            ALU.subtract).then_inc(lo_ready, 1)
                g, j = tile_of(b, t, 8)
                if valid(g):
                    dve.wait_ge(stats2_ready, g + 1)
                    apart(dve)
                    nc.vector.bn_aggr(mv2[:, j, :], stats2[:, j, :]).then_inc(mv2_ready, 1)
                if more:
                    if t < 4:
                        normalize(b + 1, [2 * t + 1])
                    if t in (1, 2, 3, 4):
                        dots(b + 1, range(2 * t - 2, 2 * t))
                    if t == 5:
                        src_bias(b + 1)
                if more >= 2:
                    if t >= 6 and t < TPB:
                        stats(b + 2, range(4 * t - 24, 4 * t - 20))
                    if t == 7:
                        aggregate(b + 2)

            dve.wait_ge(const_in, 80)
            dve.wait_ge(gate_parts_ready, 1)
            nc.vector.scalar_tensor_tensor(out=gate_parts[:, 1, :, :], in0=gate_raw[:, :, :], scalar=WS,
                                           in1=gate_parts[:, 0, :, :], op0=ALU.mult,
                                           op1=ALU.subtract).then_inc(gate_parts_ready, 1)
            nc.vector.tensor_scalar(b8_col[:, :], b_col[:, :], 1 - SLOPE, None, ALU.mult).then_inc(b8_ready, 1)
            dve.wait_ge(b8_ready, 1)
            stats(0, range(TPB))
            aggregate(0)
            dve.wait_ge(mv1_ready, TPB)
            stats(1, range(TPB))
            normalize(0, range(1, TPB, 2))
            dots(0, range(TPB))
            dve.wait_ge(shift1_ready, 1)
            aggregate(1)
            src_bias(0)
            self_loop(0, 0, 0)
            mask(0, 0)
            phase1(dve, step, last=2)

        @block.scalar
        def _(act):
            def normalize(b, tiles):
                if tiles[0] == 0:
                    act.wait_ge(shift1_ready, b + 1)
                    if not (isinstance(b, int) and b < 4):
                        act.wait_ge(att_ready, (b - 3) * TPB + 1)
                for j in tiles:
                    nc.scalar.activation(nodes[:, ds(b % 4, 1), j, :].rearrange("p b h -> p (b h)"),
                                         resid[:, ds(b * TPB + j, 1), :].rearrange("p a h -> p (a h)"), ACT.Identity,
                                         bias=shift1[:, j:j + 1], scale=rstd1[:, j:j + 1]).then_inc(nodes_ready[0], 1)

            def dst_rows(b, h):
                act.wait_ge(dst_ready, b * TPB + (h + 1) * HT)
                if h == 0 and not (isinstance(b, int) and b < 2):
                    act.wait_ge(pen_ready, (b - 1) * TPB)
                nc.scalar.activation(dst5[:, ds(b % 2, 1), h * 512:(h + 1) * 512], ps_dst[h][:, :], ACT.Copy,
                                     scale=SLOPE).then_inc(dst5_ready, 1)

            def step(b, t, valid, more):
                g, j = tile_of(b, t, 4)
                if valid(g):
                    act.wait_ge(half_ready[0], g + 1)
                    if valid(g - 2) if isinstance(g, int) else True:
                        act.wait_ge(att_ready, g - 1)
                    nc.scalar.activation(probT[:, j % 2, 0:HT, :], ps_half[0][:, :, :], ACT.Copy).then_inc(probT_ready[0], 1)
                    act.wait_ge(half_ready[1], g + 1)
                    nc.scalar.activation(probT[:, j % 2, HT:TPB, :], ps_half[1][:, :, :], ACT.Copy).then_inc(probT_ready[1], 1)
                g, j = tile_of(b, t, 2)
                if valid(g):
                    act.wait_ge(negmax_ready, g + 1)
                    nc.scalar.activation(score[:, j % 4, :], score[:, j % 4, :], ACT.Exp, bias=negmax[:, j:j + 1],
                                         accum_out=rowsum[:, j:j + 1]).then_inc(prob_ready, 1)
                g, j = tile_of(b, t, 14)
                if valid(g):
                    act.wait_ge(xT_raw, g + 1)
                    if valid(g - 2) if isinstance(g, int) else True:
                        act.wait_ge(gate_ready, g - 1)
                    nc.scalar.activation(xT[:, j % 2, :, :], ps_xT[:, :, :], ACT.Copy).then_inc(xT_ready, 1)
                g, j = tile_of(b, t, 0)
                if t < TPB:
                    if t == 0:
                        act.wait_ge(src8_ready, b + 1)
                        act.wait_ge(dst5_ready, (b + 1) * 2)
                    if valid(g - 4) if isinstance(g, int) else True:
                        act.wait_ge(half_ready[1], g - 3)
                    nc.scalar.activation(score[:, j % 4, :], dst5[:, ds(b % 2, 1), :], ACT.Relu,
                                         bias=src8[:, ds(b % 2, 1), j], scale=(1 - SLOPE) / SLOPE).then_inc(relu_ready, 1)
                g, j = tile_of(b, t, 10)
                if valid(g):
                    act.wait_ge(shift2_ready, g + 1)
                    if valid(g - 2) if isinstance(g, int) else True:
                        act.wait_ge(lo_ready, g - 1)
                    nc.scalar.activation(ln2[:, j % 2, :], resid[:, ds(g, 1), :].rearrange("p a h -> p (a h)"), ACT.Identity,
                                         bias=shift2[:, j:j + 1], scale=rstd2[:, j:j + 1]).then_inc(ln2_ready, 1)
                g, j = tile_of(b, t, 11)
                if valid(g):
                    act.wait_ge(ln2_ready, g + 1)
                    if not (isinstance(g, int) and g < 4):
                        act.wait_ge(parts_out[j % 4], (batch_of(b, t, 11) * 2 + j // 4) * 16)
                        act.wait_ge(xT_raw, g - 3)
                    nc.scalar.activation(parts[:, j % 4, 0:H], ln2[:, j % 2, :], ACT.Copy).then_inc(hi_ready, 1)
                if more and t < 4:
                    normalize(b + 1, [2 * t])
                if more and t == TPB - 1:
                    dst_rows(b + 1, 0)
                    dst_rows(b + 1, 1)

            act.wait_ge(const_in, 80)
            nc.scalar.activation(gate_parts[:, 0, :, :], gate_raw[:, :, :], ACT.Copy, scale=WS).then_inc(gate_parts_ready, 1)
            normalize(0, range(0, TPB, 2))
            dst_rows(0, 0)
            dst_rows(0, 1)
            phase1(act, step)

        @block.tensor
        def _(pe):
            def spread_dst(b, tiles):
                for j in tiles:
                    pe.wait_ge(diag_ready, b * TPB + (j + 1))
                    if j % HT == 0 and not (isinstance(b, int) and b == 0):
                        pe.wait_ge(dst5_ready, b * 2 + (j // HT - 1))
                    nc.tensor.matmul(ps_dst[j // HT][:, (j % HT) * P:(j % HT + 1) * P], ones[:, :],
                                     diag[:, j % 4, :], start=True, stop=True).then_inc(dst_ready, 1)

            def step(b, t, valid, more):
                g, j = tile_of(b, t, 5)
                if valid(g):
                    pe.wait_ge(probT_ready[0], g + 1)
                    if valid(g - 2) if isinstance(g, int) else True:
                        pe.wait_ge(resid_ready, g - 1)
                    if j == 0:
                        for half in range(2):
                            pe.wait_ge(nodes_ready[half], (batch_of(b, t, 5) + 1) * (TPB // 2))
                    for k in range(TPB):
                        if k == HT:
                            pe.wait_ge(probT_ready[1], g + 1)
                        ins = nc.tensor.matmul(ps_att[j % 2][:, 0:H], probT[:, j % 2, k, :],
                                               nodes[:, ds(batch_of(b, t, 5) % 4, 1), k, :].rearrange("p b h -> p (b h)"),
                                               start=(k == 0), stop=(k == TPB - 1))
                    ins.then_inc(att_ready, 1)
                g, j = tile_of(b, t, 3)
                if valid(g):
                    pe.wait_ge(prob_ready, g + 1)
                    for h in range(2):
                        if valid(g - 1) if isinstance(g, int) else True:
                            pe.wait_ge(probT_ready[h], g)
                        for k in range(HT):
                            c = h * HT + k
                            ins = nc.tensor.transpose(ps_half[h][:, k, :], score[:, j % 4, c * P:(c + 1) * P], ident[:, :])
                        ins.then_inc(half_ready[h], 1)
                g, j = tile_of(b, t, 13)
                if valid(g):
                    pe.wait_ge(lo_ready, g + 1)
                    if valid(g - 1) if isinstance(g, int) else True:
                        pe.wait_ge(xT_ready, g)
                    for c in range(2 * KT):
                        ins = nc.tensor.transpose(ps_xT[:, c, :], parts[:, j % 4, c * P:(c + 1) * P], ident16[:, :])
                    ins.then_inc(xT_raw, 1)
                g, j = tile_of(b, t, 15)
                if valid(g):
                    bb = batch_of(b, t, 15)
                    pe.wait_ge(xT_ready, g + 1)
                    if j == 0 and not (isinstance(bb, int) and bb == 0):
                        pe.wait_ge(logits_ready, bb)
                    terms = [(c, xp, wp) for xp, wp in ((0, 0), (0, 1), (1, 0)) for c in range(KT)]
                    for n, (c, xp, wp) in enumerate(terms):
                        ins = nc.tensor.matmul(ps_gate[:, j, :],
                                               xT[:, j % 2, xp * KT + c, :], gate_parts[:, wp, c, :],
                                               start=(n == 0), stop=(n == len(terms) - 1))
                    ins.then_inc(gate_ready, 1)
                if more and t in (3, 4, 5, 6):
                    spread_dst(b + 1, range(2 * t - 6, 2 * t - 4))

            pe.wait_ge(consts_ready, 4)
            pe.wait_ge(gate_parts_ready, 2)
            spread_dst(0, range(TPB))
            phase1(pe, step)


def expert_phases(nc, k, sw1, sb1, sw2, sb2, sact, ew1, eb1, ew2, eb2, eact, out):
    E, H, I2 = ew1.shape
    I = I2 // 2
    KT = H // P
    IT = 2
    IP = I // IT
    B, N, _ = out.shape
    TPB = N // P
    NT = B * TPB
    ST = k.expert_x.shape[0] // P
    U = 4
    UL = 2 * U
    resid, ident, ident16, ones, logits = k.resid, k.ident, k.ident16, k.ones, k.logits
    YS = WS * TS
    UP_LAG, DOWN_LAG = 2, 9
    LAST = 10
    PEELED = -(-(LAST + 1) // UL)

    ctx = ExitStack()
    with ctx:
        def sb(name, shape, dt=F32):
            return ctx.enter_context(nc.sbuf_tensor(name, shape, dt))

        def sem(name):
            return ctx.enter_context(nc.semaphore(name))

        slot = sb("slot", [P, 2, NT], I32)
        share = sb("share", [P, 2, NT])
        GROUPS = (ST + LAST) // UL + 1
        words = sb("words", [P, GROUPS], I32)
        par = sb("par", [P, 8, ST + 1])
        note = sb("note", [P, NT, 4], F16)

        idx = sb("idx", [P, 2, U, 2], I32)
        dest = sb("dest", [P, U], I32)
        wctx = ctx.enter_context(ExitStack())

        def wsb(name, shape, dt=F32):
            return wctx.enter_context(nc.sbuf_tensor(name, shape, dt))

        w1 = wsb("w1", [P, E + 1, KT, 2, I2], F16)
        w2 = wsb("w2", [IP + 2, E + 1, IT, 2, H], F16)
        b1 = wsb("b1", [2, E + 1, I2], F16)
        two16 = wsb("two16", [2, P], F16)
        raw1 = wsb("raw1", [P, KT, I2])
        raw2 = wsb("raw2", [IP, IT, H])
        two_ready = sem("two_ready")
        raw1_in = sem("raw1_in")
        raw2_in = sem("raw2_in")
        w1_high = sem("w1_high")
        w1_ready = sem("w1_ready")
        w2_high = sem("w2_high")
        w2_ready = sem("w2_ready")

        def split(eng, e, before):
            paired = raw1[:, :, :].rearrange("p k (i two) -> p k two i", two=2)
            if eng is nc.scalar:
                eng.wait_ge(raw1_in, (before + 1) * 16)
                nc.scalar.activation(w1[:, ds(e, 1), :, 0, :].rearrange("p e k (two i) -> p (e k) two i", two=2), paired,
                                     ACT.Copy, scale=WS).then_inc(w1_high, 1)
                eng.wait_ge(raw2_in, (before + 1) * 16)
                nc.scalar.activation(w2[0:IP, ds(e, 1), :, 0, :].rearrange("p e c h -> p (e c) h"), raw2[:, :, :],
                                     ACT.Copy, scale=WS).then_inc(w2_high, 1)
            else:
                eng.wait_ge(w1_high, before + 1)
                for c in range(KT):
                    nc.vector.scalar_tensor_tensor(
                        out=w1[:, ds(e, 1), c, 1, :].rearrange("p e (two i) -> p (e two) i", two=2), in0=paired[:, c, :, :],
                        scalar=WS, in1=w1[:, ds(e, 1), c, 0, :].rearrange("p e (two i) -> p (e two) i", two=2),
                        op0=ALU.mult, op1=ALU.subtract).then_inc(w1_ready, 1)
                eng.wait_ge(w2_high, before + 1)
                nc.vector.scalar_tensor_tensor(
                    out=w2[0:IP, ds(e, 1), :, 1, :].rearrange("p e c h -> p (e c) h"), in0=raw2[:, :, :], scalar=WS,
                    in1=w2[0:IP, ds(e, 1), :, 0, :].rearrange("p e c h -> p (e c) h"),
                    op0=ALU.mult, op1=ALU.subtract).then_inc(w2_ready, 1)

        def load_raw(sp, w1_d, w2_d, before):
            if not (isinstance(before, int) and before == 0):
                sp.wait_ge(w1_ready, before * KT)
            sp.dma_start(raw1[:, :, :], w1_d).then_inc(raw1_in, 16)
            if not (isinstance(before, int) and before == 0):
                sp.wait_ge(w2_ready, before)
            sp.dma_start(raw2[:, :, :], w2_d).then_inc(raw2_in, 16)

        routed = sem("routed")

        rctx = ExitStack()
        with rctx:
            def rsb(name, shape, dt=F32):
                return rctx.enter_context(nc.sbuf_tensor(name, shape, dt))

            def rsem(name):
                return rctx.enter_context(nc.semaphore(name))

            eid = rsb("eid", [P, E])
            tiles_row = rsb("tiles_row", [P, ST])
            upper = rsb("upper", [P, P])
            hit = rsb("hit", [P, NT, E], F16)
            cand = rsb("cand", [P, NT, E])
            chosen = [rsb(f"chosen{i}", [P, NT, E], F16) for i in range(2)]
            both = rsb("both", [P, E, NT], F16)
            place = rsb("place", [P, E, NT])
            best = [rsb(f"best{i}", [P, NT]) for i in range(2)]
            pick = [rsb(f"pick{i}", [P, NT]) for i in range(2)]
            slot_f = rsb("slot_f", [P, 2, NT])
            small = rsb("small", [P, 12, E])
            lead = UP_LAG
            tile_expert = rsb("tile_expert", [P, GROUPS * UL + lead])
            words_f = rsb("words_f", [P, 2, GROUPS])
            halves = rsb("halves", [P, 3, GROUPS], I32)
            gap = rsb("gap", [P, NT])
            act_raw = rsb("act_raw", [E + 1, 5])
            soft = rsb("soft", [E + 1, 6, 2])
            scalars = rsb("scalars", [E + 1, 8])
            own_no = rsb("own_no", [E + 1, 1])
            own_tile = rsb("own_tile", [E + 1, ST + 1])
            bias_raw = rsb("bias_raw", [E + 1, I2 + H])
            bias_parts = rsb("bias_parts", [E + 1, 2, I2 + H], F16)
            starts = rsb("starts", [E + 1, 2])
            starts_junk = rsb("starts_junk", [E + 1, 2, E], F16)
            fill_int = rsb("fill_int", [P, 2, E], I32)
            ps_par = [rctx.enter_context(nc.psum_tensor(f"ps_par{i}", [P, 2, 256], F32)) for i in range(4)]
            ps_count = rctx.enter_context(nc.psum_tensor("ps_count", [P, 2, E], F32))

            loaded = rsem("loaded")
            bias_in = rsem("bias_in")
            bias_high = rsem("bias_high")
            bias_low = rsem("bias_low")
            bias_stored = rsem("bias_stored")
            bias_ready = rsem("bias_ready")
            scalars_ready = rsem("scalars_ready")
            own_ready = rsem("own_ready")
            par_ready = rsem("par_ready")
            tile_expert_ready = rsem("tile_expert_ready")
            made = rsem("made")
            upper_ready = rsem("upper_ready")
            counted = rsem("counted")
            prefixed = rsem("prefixed")
            gap_ready = rsem("gap_ready")
            odds_ready = rsem("odds_ready")
            soft_in = rsem("soft_in")
            soft_exp = rsem("soft_exp")
            soft_ln = rsem("soft_ln")
            chain = rsem("chain")
            par_spread = rsem("par_spread")

            block = rctx.enter_context(nc.Block())

            @block.sync
            def _(sp):
                sp.dma_start(act_raw[0:E, :], eact).then_inc(loaded, 16)
                sp.dma_start(act_raw[E:E + 1, :], sact.rearrange("(a c) -> a c", a=1)).then_inc(loaded, 16)
                sp.dma_start(bias_raw[0:E, 0:I2], eb1).then_inc(bias_in, 16)
                sp.dma_start(bias_raw[E:E + 1, 0:I2], sb1.rearrange("(a i) -> a i", a=1)).then_inc(bias_in, 16)
                sp.dma_start(bias_raw[0:E, I2:I2 + H], eb2).then_inc(bias_in, 16)
                sp.dma_start(bias_raw[E:E + 1, I2:I2 + H], sb2.rearrange("(a h) -> a h", a=1)).then_inc(bias_in, 16)
                load_raw(sp, sw1.rearrange("(k p) i -> p k i", p=P), sw2.rearrange("(c p) h -> p c h", p=IP), 0)
                sp.wait_ge(bias_low, 2)
                for i in range(2):
                    sp.dma_start(k.bias_rows[i], bias_parts[:, i, :]).then_inc(bias_stored, 16)
                sp.wait_ge(bias_stored, 32)
                sp.dma_start(b1[:, :, :], k.bias_rows[:, :, 0:I2]).then_inc(bias_ready, 16)
                sp.dma_start(w2[IP:IP + 2, :, 0, 0, :], k.bias_rows[:, :, I2:I2 + H]).then_inc(bias_ready, 16)
                sp.wait_ge(bias_ready, 32)

            @block.gpsimd
            def _(pool):
                nc.gpsimd.iota(eid[:, :], [[1, E]], base=-E, channel_multiplier=0,
                               allow_small_or_imprecise_dtypes=True).then_inc(made, 1)
                nc.gpsimd.iota(tiles_row[:, :], [[1, ST]], base=0, channel_multiplier=0,
                               allow_small_or_imprecise_dtypes=True).then_inc(made, 1)
                nc.gpsimd.iota(note[:, :, 0], [[1, NT]], base=0, channel_multiplier=0,
                               allow_small_or_imprecise_dtypes=True).then_inc(made, 1)
                nc.gpsimd.iota(note[:, :, 1], [[0, NT]], base=0, channel_multiplier=2,
                               allow_small_or_imprecise_dtypes=True).then_inc(made, 1)
                nc.gpsimd.iota(own_no[:, :], [[0, 1]], base=0, channel_multiplier=1,
                               allow_small_or_imprecise_dtypes=True).then_inc(made, 1)
                nc.gpsimd.memset(tile_expert[:, :], 0.0).then_inc(made, 1)
                nc.gpsimd.memset(two16[:, :], 1.0).then_inc(two_ready, 1)
                nc.gpsimd.affine_select(out=upper[:, :], in_=ones[:, :], compare_op=ALU.is_gt, fill=0.0,
                                        base=0, pattern=[[1, P]], channel_multiplier=-1).then_inc(upper_ready, 1)
                pool.wait_ge(made, 6)
                pool.wait_ge(two_ready, 1)
                pool.wait_ge(upper_ready, 1)
                pool.wait_ge(loaded, 32)
                nc.gpsimd.tensor_scalar(soft[:, 4, :], act_raw[:, 3:5], 0.0, None, ALU.max).then_inc(scalars_ready, 1)
                pool.wait_ge(scalars_ready, 1)
                nc.gpsimd.tensor_scalar(soft[:, 0, :], soft[:, 4, :], 2.0, None, ALU.mult).then_inc(scalars_ready, 1)
                pool.wait_ge(scalars_ready, 2)
                nc.gpsimd.tensor_tensor(soft[:, 1, :], act_raw[:, 3:5], soft[:, 0, :], ALU.subtract).then_inc(soft_in, 1)
                pool.wait_ge(soft_in, 1)
                nc.gpsimd.tensor_scalar(scalars[:, 4:5], act_raw[:, 2:3], WS, None, ALU.mult).then_inc(scalars_ready, 1)
                nc.gpsimd.tensor_scalar(scalars[:, 5:6], act_raw[:, 0:1], 1.0 / WS, None, ALU.mult).then_inc(scalars_ready, 1)
                nc.gpsimd.tensor_scalar(scalars[:, 6:7], act_raw[:, 1:2], TS / (WS * WS), None, ALU.mult).then_inc(scalars_ready, 1)
                nc.gpsimd.tensor_copy(scalars[:, 7:8], own_no[:, :]).then_inc(scalars_ready, 1)
                pool.wait_ge(scalars_ready, 6)
                pool.wait_ge(soft_ln, 1)
                nc.gpsimd.tensor_tensor(soft[:, 5, :], soft[:, 3, :], soft[:, 4, :], ALU.add).then_inc(scalars_ready, 1)
                pool.wait_ge(scalars_ready, 7)
                nc.gpsimd.tensor_scalar(scalars[:, 0:2], soft[:, 5, :], WS, None, ALU.mult).then_inc(scalars_ready, 1)
                nc.gpsimd.tensor_scalar(scalars[:, 2:4], soft[:, 5, :], -WS, None, ALU.mult).then_inc(scalars_ready, 1)

            @block.tensor
            def _(pe):
                pe.wait_ge(upper_ready, 1)
                pe.wait_ge(counted, 1)
                nc.tensor.matmul(ps_count[:, 0, :], upper[:, :], small[:, 0, :], start=True, stop=True)
                nc.tensor.matmul(ps_count[:, 1, :], ones[:, :], small[:, 0, :], start=True, stop=True).then_inc(prefixed, 1)
                pe.wait_ge(scalars_ready, 9)
                pe.wait_ge(own_ready, 1)
                for c in range(8):
                    nc.tensor.matmul(ps_par[c // 2][:, c % 2, 0:ST + 1], scalars[:, c:c + 1].broadcast_to([E + 1, P]), own_tile[:, :],
                                     start=True, stop=True).then_inc(par_spread, 1)

            @block.scalar
            def _(act):
                act.wait_ge(soft_in, 1)
                nc.scalar.activation(soft[:, 2, :], soft[:, 1, :], ACT.Exp).then_inc(soft_exp, 1)
                act.wait_ge(soft_exp, 1)
                nc.scalar.activation(soft[:, 3, :], soft[:, 2, :], ACT.Ln, bias=ones[0:E + 1, 0:1]).then_inc(soft_ln, 1)
                act.wait_ge(bias_in, 64)
                nc.scalar.activation(bias_parts[:, 0, 0:I2].rearrange("p (two i) -> p two i", two=2),
                                     bias_raw[:, 0:I2].rearrange("p (i two) -> p two i", two=2), ACT.Copy,
                                     scale=WS).then_inc(bias_high, 1)
                nc.scalar.activation(bias_parts[:, 0, I2:I2 + H], bias_raw[:, I2:I2 + H], ACT.Copy,
                                     scale=YS).then_inc(bias_high, 1)
                split(nc.scalar, E, 0)
                act.wait_ge(gap_ready, 1)
                nc.scalar.activation(gap[:, :], gap[:, :], ACT.Exp).then_inc(odds_ready, 1)
                act.wait_ge(par_spread, 8)
                act.wait_ge(made, 6)
                nc.scalar.activation(tile_expert[:, lead:lead + ST], ps_par[3][:, 1, 0:ST], ACT.Copy).then_inc(tile_expert_ready, 1)
                for i in range(4):
                    nc.scalar.activation(par[:, 2 * i:2 * i + 2, :], ps_par[i][:, :, 0:ST + 1], ACT.Copy).then_inc(par_ready, 1)

            @block.vector
            def _(dve):
                count = [0]

                def link(ins):
                    count[0] += 1
                    ins.then_inc(chain, 1)
                    dve.wait_ge(chain, count[0])

                def over_tiles(a):
                    return a.rearrange("p (a e) -> p a e", a=1).broadcast_to([P, NT, E])

                def over_experts(a):
                    return a.rearrange("p (t a) -> p t a", a=1).broadcast_to([P, NT, E])

                dve.wait_ge(made, 6)
                source = logits
                for i in range(2):
                    link(nc.vector.tensor_reduce(best[i][:, :], source[:, :, :], AX_X, ALU.max))
                    link(nc.vector.tensor_tensor(hit[:, :, :], source[:, :, :], over_experts(best[i][:, :]), ALU.is_equal))
                    link(nc.vector.tensor_tensor(hit[:, :, :], hit[:, :, :], over_tiles(eid[:, :]), ALU.mult))
                    link(nc.vector.tensor_reduce(pick[i][:, :], hit[:, :, :], AX_X, ALU.min))
                    link(nc.vector.tensor_tensor(chosen[i][:, :, :], over_tiles(eid[:, :]), over_experts(pick[i][:, :]),
                                                 ALU.is_equal))
                    if i == 0:
                        link(nc.vector.scalar_tensor_tensor(out=cand[:, :, :], in0=chosen[0][:, :, :], scalar=-1.0e30,
                                                            in1=logits[:, :, :], op0=ALU.mult, op1=ALU.add))
                        dve.wait_ge(bias_high, 2)
                        nc.vector.scalar_tensor_tensor(out=bias_parts[:, 1, 0:I2].rearrange("p (two i) -> p two i", two=2),
                                                       in0=bias_raw[:, 0:I2].rearrange("p (i two) -> p two i", two=2), scalar=WS,
                                                       in1=bias_parts[:, 0, 0:I2].rearrange("p (two i) -> p two i", two=2),
                                                       op0=ALU.mult, op1=ALU.subtract).then_inc(bias_low, 1)
                        nc.vector.scalar_tensor_tensor(out=bias_parts[:, 1, I2:I2 + H], in0=bias_raw[:, I2:I2 + H], scalar=YS,
                                                       in1=bias_parts[:, 0, I2:I2 + H],
                                                       op0=ALU.mult, op1=ALU.subtract).then_inc(bias_low, 1)
                        split(nc.vector, E, 0)
                        source = cand
                link(nc.vector.tensor_tensor(both[:, :, :].rearrange("p e t -> p t e"), chosen[0][:, :, :],
                                             chosen[1][:, :, :], ALU.add))
                nc.vector.tensor_reduce(small[:, 0, :], both[:, :, :], AX_X, ALU.add).then_inc(counted, 1)
                nc.vector.tensor_tensor(gap[:, :], best[1][:, :], best[0][:, :], ALU.subtract).then_inc(gap_ready, 1)
                flat = both[:, :, :].rearrange("p e t -> p (e t)")
                link(nc.vector.tensor_tensor_scan(place[:, :, :].rearrange("p e t -> p (e t)"), flat, flat, 0.0,
                                                  ALU.add, ALU.max))
                dve.wait_ge(counted, 1)
                link(nc.vector.tensor_tensor_scan(small[:, 1, :], small[:, 0, :], small[:, 0, :], 0.0, ALU.add, ALU.max))
                dve.wait_ge(prefixed, 1)
                link(nc.vector.tensor_copy(small[:, 2:4, :], ps_count[:, :, :]))
                link(nc.vector.tensor_scalar(fill_int[:, 0, :], small[:, 3, :], float(P - 1), None, ALU.add))
                link(nc.vector.tensor_scalar(fill_int[:, 1, :], fill_int[:, 0, :], P.bit_length() - 1, None,
                                             ALU.arith_shift_right))
                link(nc.vector.tensor_copy(small[:, 4, :], fill_int[:, 1, :]))
                link(nc.vector.tensor_tensor_scan(small[:, 5, :], small[:, 4, :], small[:, 4, :], 0.0, ALU.add, ALU.max))
                link(nc.vector.tensor_tensor(small[:, 6, :], small[:, 5, :], small[:, 4, :], ALU.subtract))
                for i, row in enumerate((6, 5)):
                    link(nc.vector.scalar_tensor_tensor(out=starts_junk[:, i, :], in0=small[0:E + 1, row, :], scalar=1.0,
                                                        in1=ident[0:E + 1, 0:E], op0=ALU.mult, op1=ALU.mult,
                                                        accum_out=starts[:, i:i + 1]))
                link(nc.vector.tensor_scalar(own_tile[:, ST:ST + 1], own_no[:, :], float(E), None, ALU.is_equal))
                link(nc.vector.tensor_scalar(own_tile[:, 0:ST], tiles_row[0:E + 1, :], starts[:, 0:1], None, ALU.is_ge))
                nc.vector.scalar_tensor_tensor(out=own_tile[:, 0:ST], in0=tiles_row[0:E + 1, :], scalar=starts[:, 1:2],
                                               in1=own_tile[:, 0:ST], op0=ALU.is_lt, op1=ALU.mult).then_inc(own_ready, 1)
                link(nc.vector.scalar_tensor_tensor(out=small[:, 7, :], in0=small[:, 6, :], scalar=float(P),
                                                    in1=small[:, 2, :], op0=ALU.mult, op1=ALU.add))
                link(nc.vector.tensor_tensor(small[:, 8, :], small[:, 0, :], small[:, 1, :], ALU.subtract))
                link(nc.vector.scalar_tensor_tensor(out=small[:, 9, :], in0=small[:, 8, :], scalar=-1.0,
                                                    in1=small[:, 7, :], op0=ALU.add, op1=ALU.add))
                link(nc.vector.tensor_tensor(place[:, :, :], place[:, :, :],
                                             small[:, 9, :].rearrange("p (e a) -> p e a", a=1).broadcast_to([P, E, NT]),
                                             ALU.add))
                for i in range(2):
                    link(nc.vector.tensor_tensor(cand[:, :, :], chosen[i][:, :, :], place[:, :, :].rearrange("p e t -> p t e"),
                                                 ALU.mult))
                    link(nc.vector.tensor_reduce(slot_f[:, i, :], cand[:, :, :], AX_X, ALU.add))
                nc.vector.tensor_copy(slot[:, :, :], slot_f[:, :, :]).then_inc(routed, 1)
                for c in (2, 3):
                    nc.vector.tensor_scalar(note[:, :, c], pick[1][:, :], float(E), None, ALU.add).then_inc(routed, 1)
                dve.wait_ge(tile_expert_ready, 1)
                for i in range(2):
                    def member(j):
                        first = lead - UP_LAG + i * U + j
                        return tile_expert[:, first:first + (GROUPS - 1) * UL + 1:UL]

                    link(nc.vector.scalar_tensor_tensor(out=words_f[:, i, :], in0=member(3), scalar=16.0, in1=member(2),
                                                        op0=ALU.mult, op1=ALU.add))
                    link(nc.vector.scalar_tensor_tensor(out=words_f[:, i, :], in0=words_f[:, i, :], scalar=16.0,
                                                        in1=member(1), op0=ALU.mult, op1=ALU.add))
                    link(nc.vector.scalar_tensor_tensor(out=halves[:, i, :], in0=words_f[:, i, :], scalar=16.0,
                                                        in1=member(0), op0=ALU.mult, op1=ALU.add))
                link(nc.vector.tensor_scalar(halves[:, 2, :], halves[:, 1, :], 4 * U, None, ALU.logical_shift_left))
                nc.vector.tensor_tensor(words[:, :], halves[:, 0, :], halves[:, 2, :], ALU.bitwise_or).then_inc(routed, 1)
                dve.wait_ge(odds_ready, 1)
                link(nc.vector.tensor_scalar(best[0][:, :], gap[:, :], 1.0, None, ALU.add))
                link(nc.vector.reciprocal(share[:, 0, :], best[0][:, :]))
                nc.vector.tensor_tensor(share[:, 1, :], gap[:, :], share[:, 0, :], ALU.mult).then_inc(routed, 1)

        xrow = wsb("xrow", [P, U, k.row], F16)
        xT = wsb("rows_T", [P, U, 2 * KT, P], F16)
        gated = wsb("gated", [P, U, I])
        up = wsb("up", [P, U, I])
        sig = wsb("sig", [P, 2, I])
        gs = wsb("gs", [P, 2, I])
        hid = wsb("hid", [P, 2, I])
        hidT = wsb("hidT", [IP + 2, U, 2, IT, P], F16)

        def run_tiles(eng, tiles, step, lag):
            for q in range(PEELED):
                for u in range(UL):
                    step(q, u, lambda n: n >= 0)
            with eng.Fori(PEELED, tiles // UL) as q:
                for u in range(UL):
                    step(q, u, lambda n: True)
            for u in range(UL, UL + lag):
                step(tiles // UL - 1, u, lambda n: n < tiles)

        def run_both(eng, shared_step, routed_step):
            for q in range(PEELED):
                for u in range(UL):
                    shared_step(q, u, lambda n: n >= 0)
            with eng.Fori(PEELED, NT // UL) as q:
                for u in range(UL):
                    shared_step(q, u, lambda n: True)
            for i in range(PEELED * UL):
                if i < LAST:
                    shared_step(NT // UL - 1, UL + i, lambda n: n < NT)
                routed_step(i // UL, i % UL, lambda n: n >= 0)
            with eng.Fori(PEELED, ST // UL) as q:
                for u in range(UL):
                    routed_step(q, u, lambda n: True)
            for u in range(UL, UL + LAST):
                routed_step(ST // UL - 1, u, lambda n: n < ST)

        def nth(q, u):
            return q * (UL // U) + u // U

        def since(n, before):
            return not isinstance(n, int) or n >= before

        class Signals:

            def __init__(self, name, enter, before=None):
                self.before = before
                self.xT_raw = enter(nc.semaphore(name + "xT_raw"))
                self.xT_ready = enter(nc.semaphore(name + "xT_ready"))
                self.up_done = enter(nc.semaphore(name + "up_done"))
                self.gated_ready = enter(nc.semaphore(name + "gated_ready"))
                self.up_ready = enter(nc.semaphore(name + "up_ready"))
                self.sig_ready = enter(nc.semaphore(name + "sig_ready"))
                self.gs_ready = enter(nc.semaphore(name + "gs_ready"))
                self.hid_ready = enter(nc.semaphore(name + "hid_ready"))
                self.hidT_raw = enter(nc.semaphore(name + "hidT_raw"))
                self.hidT_high = enter(nc.semaphore(name + "hidT_high"))
                self.hidT_ready = enter(nc.semaphore(name + "hidT_ready"))
                self.down_done = enter(nc.semaphore(name + "down_done"))
                self.y_taken = enter(nc.semaphore(name + "y_taken"))

        def slot_wait(eng, s, signal, n, slots):
            if since(n, slots):
                eng.wait_ge(signal(s), n - (slots - 1))
            elif s.before:
                eng.wait_ge(signal(s.before), NT + n - (slots - 1))

        def gate_by_sigmoid(eng, ops, s, n, v, apart=None):
            eng.wait_ge(s.sig_ready, n + 1)
            eng.wait_ge(s.gated_ready, n + 1)
            slot_wait(eng, s, lambda r: r.hid_ready, n, 2)
            if apart:
                apart(eng)
            ops.tensor_tensor(gs[:, v % 2, :], gated[:, v, :], sig[:, v % 2, :], ALU.mult).then_inc(s.gs_ready, 1)

        def feed_forward(s, experts_of, load_words, par_at, x_wait, take_y, y_engine, prepare):
            terms = [(c, xp, wp) for xp, wp in ((0, 0), (0, 1), (1, 0)) for c in range(KT)]
            hid_terms = [(c, xp, wp) for xp, wp in ((0, 0), (0, 1), (1, 0)) for c in range(IT)]

            def at(q, u, lag):
                return q * UL + (u - lag), (u - lag) % 2, (u - lag) % U

            def tensor_step(pe):
                def step(q, u, valid):
                    n, b, v = at(q, u, 7)
                    if valid(n):
                        pe.wait_ge(s.hid_ready, n + 1)
                        slot_wait(pe, s, lambda r: r.hidT_ready, n, 2)
                        for c in range(IT):
                            ins = nc.tensor.transpose(ps_hT[b][:, c, :], hid[:, b, c * IP:(c + 1) * IP], ident[:, :])
                        ins.then_inc(s.hidT_raw, 1)
                    e_up, e_down = experts_of(pe, q, u)
                    n, b, v = at(q, u, 0)
                    if u < UL:
                        x_wait(pe, q, u, n)
                        slot_wait(pe, s, lambda r: r.xT_ready, n, 2)
                        for c in range(2 * KT):
                            ins = nc.tensor.transpose(ps_xT[b][:, c, :], xrow[:, v, c * P:(c + 1) * P], ident16[:, :])
                        ins.then_inc(s.xT_raw, 1)
                    n, b, v = at(q, u, UP_LAG)
                    if valid(n):
                        pe.wait_ge(s.xT_ready, n + 1)
                        slot_wait(pe, s, lambda r: r.up_ready, n, 2)
                        nc.tensor.matmul(ps_h[b][:, :], two16[:, :], b1[:, ds(e_up, 1), :].rearrange("p e i -> p (e i)"),
                                         start=True, stop=False)
                        for i, (c, xp, wp) in enumerate(terms):
                            ins = nc.tensor.matmul(ps_h[b][:, :], xT[:, v, xp * KT + c, :],
                                                   w1[:, ds(e_up, 1), c, wp, :].rearrange("p e i -> p (e i)"),
                                                   start=False, stop=(i == len(terms) - 1))
                        ins.then_inc(s.up_done, 1)
                    n, b, v = at(q, u, DOWN_LAG)
                    if valid(n):
                        pe.wait_ge(s.hidT_ready, n + 1)
                        slot_wait(pe, s, lambda r: r.y_taken, n, 2)
                        for i, (c, xp, wp) in enumerate(hid_terms):
                            rows = IP + 2 if i == 0 else IP
                            ins = nc.tensor.matmul(ps_y[b][:, :], hidT[0:rows, v, xp, c, :],
                                                   w2[0:rows, ds(e_down, 1), c, wp, :].rearrange("p e h -> p (e h)"),
                                                   start=(i == 0), stop=(i == len(hid_terms) - 1))
                        ins.then_inc(s.down_done, 1)
                    load_words(pe, q, u)
                return step

            def scalar_step(act):
                def step(q, u, valid):
                    n, b, v = at(q, u, 8)
                    if valid(n):
                        e = par_at(n)
                        act.wait_ge(s.hidT_raw, n + 1)
                        slot_wait(act, s, lambda r: r.down_done, n, U)
                        nc.scalar.activation(hidT[0:IP, v, 0, :, :], ps_hT[b][:, :, :], ACT.Copy,
                                             scale=par[0:IP, 6, ds(e, 1)]).then_inc(s.hidT_high, 1)
                    n, b, v = at(q, u, 1)
                    if valid(n):
                        act.wait_ge(s.xT_raw, n + 1)
                        slot_wait(act, s, lambda r: r.up_done, n, U)
                        nc.scalar.activation(xT[:, v, :, :], ps_xT[b][:, :, :], ACT.Copy).then_inc(s.xT_ready, 1)
                    n, b, v = at(q, u, 4)
                    if valid(n):
                        e = par_at(n)
                        act.wait_ge(s.gated_ready, n + 1)
                        slot_wait(act, s, lambda r: r.gs_ready, n, 2)
                        nc.scalar.activation(sig[:, b, :], gated[:, v, :], ACT.Sigmoid,
                                             scale=par[:, 5, ds(e, 1)]).then_inc(s.sig_ready, 1)
                    n, b, v = at(q, u, LAST)
                    if valid(n) and y_engine == "scalar":
                        act.wait_ge(s.down_done, n + 1)
                        take_y(act, s, q, u - LAST, n, ps_y[b])
                    if prepare:
                        prepare(act, q, u)
                return step

            def vector_step(dve):
                def step(q, u, valid):
                    n, b, v = at(q, u, 3)
                    if valid(n):
                        e = par_at(n)
                        dve.wait_ge(s.up_done, n + 1)
                        slot_wait(dve, s, lambda r: r.gs_ready, n, U)
                        slot_wait(dve, s, lambda r: r.hid_ready, n, U)
                        nc.vector.tensor_scalar(gated[:, v, :], ps_h[b][:, 0:I], par[:, 2, ds(e, 1)], par[:, 0, ds(e, 1)],
                                                ALU.max, ALU.min).then_inc(s.gated_ready, 1)
                        nc.vector.tensor_scalar(up[:, v, :], ps_h[b][:, I:I2], par[:, 3, ds(e, 1)], par[:, 1, ds(e, 1)],
                                                ALU.max, ALU.min).then_inc(s.up_ready, 1)
                    n, b, v = at(q, u, 8)
                    if valid(n):
                        e = par_at(n)
                        dve.wait_ge(s.hidT_high, n + 1)
                        nc.vector.scalar_tensor_tensor(out=hidT[0:IP, v, 1, :, :], in0=ps_hT[b][:, :, :],
                                                       scalar=par[0:IP, 6, ds(e, 1)], in1=hidT[0:IP, v, 0, :, :],
                                                       op0=ALU.mult, op1=ALU.subtract).then_inc(s.hidT_ready, 1)
                    n, b, v = at(q, u, 6)
                    if valid(n):
                        e = par_at(n)
                        dve.wait_ge(s.up_ready, n + 1)
                        dve.wait_ge(s.gs_ready, n + 1)
                        slot_wait(dve, s, lambda r: r.hidT_raw, n, 2)
                        nc.vector.scalar_tensor_tensor(out=hid[:, b, :], in0=up[:, v, :], scalar=par[:, 4, ds(e, 1)],
                                                       in1=gs[:, b, :], op0=ALU.add, op1=ALU.mult
                                                       ).then_inc(s.hid_ready, 1)
                    n, b, v = at(q, u, 5)
                    if valid(n) and y_engine == "vector":
                        gate_by_sigmoid(dve, nc.vector, s, n, v)
                    n, b, v = at(q, u, LAST)
                    if valid(n) and y_engine == "vector":
                        dve.wait_ge(s.down_done, n + 1)
                        take_y(dve, s, q, u - LAST, n, ps_y[b])
                    if prepare:
                        prepare(dve, q, u)
                return step

            return tensor_step, scalar_step, vector_step

        sctx = ExitStack()
        with sctx:
            def banks(name, shape, dt=F32):
                return [sctx.enter_context(nc.psum_tensor(f"{name}{i}", shape, dt)) for i in range(2)]

            ps_xT = banks("ps_rows_T", [P, 2 * KT, P], F16)
            ps_h = banks("ps_h", [P, I2])
            ps_hT = banks("ps_hT", [IP, IT, P])
            ps_y = banks("ps_y", [P, H])
            def ssem(name):
                return sctx.enter_context(nc.semaphore(name))

            s = Signals("s_", sctx.enter_context)
            x_in = [ssem(f"rows_in{i}") for i in range(U)]
            scattered = [ssem(f"scattered{i}") for i in range(U)]
            idx_ready = ssem("idx_ready")
            noted = ssem("noted")

            def note_and_split(eng, q, u):
                if eng is nc.scalar and u < UL:
                    n = q * UL + u
                    if since(n, U):
                        eng.wait_ge(scattered[u % U], nth(q, u) * 32)
                    nc.scalar.activation(xrow[:, u % U, 2 * H:2 * H + 4],
                                         note[:, ds(n, 1), :].rearrange("p n c -> p (n c)"), ACT.Copy).then_inc(noted, 1)
                if u % U == U - 1 and u < UL:
                    split(eng, nth(q, u), nth(q, u) + 1)

            def shared_x_wait(eng, q, u, n):
                eng.wait_ge(x_in[u % U], (nth(q, u) + 1) * 16)

            def add_shared(dve, s, q, u, n, bank):
                nc.vector.scalar_tensor_tensor(out=resid[:, ds(n, 1), :].rearrange("p t h -> p (t h)"), in0=bank[:, :],
                                               scalar=1.0 / YS, in1=resid[:, ds(n, 1), :].rearrange("p t h -> p (t h)"),
                                               op0=ALU.mult, op1=ALU.add).then_inc(s.y_taken, 1)

            shared_steps = feed_forward(
                s, lambda pe, q, u: (E, E), lambda pe, q, u: None, lambda n: ST, shared_x_wait,
                add_shared, "vector", note_and_split)

            y = sctx.enter_context(nc.sbuf_tensor("y", [P, U, H], F32))
            dest_f = sctx.enter_context(nc.sbuf_tensor("dest_f", [P, ST], F32))
            placed = sctx.enter_context(nc.semaphore("placed"))
            within = sctx.enter_context(nc.sbuf_tensor("within", [P, 2], F32))
            within_ready = sctx.enter_context(nc.semaphore("within_ready"))
            dest_ready = sctx.enter_context(nc.semaphore("dest_ready"))
            r = Signals("e_", sctx.enter_context, s)
            routed_in = [sctx.enter_context(nc.semaphore(f"e_rows_in{i}")) for i in range(U)]
            y_out = [sctx.enter_context(nc.semaphore(f"e_y_out{i}")) for i in range(U)]

            word_regs = {}

            def load_word(pe, reg, g):
                pe.reg_load(reg, words[0:1, ds(g, 1)])

            def expert_at(reg, u):
                return (bass.RuntimeValue.of_register_unchecked(reg) >> 4 * u) & (E - 1)

            def routed_experts(pe, q, u):
                if isinstance(q, int) and q == 0 and u == 0:
                    for name in [f"round{i}" for i in range(PEELED)] + ["this", "last"]:
                        word_regs[name] = pe.alloc_register(f"{name}_word")
                    load_word(pe, word_regs["round0"], 0)
                if isinstance(q, int) and q < PEELED:
                    this, last = word_regs[f"round{q}"], word_regs[f"round{max(q - 1, 0)}"]
                elif u < 2 * UL:
                    this, last = word_regs["this"], word_regs["last"]
                else:
                    this = last = word_regs["this"]
                u = u % UL
                return expert_at(this, u), (expert_at(last, u + 1) if u < UL - 1 else expert_at(this, 0))

            def load_words(pe, q, u):
                if u != UL - 1:
                    return
                if isinstance(q, int) and q + 1 < PEELED:
                    load_word(pe, word_regs[f"round{q + 1}"], q + 1)
                else:
                    pe.reg_mov(word_regs["last"], word_regs[f"round{q}"] if isinstance(q, int) else word_regs["this"])
                    load_word(pe, word_regs["this"], q + 1)

            def expert_x_wait(eng, q, u, n):
                eng.wait_ge(routed_in[u % U], (nth(q, u) + 1) * 16)

            def store_y(act, s, q, u, n, bank):
                if since(n, U):
                    act.wait_ge(y_out[u % U], nth(q, u) * 16)
                nc.scalar.activation(y[:, u % U, :], bank[:, :], ACT.Copy, scale=1.0 / YS).then_inc(s.y_taken, 1)

            def place_rows(eng, q, u):
                if eng is not nc.vector:
                    return
                n, v, w = q * UL + (u - 1), (u - 1) % U, (u - 1) % 2
                if since(n, 0) and u <= UL:
                    eng.wait_ge(within_ready, n + 1)
                    nc.vector.scalar_tensor_tensor(out=dest_f[:, ds(n, 1)], in0=xrow[:, v, 2 * H:2 * H + 1],
                                                   scalar=2.0 * P, in1=within[:, w:w + 1], op0=ALU.mult,
                                                   op1=ALU.add).then_inc(placed, 1)
                if u < UL:
                    n, v, w = q * UL + u, u % U, u % 2
                    eng.wait_ge(routed_in[v], (nth(q, u) + 1) * 16)
                    if since(n, 2):
                        eng.wait_ge(placed, n - 1)
                    nc.vector.scalar_tensor_tensor(out=within[:, w:w + 1], in0=xrow[:, v, 2 * H + 2:2 * H + 3],
                                                   scalar=par[:, 7, ds(n, 1)], in1=xrow[:, v, 2 * H + 1:2 * H + 2],
                                                   op0=ALU.is_equal, op1=ALU.add).then_inc(within_ready, 1)

            def gate_by_sigmoid_on_pool(pool, q, u, valid):
                n, v = q * UL + (u - 5), (u - 5) % U
                if valid(n):
                    gate_by_sigmoid(pool, nc.gpsimd, r, n, v, apart)

            routed_steps = feed_forward(
                r, routed_experts, load_words, lambda n: n, expert_x_wait, store_y, "scalar", place_rows)

            apart = Apart("rows")
            block = sctx.enter_context(nc.Block())

            @block.sync
            def _(sp):
                done = sp.alloc_register("scatters_done")
                sp.reg_mov(done, 0)

                def load_tokens(q, u, valid):
                    n, v = q * UL + u, u % U
                    if v == 0 and since(n, U):
                        sp.reg_alu(done, done, 32, ALU.add)
                    if since(n, U):
                        sp.wait_ge(s.xT_raw, n - (U - 1))
                        sp.wait_ge(scattered[v], done)
                    sp.dma_start(xrow[:, v, 0:2 * H], k.token_x[ds(n, 1)].rearrange("t p c -> p (t c)")).then_inc(x_in[v], 16)
                    if v == U - 1:
                        e = nth(q, u)
                        load_raw(sp, ew1[ds(e, 1)].rearrange("e (k p) i -> p (e k) i", p=P),
                                 ew2[ds(e, 1)].rearrange("e (c p) h -> p (e c) h", p=IP), e + 1)
                run_tiles(sp, NT, load_tokens, 0)

                for v in range(U):
                    sp.wait_ge(scattered[v], NT // U * 32)

                def load_rows(q, u, valid):
                    n, v = q * UL + u, u % U
                    slot_wait(sp, r, lambda g: g.xT_raw, n, U)
                    if since(n, U):
                        sp.wait_ge(placed, n - (U - 1))
                    sp.dma_start(xrow[:, v, :], k.expert_x[ds(n * P, P), :]).then_inc(routed_in[v], 16)
                run_tiles(sp, ST, load_rows, 0)

            @block.gpsimd
            def _(pool):
                nc.gpsimd.memset(hidT[IP:IP + 2, :, 0, 0, :], 1.0).then_inc(two_ready, 1)
                pool.wait_ge(two_ready, 2)

                def scatter(r, h):
                    first = isinstance(r, int) and r == 0
                    if not first:
                        for u in range(U):
                            pool.wait_ge(scattered[u], (2 * r + (h - 1)) * 32)
                    apart(pool)
                    nc.gpsimd.tensor_copy(idx[:, h, :, :].rearrange("p u c -> p c u"),
                                          slot[:, :, ds(r * 2 * U + h * U, U)]).then_inc(idx_ready, 1)
                    pool.wait_ge(idx_ready, 2 * r + (h + 1))
                    for u in range(U):
                        pool.wait_ge(x_in[u], (2 * r + (h + 1)) * 16)
                        pool.wait_ge(noted, r * 2 * U + (h * U + u + 1))
                        apart(pool)
                        for i in range(2):
                            nc.gpsimd.indirect_dma_start(
                                out=k.expert_x[:, :], out_offset=bass.IndirectOffsetOnAxis(ap=idx[:, h, u, i:i + 1], axis=0),
                                in_=xrow[:, u, :], in_offset=None).then_inc(scattered[u], 16)

                scatter(0, 0)
                scatter(0, 1)
                with pool.Fori(1, NT // (2 * U)) as pair:
                    scatter(pair, 0)
                    scatter(pair, 1)
                apart.end(pool, idx_ready)
                for u in range(U):
                    pool.wait_ge(scattered[u], NT // U * 32)

                def step(q, u, valid):
                    gate_by_sigmoid_on_pool(pool, q, u, valid)
                    n, v = q * UL + (u - LAST), (u - LAST) % U
                    if valid(n):
                        if since(n, U):
                            pool.wait_ge(y_out[v], nth(q, u - LAST) * 16)
                        pool.wait_ge(placed, n + 1)
                        apart(pool)
                        nc.gpsimd.tensor_copy(dest[:, v:v + 1], dest_f[:, ds(n, 1)]).then_inc(dest_ready, 1)
                        pool.wait_ge(dest_ready, n + 1)
                        pool.wait_ge(r.y_taken, n + 1)
                        apart(pool)
                        nc.gpsimd.indirect_dma_start(
                            out=k.choice_y[:, :], out_offset=bass.IndirectOffsetOnAxis(ap=dest[:, v:v + 1], axis=0),
                            in_=y[:, v, :], in_offset=None, bounds_check=2 * NT * P - 1, oob_is_err=False
                            ).then_inc(y_out[v], 16)
                run_tiles(pool, ST, step, LAST)
                apart.end(pool, dest_ready)
                for u in range(U):
                    pool.wait_ge(y_out[u], ST // U * 16)

            @block.tensor
            def _(pe):
                pe.wait_ge(two_ready, 2)
                run_both(pe, shared_steps[0](pe), routed_steps[0](pe))

            @block.scalar
            def _(act):
                run_both(act, shared_steps[1](act), routed_steps[1](act))

            @block.vector
            def _(dve):
                run_both(dve, shared_steps[2](dve), routed_steps[2](dve))

        wctx.close()
        cctx = ExitStack()
        with cctx:
            CU, CB = 2, 4
            STEPS = NT // CU
            choice = cctx.enter_context(nc.sbuf_tensor("choice", [P, CB, CU, 2, H], F32))
            chosen_in = [cctx.enter_context(nc.semaphore(f"chosen_in{i}")) for i in range(CB)]
            half_added = cctx.enter_context(nc.semaphore("half_added"))
            both_added = cctx.enter_context(nc.semaphore("both_added"))
            stored = cctx.enter_context(nc.semaphore("stored"))
            out_tiles = out.rearrange("b (t p) h -> p (b t) h", p=P)
            choice_rows = k.choice_y.rearrange("(t p c) h -> p t c h", p=P, c=2)

            block = cctx.enter_context(nc.Block())

            def run_steps(eng, step):
                for v in range(CB):
                    step(0, v)
                with eng.Fori(1, STEPS // CB) as r:
                    for v in range(CB):
                        step(r, v)

            @block.sync
            def _(sp):
                def step(r, v):
                    m = r * CB + v
                    if not (isinstance(r, int) and r == 0):
                        sp.wait_ge(both_added, (m - (CB - 1)) * CU)
                    sp.dma_start(choice[:, v, :, :, :].rearrange("p t c h -> p t (c h)"),
                                 choice_rows[:, ds(m * CU, CU), :, :].rearrange("p t c h -> p t (c h)")
                                 ).then_inc(chosen_in[v], 16)
                run_steps(sp, step)

            @block.vector
            def _(dve):
                def step(r, v):
                    m = r * CB + v
                    dve.wait_ge(chosen_in[v], (r + 1) * 16)
                    for i in range(2):
                        for c in range(CU):
                            n = m * CU + c
                            if i == 1:
                                dve.wait_ge(half_added, n + 1)
                            tile = resid[:, ds(n, 1), :].rearrange("p t h -> p (t h)")
                            nc.vector.scalar_tensor_tensor(
                                out=tile, in0=choice[:, v, c, i, :], scalar=share[:, i, ds(n, 1)], in1=tile,
                                op0=ALU.mult, op1=ALU.add).then_inc((half_added, both_added)[i], 1)
                run_steps(dve, step)

            @block.scalar
            def _(act):
                def step(r, v):
                    m = r * CB + v
                    act.wait_ge(both_added, (m + 1) * CU)
                    act.dma_start(out_tiles[:, ds(m * CU, CU), :], resid[:, ds(m * CU, CU), :]).then_inc(stored, 16)
                run_steps(act, step)
                act.wait_ge(stored, STEPS * 16)


class Kept:
    pass


def gnn_moe_kernel(nc, x, adj, w_src, w_dst, attn_b, gate_w, gate_b, sw1, sb1, sw2, sb2, sact,
                   ew1, eb1, ew2, eb2, eact, out):
    B, N, H = x.shape
    E, _, I2 = ew1.shape
    NT = B * N // P
    K = 2
    ST = NT * K + E
    k = Kept()
    k.token_x = nc.dram_tensor("token_x", (NT, P, 2 * H), F16, kind="Internal").ap()
    k.row = 2 * H + 4
    k.expert_x = nc.dram_tensor("expert_x", (ST * P, k.row), F16, kind="Internal").ap()
    k.choice_y = nc.dram_tensor("choice_y", (NT * P * K, H), F32, kind="Internal").ap()
    k.bias_rows = nc.dram_tensor("bias_rows", (2, E + 1, I2 + H), F16, kind="Internal").ap()
    with ExitStack() as ctx:
        k.resid = ctx.enter_context(nc.sbuf_tensor("resid", [P, NT, H], F32))
        k.ident = ctx.enter_context(nc.sbuf_tensor("ident", [P, P], F32))
        k.ident16 = ctx.enter_context(nc.sbuf_tensor("ident16", [P, P], F16))
        k.ones = ctx.enter_context(nc.sbuf_tensor("ones", [P, P], F32))
        k.logits = ctx.enter_context(nc.sbuf_tensor("logits", [P, NT, E], F32))
        attention_phase(nc, k, x, adj, w_src, w_dst, attn_b, gate_w, gate_b)
        expert_phases(nc, k, sw1, sb1, sw2, sb2, sact, ew1, eb1, ew2, eb2, eact, out)



_INS = ["x", "adj", "L0_gnn_attn_w_src", "L0_gnn_attn_w_dst", "L0_gnn_attn_b", "L0_ffn_gate_w", "L0_ffn_gate_b",
        "L0_ffn_shared_w1", "L0_ffn_shared_b1", "L0_ffn_shared_w2", "L0_ffn_shared_b2", "L0_ffn_shared_act",
        "L0_ffn_expert_w1", "L0_ffn_expert_b1", "L0_ffn_expert_w2", "L0_ffn_expert_b2", "L0_ffn_expert_act"]


def kernel(**inputs):
    import numpy as np
    import concourse.bacc as bacc
    from concourse import mybir as mb
    from concourse.bass_utils import run_bass_kernel_spmd

    nc = bacc.Bacc("TRN2", target_bir_lowering=False, num_devices=1)
    arrays, args = {}, []
    for name in _INS:
        a = np.ascontiguousarray(inputs[name])
        arrays[f"in_{name}"] = a
        args.append(nc.dram_tensor(f"in_{name}", a.shape, mb.dt.from_np(a.dtype), kind="ExternalInput").ap())
    out = nc.dram_tensor("out_x", inputs["x"].shape, mb.dt.float32, kind="ExternalOutput").ap()
    gnn_moe_kernel(nc, *args, out)
    r = run_bass_kernel_spmd(nc, [arrays], core_ids=[0])
    return r.results[0]["out_x"]
```
